# Optimizing a Trainium2 kernel written in Bass

```python
import numpy as np
import jax
import jax.numpy as jnp

def _softmax(x, axis=-1):
    return jax.nn.softmax(x, axis=axis)

def _gelu(x):
    return jax.nn.gelu(x, approximate=True)

def _silu(x):
    return jax.nn.silu(x)

def _sigmoid(x):
    return jax.nn.sigmoid(x)

def _layernorm(x, axis=-1, eps=1e-05):
    m = jnp.mean(x, axis=axis, keepdims=True)
    v = jnp.var(x, axis=axis, keepdims=True)
    return (x - m) / jnp.sqrt(v + eps)

def _scatter_add(tgt, idx, src, axis=0):
    return tgt.at[idx].add(src)

def _segment_sum(src, seg, n):
    return jax.ops.segment_sum(src, seg, n)
kernel_name = 'mk_macaron_d1_jaxref_r4_5dcc6d'

def setup_inputs(seed: int=0):
    np.random.seed(seed)
    _w = jnp.asarray

    def _L0_attn_setup():
        import jax, jax.numpy as jnp
        import numpy as np
        B, T, D, H = (2, 512, 256, 16)
        HD = D // H
        key = jax.random.key(seed)
        ks = jax.random.split(key, 9)
        s = 1.0 / np.sqrt(D)
        return {'x': jax.random.normal(ks[0], (B, T, D), dtype=jnp.float32), 'Wq': jax.random.uniform(ks[1], (D, D), minval=-s, maxval=s, dtype=jnp.float32), 'bq': jax.random.uniform(ks[2], (D,), minval=-s, maxval=s, dtype=jnp.float32), 'Wk': jax.random.uniform(ks[3], (D, D), minval=-s, maxval=s, dtype=jnp.float32), 'bk': jax.random.uniform(ks[4], (D,), minval=-s, maxval=s, dtype=jnp.float32), 'Wv': jax.random.uniform(ks[5], (D, D), minval=-s, maxval=s, dtype=jnp.float32), 'bv': jax.random.uniform(ks[6], (D,), minval=-s, maxval=s, dtype=jnp.float32), 'Wo': jax.random.uniform(ks[7], (D, D), minval=-s, maxval=s, dtype=jnp.float32), 'bo': jax.random.uniform(ks[8], (D,), minval=-s, maxval=s, dtype=jnp.float32)}
    _L0_attn_in = _L0_attn_setup()

    def _L0_ffn_setup():
        import jax, jax.numpy as jnp
        import numpy as np
        EPS_LN = 1e-05
        EPS_GATE = 1e-08

        def layer_norm(x, gamma, beta):
            mu = jnp.mean(x, axis=-1, keepdims=True)
            var = jnp.mean(jnp.square(x - mu), axis=-1, keepdims=True)
            return (x - mu) * jax.lax.rsqrt(var + EPS_LN) * gamma + beta
        key = jax.random.key(seed)
        ks = jax.random.split(key, 8)
        B, S, D, E, H = (4, 1024, 256, 4, 512)
        s_in = 1.0 / np.sqrt(D)
        s_h = 1.0 / np.sqrt(H)
        return {'h': jax.random.normal(ks[0], (B, S, D), dtype=jnp.float32), 'router_w': jax.random.uniform(ks[1], (E, D), jnp.float32, -s_in, s_in), 'rn_g': jnp.ones((D,), jnp.float32), 'rn_b': jnp.zeros((D,), jnp.float32), 'w1': jax.random.uniform(ks[2], (E, D, H), jnp.float32, -s_in, s_in), 'ln_g': jnp.ones((E, H), jnp.float32), 'ln_b': jnp.zeros((E, H), jnp.float32), 'w2': jax.random.uniform(ks[3], (E, H, D), jnp.float32, -s_h, s_h), 'on_g': jnp.ones((D,), jnp.float32), 'on_b': jnp.zeros((D,), jnp.float32)}
    _L0_ffn_in = _L0_ffn_setup()
    _d = {'L0_attn_x': _L0_attn_in['x'], 'L0_attn_Wq': _L0_attn_in['Wq'], 'L0_attn_bq': _L0_attn_in['bq'], 'L0_attn_Wk': _L0_attn_in['Wk'], 'L0_attn_bk': _L0_attn_in['bk'], 'L0_attn_Wv': _L0_attn_in['Wv'], 'L0_attn_bv': _L0_attn_in['bv'], 'L0_attn_Wo': _L0_attn_in['Wo'], 'L0_attn_bo': _L0_attn_in['bo'], 'L0_ffn_router_w': _L0_ffn_in['router_w'], 'L0_ffn_rn_g': _L0_ffn_in['rn_g'], 'L0_ffn_rn_b': _L0_ffn_in['rn_b'], 'L0_ffn_w1': _L0_ffn_in['w1'], 'L0_ffn_ln_g': _L0_ffn_in['ln_g'], 'L0_ffn_ln_b': _L0_ffn_in['ln_b'], 'L0_ffn_w2': _L0_ffn_in['w2'], 'L0_ffn_on_g': _L0_ffn_in['on_g'], 'L0_ffn_on_b': _L0_ffn_in['on_b']}
    _x0 = _d['L0_attn_x']
    _d['L0_attn_x'] = jax.random.normal(jax.random.fold_in(jax.random.key(seed), 1), (2, 2048, 256), dtype=_x0.dtype)
    del _x0
    return _d

def reference(L0_attn_x, L0_attn_Wq, L0_attn_bq, L0_attn_Wk, L0_attn_bk, L0_attn_Wv, L0_attn_bv, L0_attn_Wo, L0_attn_bo, L0_ffn_router_w, L0_ffn_rn_g, L0_ffn_rn_b, L0_ffn_w1, L0_ffn_ln_g, L0_ffn_ln_b, L0_ffn_w2, L0_ffn_on_g, L0_ffn_on_b):

    def _L0_attn_ref(x, Wq, bq, Wk, bk, Wv, bv, Wo, bo):
        import jax, jax.numpy as jnp
        import numpy as np
        B, T, D, H = (2, 512, 256, 16)
        HD = D // H
        b, t, d = x.shape

        def split_heads(y):
            return y.reshape(b, t, H, HD).transpose(0, 2, 1, 3)
        Q = split_heads(x @ Wq.T + bq)
        K = split_heads(x @ Wk.T + bk)
        V = split_heads(x @ Wv.T + bv)
        Z = jnp.einsum('bhsp,bhsn->bhspn', V, K)
        Z_cum = jnp.cumsum(Z, axis=2)
        Y = jnp.einsum('bhtn,bhtpn->bhtp', Q, Z_cum)
        Y = Y.transpose(0, 2, 1, 3).reshape(b, t, d)
        return Y @ Wo.T + bo

    def _L0_ffn_ref(h, router_w, rn_g, rn_b, w1, ln_g, ln_b, w2, on_g, on_b):
        import jax, jax.numpy as jnp
        import numpy as np
        EPS_LN = 1e-05
        EPS_GATE = 1e-08

        def layer_norm(x, gamma, beta):
            mu = jnp.mean(x, axis=-1, keepdims=True)
            var = jnp.mean(jnp.square(x - mu), axis=-1, keepdims=True)
            return (x - mu) * jax.lax.rsqrt(var + EPS_LN) * gamma + beta
        D = h.shape[-1]
        h_norm = layer_norm(h, rn_g, rn_b)
        g = jax.nn.softmax(jnp.einsum('bsd,ed->bse', h_norm, router_w), axis=-1)
        top2_w, top2_idx = jax.lax.top_k(g, 2)
        top2_w = top2_w / (jnp.sum(top2_w, axis=-1, keepdims=True) + EPS_GATE)
        hid = jnp.einsum('bsd,edh->bseh', h, w1)
        hid = jax.nn.relu(layer_norm(hid, ln_g, ln_b))
        expert_out = jnp.einsum('bseh,ehd->bsed', hid, w2)
        idx = jnp.broadcast_to(top2_idx[..., None], top2_idx.shape + (D,))
        top2_out = jnp.take_along_axis(expert_out, idx, axis=-2)
        out = jnp.sum(top2_out * top2_w[..., None], axis=-2)
        return layer_norm(out, on_g, on_b)
    x = L0_attn_x
    x = x + 0.5 * _L0_ffn_ref(_layernorm(x, axis=-1), L0_ffn_router_w, L0_ffn_rn_g, L0_ffn_rn_b, L0_ffn_w1, L0_ffn_ln_g, L0_ffn_ln_b, L0_ffn_w2, L0_ffn_on_g, L0_ffn_on_b)
    x = x + _L0_attn_ref(_layernorm(x, axis=-1), L0_attn_Wq, L0_attn_bq, L0_attn_Wk, L0_attn_bk, L0_attn_Wv, L0_attn_bv, L0_attn_Wo, L0_attn_bo)
    x = x + 0.5 * _L0_ffn_ref(_layernorm(x, axis=-1), L0_ffn_router_w, L0_ffn_rn_g, L0_ffn_rn_b, L0_ffn_w1, L0_ffn_ln_g, L0_ffn_ln_b, L0_ffn_w2, L0_ffn_on_g, L0_ffn_on_b)
    return x

_drawn_inputs = setup_inputs


def setup_inputs(seed=0):
    import zlib

    import numpy as np

    out = dict(_drawn_inputs(seed))
    spreads = {'L0_ffn_rn_g': (1.0, 0.2),
     'L0_ffn_rn_b': (0.0, 0.1),
     'L0_ffn_ln_g': (1.0, 0.2),
     'L0_ffn_ln_b': (0.0, 0.1),
     'L0_ffn_on_g': (1.0, 0.2),
     'L0_ffn_on_b': (0.0, 0.1)}
    factors = {'L0_attn_bo': 64.0}
    for name, (base, spread) in spreads.items():
        noise = np.random.default_rng([zlib.crc32(name.encode()), seed]).standard_normal(out[name].shape)
        drawn = base * np.exp(spread * noise) if base else spread * noise
        out[name] = jnp.asarray(drawn.astype(out[name].dtype))
    for name, factor in factors.items():
        out[name] = (out[name] * factor).astype(out[name].dtype)
    return out
```

```python
from contextlib import ExitStack

import concourse.bass as bass
from concourse import mybir

ALU = mybir.AluOpType
ACT = mybir.ActivationFunctionType
AX = mybir.AxisListType
F32 = mybir.dt.float32
F16 = mybir.dt.float16
U32 = mybir.dt.uint32
RMAX = bass.bass_isa.ReduceOp.max

P = 128
EPS = 1e-5
EPS_GATE = 1e-8
EXPONENT = 0x7F800000
TINY = 2.0 ** -40
TINY_ATT = 2.0 ** -16
S_SHIFT = 2.0 ** -19
STD_SHIFT = 64.0


def macaron_kernel(nc, x, Wq, bq, Wk, bk, Wv, bv, Wo, bo, router_w, rn_g, rn_b, w1, ln_g, ln_b, w2, on_g, on_b, out):
    NB, T, D = x.shape
    E, _, H = w1.shape
    NT = NB * T // P
    KC = D // P
    HC = H // P
    TB = 4
    BT = TB * P
    NBLK = NT // TB
    NSTD = 3 * E
    NU = TB * E // 2
    NA = E * HC
    NO = E * TB
    HD = 16
    HPC = P // HD
    NG = D // HD // 4
    NX = 16 * HPC

    x_t = x.rearrange("b (n p) d -> p (b n) d", p=P)
    out_t = out.rearrange("b (n p) d -> p (b n) d", p=P)

    with ExitStack() as ctx:
        def sb(name, shape, dt=F32):
            return ctx.enter_context(nc.sbuf_tensor(name, shape, dt))

        def sem(name):
            return ctx.enter_context(nc.semaphore(name))

        bank = [ctx.enter_context(nc.psum_tensor(f"bank{i}", [P, 512], F32)) for i in range(8)]

        X = sb("X", [P, NT, D])
        w1h = sb("w1h", [P, E, KC, H], F16)
        w1l = sb("w1l", [P, E, KC, H], F16)
        w2h = sb("w2h", [P, E, HC, D], F16)
        w2l = sb("w2l", [P, E, HC, D], F16)
        gramh = sb("gramh", [P, KC, E, D], F16)
        graml = sb("graml", [P, KC, E, D], F16)
        betas = sb("betas", [NSTD, E, H], F16)
        routw = sb("routw", [P, KC, 2 * E], F16)
        routc = sb("routc", [P, E])
        ong = sb("ong", [P, D])
        onb = sb("onb", [P, D])
        identf = sb("identf", [P, P])
        ident16 = sb("ident16", [P, P], F16)
        nhalf = sb("nhalf", [P, TB, E])
        phalf = sb("phalf", [P, TB, E])
        inv_std = sb("inv_std", [P, TB, E])
        consts = sb("consts", [P, 5, TB])
        half_, inv_d, eps_, mone = (consts[:, k] for k in range(4))
        before = sb("before", [P, E, E])
        after = sb("after", [P, E, E])

        area = sb("area", [P, 101 * 256])

        def at_kb(kb, shape, dt=F32):
            n = 1
            for k in shape:
                n *= k
            words = n if dt == F32 else n // 2
            assert 256 * kb + words <= 101 * 256
            v = area[:, int(256 * kb):int(256 * kb) + words]
            v = v if dt == F32 else v.bitcast(dt)
            names = "abcdef"[:len(shape)]
            if len(shape) == 1:
                return v
            return v.rearrange(f"p ({' '.join(names)}) -> p {' '.join(names)}", **dict(zip(names, shape)))

        Rh = at_kb(0, [2, HC, BT], F16)
        Rl = at_kb(8, [2, HC, BT], F16)
        junk = at_kb(16, [TB * E, D], F16)
        h2 = at_kb(24, [TB, D])
        hr = at_kb(28, [TB, D], F16)
        sdT = at_kb(30, [2, BT], F16)[0:NSTD]
        acc = at_kb(32, [TB, D])
        z = at_kb(36, [TB, D])
        gamB = at_kb(0, [E, H])
        w1T = at_kb(8, [2, HC, D])
        wqkv = at_kb(16, [4, KC, D])
        betr = at_kb(32, [H])[0:NSTD]
        betl = at_kb(34, [H])[0:NSTD]
        betv = at_kb(36, [H])[0:NSTD]
        beth = at_kb(38, [H], F16)[0:NSTD]
        w1r = at_kb(40, [E, KC, H])
        w1g = at_kb(56, [E, KC, H])
        w2r = at_kb(72, [E, HC, D])
        rnbB = at_kb(88, [KC, P])
        ones = at_kb(89, [P])
        qf = at_kb(0, [2, KC, BT])
        kf = at_kb(8, [KC, BT])
        qp = at_kb(12, [KC, 2, BT], F16)
        kp = at_kb(16, [2, KC, 2, BT], F16)
        ktok = at_kb(24, [2, 2, TB, D], F16)
        vtok = at_kb(32, [2, 2, TB, D], F16)
        qx = at_kb(40, [HPC, KC, 2, BT], F16)
        vf = at_kb(8, [TB, D])
        sm = at_kb(72, [NG, 4, P])
        shl = at_kb(80, [2, 2, NG, 4, P], F16)
        ysb = at_kb(96, [D])
        yT = at_kb(97, [KC, P])
        dz = at_kb(98, [KC, P])
        zst = at_kb(99, [2, KC, P])

        pick = sb("pick", [NSTD, E + 2])
        rw = sb("rw", [E, D])
        rwT = sb("rwT", [P, KC, E])
        rwg = sb("rwg", [P, KC, E])
        rngc = sb("rngc", [P, KC])
        rnbc = sb("rnbc", [P, KC])
        rsum = sb("rsum", [P, E * KC])
        rmean = sb("rmean", [P, E * KC])
        NMX = 7
        mx = sb("mx", [P, NMX + 3])
        mxa = sb("mxa", [P, NMX + 3])
        big = sb("big", [P, 6])
        capn = sb("capn", [P, 6])
        q = sb("q", [P, 6])
        qi = sb("qi", [P, 6])
        sc = sb("sc", [P, 8])
        epsq, bscale, kappa, aev, iys = sc[:, 0:1], sc[:, 1:2], sc[:, 2:3], sc[:, 4:5], sc[:, 5:6]
        qc, q1, q2, qr, qri = q[:, 0:1], q[:, 1:2], q[:, 2:3], q[:, 3:4], qi[:, 3:4]
        qa, sa = q[:, 4:5], q[:, 5:6]
        wTh = sb("wTh", [P, 3, KC, D], F16)
        wTl = sb("wTl", [P, 3, KC, D], F16)
        woT = sb("woT", [P, KC, D])
        bqk = sb("bqk", [P, 2, KC])
        bvB = sb("bvB", [P, D])
        boB = sb("boB", [P, D])
        causal = sb("causal", [P, P])
        sameh = sb("sameh", [P, P])

        xst = sb("xst", [P, TB, 6])
        xf = sb("xf", [P, 12, TB])
        xrs, xnr = xf[:, 10], xf[:, 11]
        r2a = sb("r2a", [P, TB])
        r2b = sb("r2b", [P, TB])
        r2c = sb("r2c", [P, TB])
        r2d = sb("r2d", [P, TB])
        r2 = sb("r2", [P, TB])
        h = sb("h", [P, TB, D])
        hTh = sb("hTh", [P, 2, KC, BT], F16)
        hTl = sb("hTl", [P, 2, KC, BT], F16)
        lsb = sb("lsb", [P, TB, 2 * E])
        lga = sb("lga", [P, TB, E])
        lgb = sb("lgb", [P, TB, E])
        lgc = sb("lgc", [P, TB, E])
        lgd = sb("lgd", [P, TB, E])
        lmax = sb("lmax", [P, TB])
        ex = sb("ex", [P, TB, E])
        var = sb("var", [P, TB, E])
        vare = sb("vare", [P, TB, E])
        sd = sb("sd", [P, TB, E])
        sds = sb("sds", [P, TB, E])
        rsd = sb("rsd", [P, TB, E])
        s12 = sb("s12", [P, TB, NSTD], F16)
        gt = sb("gt", [P, TB, E, E])
        ge = sb("ge", [P, TB, E, E])
        rank = sb("rank", [P, TB, E])
        es = sb("es", [P, TB, E])
        ws = sb("ws", [P, TB, E])
        wr = sb("wr", [P, TB, E])
        tot = sb("tot", [P, 2, TB])
        den = sb("den", [P, TB])
        rden = sb("rden", [P, TB])
        coef = sb("coef", [P, 2, TB, E])
        ast = sb("ast", [P, TB, 6])
        af = sb("af", [P, 12, TB])
        ars, anr = af[:, 10], af[:, 11]

        l_att = sem("l_att")
        l_w1, l_w2, l_gam, l_bet, l_rw, l_on, l_x = (sem(n) for n in (
            "l_w1", "l_w2", "l_gam", "l_bet", "l_rw", "l_on", "l_x"))
        p_id = sem("p_id")
        p_c = sem("p_c")
        p_mx = sem("p_mx")
        p_mxa = sem("p_mxa")
        p_q = sem("p_q")
        p_hi = sem("p_hi")
        p_wt = sem("p_wt")
        p_wtc = sem("p_wtc")
        p_g = sem("p_g")
        p_gh = sem("p_gh")
        p_gl = sem("p_gl")
        p_rt = sem("p_rt")
        p_rc = sem("p_rc")
        (s_mv, s_rs, s_h, s_hr, s_T, s_hTh, s_hTl, s_h2, s_L, s_lg, s_lgl, s_lmax, s_lgm, s_E, s_U, s_var, s_sd,
         s_rsd, s_vare, s_s12, s_ST, s_sdT, s_coef, s_A, s_Rh, s_Rl, s_O, s_acc, s_amv, s_ars, s_z, s_x, s_out) = (sem(n) for n in (
            "x_stats", "x_rstd", "h_ready", "h_rounded", "hT_psum", "hT_high", "hT_low", "h2_ready", "logits_psum",
            "logits_copied", "logits_ready", "logits_max", "logits_less_max", "exp_ready", "gram_psum", "var_ready",
            "std_ready", "rstd_ready", "var_guarded", "std_parts", "stdT_psum", "stdT_ready", "coef_ready", "hid_psum", "relu_high", "relu_low",
            "out_psum", "acc_ready", "acc_stats", "acc_rstd", "z_ready", "x_updated", "stored"))
        (a_zero, a_mask, a_w, a_wh, a_wl, a_qk, a_qf, a_qh, a_kh, a_qp, a_kl, a_kt, a_kth, a_ktl, a_v, a_vf,
         a_vh, a_vl, a_xb, a_s, a_sm, a_sh, a_sl, a_sll, a_y, a_ysb, a_yt, a_ytc, a_wo, a_x, a_dz, a_dzm, a_z) = (
            sem("a_" + n) for n in (
            "queries_cleared", "masks", "weights_T_psum", "weights_high", "weights_low", "qk_psum", "qk_copied",
            "q_high", "k_high", "q_parts", "k_parts", "ktok_psum", "ktok_high", "ktok_low", "v_psum",
            "v_copied", "v_high", "v_low", "bias_added", "scores_psum", "scores_masked", "scores_high", "scores_low",
            "last_scores_low",
            "y_psum", "y_copied", "yT_psum", "yT_copied", "proj_psum", "x_updated", "kv_psum", "kv_masked",
            "kv_added"))
        a_qx = [sem(f"a_q_expanded{half}") for half in range(2)]
        dve_done = sem("dve_done")
        pool_done = sem("pool_done")

        block = ctx.enter_context(nc.Block())

        def wait(eng, s, value):
            if isinstance(value, int) and value <= 0:
                return
            eng.wait_ge(s, value)

        def tile0(n, n0, par):
            return (n - par - n0) * (TB // 2) + par * (NT // 2)

        class Steps:
            def __init__(self, eng, s, at=0):
                self.eng, self.s, self.at = eng, s, at

            def __call__(self, ins):
                ins.then_inc(self.s, 1)
                self.at = self.at + 1
                self.eng.wait_ge(self.s, self.at)

        def blocks(eng, n0, body):
            body(n0, 0, False)
            body(n0 + 1, 1, False)
            with eng.Fori(n0 // 2 + 1, (n0 + NBLK) // 2 - 1, 1) as pair:
                body(2 * pair, 0, False)
                body(2 * pair + 1, 1, False)
            body(n0 + NBLK - 2, 0, False)
            return body(n0 + NBLK - 1, 1, True)

        @block.sync
        def _(sp):
            for e in range(E):
                sp.dma_start(w1r[:, e], w1[e].rearrange("(c p) n -> p c n", p=P)).then_inc(l_w1, 16)
            for r in range(3):
                sp.dma_start(betr[r * E:(r + 1) * E, :], ln_b).then_inc(l_bet, 16)
            for e in range(E):
                sp.dma_start(w2r[:, e], w2[e].rearrange("(c p) n -> p c n", p=P)).then_inc(l_w2, 16)
            for k, w in enumerate((Wq, Wk, Wv, Wo)):
                sp.dma_start(wqkv[:, k], w.rearrange("(c p) n -> p c n", p=P)).then_inc(l_att, 16)
            for b in range(NBLK):
                sp.dma_start(X[:, b * TB:(b + 1) * TB, :], x_t[:, b * TB:(b + 1) * TB, :]).then_inc(l_x, 16)

            def expand(n):
                wait(sp, a_qp, n + 1)
                for half in range(2):
                    cols = slice(half * BT // 2, (half + 1) * BT // 2)
                    wait(sp, a_s, NG * TB * (n - 1) + NG * 2 * (half + 1))
                    for j in range(HPC):
                        rows = slice(j * HD, (j + 1) * HD)
                        sp.dma_start(qx[rows, j, :, :, cols], qp[rows, :, :, cols]).then_inc(a_qx[half], 16)

            sp.wait_ge(a_zero, 1)
            expand(0)
            with sp.Fori(1, NBLK, 1) as n:
                expand(n)

            def store(n):
                for par in range(2):
                    sp.wait_ge(s_x, TB * (n + par + 1))
                    t0 = tile0(n + par, NBLK, par)
                    sp.dma_start(out_t[:, bass.ds(t0, TB), :], X[:, bass.ds(t0, TB), :]).then_inc(s_out, 16)

            with sp.Fori(NBLK // 2, NBLK, 1) as pair:
                store(2 * pair)
            sp.wait_ge(s_out, 16 * NBLK)

        @block.gpsimd
        def _(pool):
            step = Steps(pool, pool_done)
            step(pool.memset(identf[:, :], 0.0))
            step(pool.affine_select(out=identf[:, :], in_=identf[:, :], compare_op=ALU.not_equal, fill=1.0,
                                    base=0, pattern=[[-1, P]], channel_multiplier=1))
            step(pool.tensor_copy(ident16[:, :], identf[:, :]))
            step(pool.memset(nhalf[:, :, :], -0.5))
            step(pool.memset(phalf[:, :, :], 0.5))
            step(pool.memset(inv_std[:, :, :], 1.0 / STD_SHIFT))
            for k, v in enumerate((0.5, 1.0 / D, EPS, -1.0)):
                step(pool.memset(consts[:, k], v))
            step(pool.memset(ones, 1.0))
            step(pool.memset(before[:, :, :], 1.0))
            step(pool.affine_select(out=before[:, :, :], in_=before[:, :, :], compare_op=ALU.is_ge, fill=0.0,
                                    base=-1, pattern=[[1, E], [-1, E]], channel_multiplier=0))
            step(pool.tensor_scalar(after[:, :, :], before[:, :, :], -1.0, 1.0, ALU.mult, ALU.add))
            step(pool.memset(causal[:, :], 1.0))
            step(pool.affine_select(out=causal[:, :], in_=causal[:, :], compare_op=ALU.is_ge, fill=0.0,
                                    base=0, pattern=[[1, P]], channel_multiplier=-1))
            step(pool.memset(sameh[:, :], 1.0))
            sameh_v = sameh[:, :].rearrange("p (j d) -> p j d", d=HD)
            for base, jd, cm in ((0, -HD, 1), (HD - 1, HD, -1)):
                step(pool.affine_select(out=sameh_v, in_=sameh_v, compare_op=ALU.is_ge, fill=0.0,
                                        base=base, pattern=[[jd, HPC], [0, HD]], channel_multiplier=cm))
            for j, c in enumerate((128.0, 128.0, 32768.0, 1024.0, 1024.0, 32768.0)):
                step(pool.memset(capn[:, j:j + 1], c))
            pool.memset(mx[:, :], 0.0).then_inc(p_id, 1)
            pool.wait_ge(p_mx, 1)
            pool.partition_all_reduce(mxa[:, :], mx[:, :], P, RMAX).then_inc(p_mxa, 1)
            pool.wait_ge(p_q, 1)
            def bc(a):
                return a.unsqueeze(2).to_broadcast([P, TB, E])

            def norm_factors(stats, f, at, done):
                me, qe, mo, qo = (stats[:, :, k] for k in (1, 2, 4, 5))
                pool.tensor_tensor(f[:, 0], me, mo, ALU.add)
                pool.tensor_tensor(f[:, 1], me, mo, ALU.subtract)
                at(pool.tensor_tensor(f[:, 2], qe, qo, ALU.add))
                pool.tensor_tensor(f[:, 3], f[:, 0], half_, ALU.mult)
                pool.tensor_tensor(f[:, 4], f[:, 1], half_, ALU.mult)
                at(pool.tensor_tensor(f[:, 5], f[:, 2], inv_d, ALU.mult))
                at(pool.tensor_tensor(f[:, 6], f[:, 4], f[:, 4], ALU.mult))
                at(pool.tensor_tensor(f[:, 8], f[:, 5], f[:, 6], ALU.add))
                at(pool.tensor_tensor(f[:, 9], f[:, 8], eps_, ALU.add))
                at(pool.tensor_tensor(f[:, 10], f[:, 9], nhalf[:, :, 0], ALU.pow))
                at(pool.tensor_tensor(f[:, 7], f[:, 3], f[:, 10], ALU.mult))
                pool.tensor_tensor(f[:, 11], f[:, 7], mone, ALU.mult).then_inc(done, 1)

            def rs(g, at, router):
                wait(pool, s_mv, g + 1)
                wait(pool, s_h, g)
                norm_factors(xst, xf, at, s_rs)
                if not router:
                    return
                at(pool.tensor_tensor(r2a[:, :], xf[:, 8], xrs, ALU.mult))
                at(pool.tensor_tensor(r2b[:, :], r2a[:, :], xrs, ALU.mult))
                at(pool.tensor_tensor(r2c[:, :], r2b[:, :], eps_, ALU.add))
                at(pool.tensor_tensor(r2d[:, :], r2c[:, :], nhalf[:, :, 0], ALU.pow))
                at(pool.tensor_tensor(r2[:, :], r2d[:, :], qri.to_broadcast([P, TB]), ALU.mult))

            def logits(n, at):
                wait(pool, s_lg, n + 1)
                at(pool.tensor_tensor(lga[:, :, :], lsb[:, :, 0:E], lsb[:, :, E:2 * E], ALU.add))
                at(pool.tensor_tensor(lgb[:, :, :], lga[:, :, :], bc(r2[:, :]), ALU.mult))
                pool.tensor_tensor(lgc[:, :, :], lgb[:, :, :], routc[:, :].unsqueeze(1).to_broadcast([P, TB, E]),
                                   ALU.add).then_inc(s_lgl, 1)

            def less_max(n, at):
                wait(pool, s_lmax, n + 1)
                pool.tensor_tensor(lgd[:, :, :], lgc[:, :, :], bc(lmax[:, :]), ALU.subtract).then_inc(s_lgm, 1)

            def std(n, at):
                wait(pool, s_vare, n + 1)
                wait(pool, s_s12, n)
                wait(pool, s_coef, n)
                at(pool.tensor_tensor(sd[:, :, :], vare[:, :, :], phalf[:, :, :], ALU.pow))
                pool.tensor_tensor(sds[:, :, :], sd[:, :, :], inv_std[:, :, :], ALU.mult).then_inc(s_sd, 1)
                pool.tensor_tensor(rsd[:, :, :], vare[:, :, :], nhalf[:, :, :], ALU.pow).then_inc(s_rsd, 1)

            def post_stats(n, at):
                wait(pool, s_amv, n + 1)
                wait(pool, s_z, TB * n)
                norm_factors(ast, af, at, s_ars)

            def post(n, par, f, at):
                for t in range(TB):
                    xt = X[:, tile0(n, f * NBLK, par) + t, :]
                    wait(pool, s_z, TB * n + (t + 1))
                    at(pool.tensor_tensor(z[:, t, :], z[:, t, :], ong[:, :], ALU.mult))
                    at(pool.tensor_tensor(z[:, t, :], z[:, t, :], onb[:, :], ALU.add))
                    pool.tensor_tensor(xt, xt, z[:, t, :], ALU.add).then_inc(s_x, 1)

            def ffn(f):
                n0 = f * NBLK
                g0 = 2 * f * NBLK
                at = Steps(pool, pool_done, step.at)
                rs(g0, at, True)
                logits(n0, at)
                less_max(n0, at)
                std(n0, at)
                per_prep = at.at - step.at
                start = at.at
                n_post = 7 + 2 * TB
                per = per_prep + n_post

                def body(n, par, last):
                    first = isinstance(n, int) and n == n0
                    at = Steps(pool, pool_done, start if first else (n - n0) * per + (start - n_post))
                    if not first:
                        post_stats(n - 1, at)
                    if not last:
                        rs(n + (1 + g0 - n0), at, True)
                    if not first:
                        post(n - 1, 1 - par, f, at)
                    if not last:
                        logits(n + 1, at)
                        less_max(n + 1, at)
                        std(n + 1, at)
                    if f == 0 and first:
                        pool.wait_ge(p_gl, E + 1)
                        pool.wait_ge(p_g, E)
                        pool.memset(qx.rearrange("p a b c d -> p (a b c d)").bitcast(F32), 0.0).then_inc(a_zero, 1)
                    return at

                at = blocks(pool, n0, body)
                post_stats(n0 + NBLK - 1, at)
                post(n0 + NBLK - 1, 1, f, at)
                step.at = at.at

            def attention():
                pool.wait_ge(s_x, TB * NBLK)
                pool.memset(zst, 0.0).then_inc(a_mask, 1)
                pool.wait_ge(a_mask, 1)

                def add_bias(n, par):
                    t0 = tile0(n, 0, par)
                    wait(pool, s_h, n + (NBLK + 1))
                    xt = X[:, bass.ds(t0, TB), :]
                    pool.tensor_tensor(xt, xt, boB[:, :].unsqueeze(1).to_broadcast([P, TB, D]),
                                       ALU.add).then_inc(a_xb, 1)

                def key_low(n, par):
                    wait(pool, a_kh, n + 1)
                    pool.tensor_tensor(kp[:, par, :, 1], kf, kp[:, par, :, 0], ALU.subtract).then_inc(a_kl, 1)

                def score_low(c, cp, g):
                    wait(pool, a_sh, NG * c + (g + 1))
                    wait(pool, a_y, c - 1)
                    pool.tensor_tensor(shl[:, cp, 1, g], sm[:, g], shl[:, cp, 0, g], ALU.subtract).then_inc(a_sl, 1)

                def add_state(c, par):
                    wait(pool, a_dzm, c + 1)
                    wait(pool, a_y, c + 1)
                    pool.tensor_tensor(zst[:, par], zst[:, par], dz, ALU.add).then_inc(a_z, 1)

                at = Steps(pool, pool_done, step.at)
                rs(NBLK, at, False)
                add_bias(0, 0)
                key_low(0, 0)
                for g in range(NG - 1):
                    score_low(0, 0, g)
                start = at.at
                per = 7

                def body(n, par, last):
                    at = Steps(pool, pool_done, n * per + start)
                    for t in range(TB):
                        c = n * TB + t
                        if t == 0 and not last:
                            rs(n + (NBLK + 1), at, False)
                        for g in range(NG - 1):
                            if not (last and t == TB - 1):
                                score_low(c + 1, (t + 1) % 2, g)
                            if t == 2 and g == 0 and not last:
                                key_low(n + 1, 1 - par)
                        if t == 1 and not last:
                            add_bias(n + 1, 1 - par)
                        add_state(c, par)
                    return at

                at = blocks(pool, 0, body)
                step.at = at.at

            ffn(0)
            attention()
            pool.wait_ge(a_x, TB * NBLK)
            ffn(1)

        @block.vector
        def _(dve):
            step = Steps(dve, dve_done)
            dve.wait_ge(l_w1, 16 * E)
            w1v = w1r[:, :, :, :].rearrange("p e c n -> p (e c) n")
            step(dve.tensor_reduce(rsum[:, :], w1v, AX.X, ALU.add))
            step(dve.tensor_scalar(rmean[:, :], rsum[:, :], 1.0 / H, None, ALU.mult))
            for k in range(E * KC):
                last = dve.tensor_scalar(w1v[:, k, :], w1v[:, k, :], rmean[:, k:k + 1], None, ALU.subtract)
            last.then_inc(p_c, 1)
            dve.wait_ge(p_c, 1)
            dve.wait_ge(l_gam, 16)
            for c in range(KC):
                last = dve.tensor_tensor(w1g[:, :, c, :], w1r[:, :, c, :], gamB[:, :, :], ALU.mult)
            step(last)
            dve.wait_ge(l_rw, 48)
            dve.wait_ge(p_id, 1)
            for c in range(KC):
                last = dve.tensor_scalar(rnbB[:, c, :], ones[:, :], rnbc[:, c:c + 1], None, ALU.mult)
            dve.wait_ge(p_rt, 1)
            step(dve.tensor_copy(rwT[:, :, :], bank[6][:, 0:KC * E].rearrange("p (c e) -> p c e", c=KC)))
            for c in range(KC):
                last = dve.tensor_scalar(rwg[:, c, :], rwT[:, c, :], rngc[:, c:c + 1], None, ALU.mult)
            last.then_inc(p_rc, 1)
            dve.wait_ge(p_rc, 1)
            dve.wait_ge(l_bet, 48)
            dve.wait_ge(l_w2, 16 * E)
            dve.wait_ge(l_att, 16 * 8)
            for j, a, axis in ((0, w1r[:, :, :, :].rearrange("p e c n -> p (e c n)"), AX.X),
                               (1, w1g[:, :, :, :].rearrange("p e c n -> p (e c n)"), AX.X),
                               (2, w2r[:, :, :, :].rearrange("p e c n -> p (e c n)"), AX.X),
                               (4, rwg[:, :, :].rearrange("p c e -> p (c e)"), AX.X),
                               (5, wqkv[:, 0:3].rearrange("p k c n -> p (k c n)"), AX.X),
                               (6, bqk[:, :, :].rearrange("p k c -> p (k c)"), AX.X),
                               (7, bvB[:, :], AX.X)):
                dve.tensor_reduce(mx[:, j:j + 1], a, axis, ALU.max, apply_absolute_value=True)
            dve.tensor_reduce(mx[0:NSTD, 3:4], betr[:, :], AX.X, ALU.max, apply_absolute_value=True).then_inc(p_mx, 1)
            dve.wait_ge(p_mxa, 1)
            step(dve.tensor_scalar(big[:, 0:1], mxa[:, 0:1], TINY, None, ALU.max))
            step(dve.scalar_tensor_tensor(out=big[:, 1:2], in0=mxa[:, 3:4], scalar=big[:, 0:1], in1=mxa[:, 1:2],
                                          op0=ALU.mult, op1=ALU.add))
            step(dve.tensor_copy(big[:, 2:3], mxa[:, 2:3]))
            step(dve.tensor_copy(big[:, 3:4], mxa[:, 4:5]))
            step(dve.tensor_scalar(big[:, 1:4], big[:, 1:4], TINY, None, ALU.max))
            step(dve.tensor_scalar(big[:, 4:5], mxa[:, 5:6], TINY_ATT, None, ALU.max))
            step(dve.tensor_tensor(mxa[:, 6:7], mxa[:, 6:7], mxa[:, 7:8], ALU.max))
            step(dve.scalar_tensor_tensor(out=big[:, 5:6], in0=big[:, 4:5], scalar=float(D), in1=mxa[:, 6:7],
                                          op0=ALU.mult, op1=ALU.add))
            step(dve.reciprocal(q[:, :], big[:, :]))
            step(dve.tensor_tensor(q[:, :], q[:, :], capn[:, :], ALU.mult))
            step(dve.tensor_scalar(q[:, :].bitcast(U32), q[:, :].bitcast(U32), EXPONENT, None, ALU.bitwise_and))
            step(dve.reciprocal(qi[:, :], q[:, :]))
            step(dve.tensor_scalar(epsq, qc, qc, EPS, ALU.mult, ALU.mult))
            step(dve.tensor_scalar(bscale, q1, qi[:, 0:1], STD_SHIFT, ALU.mult, ALU.mult))
            step(dve.tensor_scalar(sc[:, 3:4], qc, qi[:, 1:2], None, ALU.mult))
            step(dve.tensor_scalar(aev, sa, qi[:, 4:5], None, ALU.mult))
            step(dve.tensor_scalar(sc[:, 6:7], qi[:, 5:6], qi[:, 5:6], None, ALU.mult))
            step(dve.tensor_scalar(iys, sc[:, 6:7], qi[:, 5:6], 1.0 / S_SHIFT, ALU.mult, ALU.mult))
            step(dve.tensor_scalar(bqk[:, :, :], bqk[:, :, :], sa, None, ALU.mult))
            step(dve.tensor_scalar(bvB[:, :], bvB[:, :], sa, None, ALU.mult))
            dve.tensor_scalar(kappa, sc[:, 3:4], qi[:, 2:3], None, ALU.mult).then_inc(p_q, 1)
            dve.wait_ge(p_q, 1)
            step(dve.tensor_scalar(routw[:, :, 0:E], rwg[:, :, :], qr, None, ALU.mult))
            step(dve.scalar_tensor_tensor(out=routw[:, :, E:2 * E], in0=rwg[:, :, :], scalar=qr,
                                          in1=routw[:, :, 0:E], op0=ALU.mult, op1=ALU.subtract))
            step(dve.tensor_scalar(beth[:, :], betr[:, :], bscale[0:NSTD], None, ALU.mult))
            step(dve.scalar_tensor_tensor(out=betl[:, :], in0=betr[:, :], scalar=bscale[0:NSTD], in1=beth[:, :],
                                          op0=ALU.mult, op1=ALU.subtract))
            step(dve.tensor_tensor(pick[:, 0:E], identf[0:NSTD, 0:E], identf[0:NSTD, E:2 * E], ALU.add))
            step(dve.tensor_reduce(pick[:, E:E + 1], pick[:, 0:E], AX.X, ALU.add))
            step(dve.tensor_tensor(pick[:, 0:E], pick[:, 0:E], identf[0:NSTD, 2 * E:3 * E], ALU.add))
            step(dve.tensor_scalar(pick[:, E + 1:E + 2], pick[:, E:E + 1], -1.0, 1.0, ALU.mult, ALU.add))
            step(dve.tensor_scalar(betl[:, :], betl[:, :], pick[:, E + 1:E + 2], None, ALU.mult))
            step(dve.scalar_tensor_tensor(out=betv[:, :], in0=beth[:, :], scalar=pick[:, E:E + 1], in1=betl[:, :],
                                          op0=ALU.mult, op1=ALU.add))
            for e in range(E):
                step(dve.tensor_scalar(betas[:, e, :], betv[:, :], pick[:, e:e + 1], None, ALU.mult))
            dve.wait_ge(p_rt, 2)
            step(dve.tensor_copy(routc[:, :], bank[7][:, 0:E]))
            dve.wait_ge(l_on, 32)
            step(dve.tensor_scalar(ong[:, :], ong[:, :], 0.5, None, ALU.mult))
            step(dve.tensor_scalar(onb[:, :], onb[:, :], 0.5, None, ALU.mult))
            for e in range(E):
                dve.wait_ge(p_hi, e + 1)
                dve.scalar_tensor_tensor(out=w1l[:, e].rearrange("p c n -> p (c n)"),
                                         in0=w1g[:, e].rearrange("p c n -> p (c n)"), scalar=q1,
                                         in1=w1h[:, e].rearrange("p c n -> p (c n)"),
                                         op0=ALU.mult, op1=ALU.subtract)
                dve.wait_ge(p_gh, e + 1)
                dve.scalar_tensor_tensor(out=graml[:, :, e, :],
                                         in0=bank[4 + e % 2][:, :].rearrange("p (c n) -> p c n", c=KC),
                                         scalar=1.0 / H, in1=gramh[:, :, e, :],
                                         op0=ALU.mult, op1=ALU.subtract).then_inc(p_gl, 1)
            for e in range(E):
                dve.wait_ge(p_hi, E + e + 1)
                last = dve.scalar_tensor_tensor(out=w2l[:, e].rearrange("p c n -> p (c n)"),
                                                in0=w2r[:, e].rearrange("p c n -> p (c n)"), scalar=q2,
                                                in1=w2h[:, e].rearrange("p c n -> p (c n)"),
                                                op0=ALU.mult, op1=ALU.subtract)
            last.then_inc(p_gl, 1)
            for k in range(3):
                dve.wait_ge(a_wh, k + 1)
                dve.scalar_tensor_tensor(out=wTl[:, k].rearrange("p c n -> p (c n)"), in0=bank[k][:, :], scalar=qa,
                                         in1=wTh[:, k].rearrange("p c n -> p (c n)"),
                                         op0=ALU.mult, op1=ALU.subtract).then_inc(a_wl, 1)
            dve.wait_ge(l_x, 16 * NBLK)

            def x_stats(g, t0):
                wait(dve, s_rs, g)
                for t in range(TB):
                    last = dve.bn_stats(xst[:, t, :], X[:, t0 + t, :])
                last.then_inc(s_mv, 1)

            def hT_low(g, par):
                for c in range(KC):
                    wait(dve, s_hTh, KC * g + (c + 1))
                    dve.tensor_tensor(hTl[:, par, c, :], bank[6 + c][:, :], hTh[:, par, c, :],
                                      ALU.subtract).then_inc(s_hTl, 1)

            def h_twice(n):
                wait(dve, s_hr, n + 1)
                wait(dve, s_var, NU * n)
                dve.scalar_tensor_tensor(out=h2.rearrange("p t d -> p (t d)"),
                                         in0=h[:, :, :].rearrange("p t d -> p (t d)"), scalar=2.0,
                                         in1=hr.rearrange("p t d -> p (t d)"),
                                         op0=ALU.mult, op1=ALU.subtract).then_inc(s_h2, 1)

            def logits_copy(n):
                wait(dve, s_L, n + 1)
                wait(dve, s_lgl, n)
                dve.tensor_copy(lsb[:, :, :].rearrange("p t e -> p (t e)"),
                                bank[6][:, 0:TB * 2 * E]).then_inc(s_lg, 1)

            def logits_max(n):
                wait(dve, s_lgl, n + 1)
                wait(dve, s_lgm, n)
                dve.tensor_reduce(lmax[:, :], lgc[:, :, :], AX.X, ALU.max).then_inc(s_lmax, 1)

            def variance(n, j):
                t, e0 = j // 2, 2 * (j % 2)
                if j == 0:
                    wait(dve, s_h2, n + 1)
                    wait(dve, s_sd, n)
                wait(dve, s_U, NU * n + (j + 1))
                for e in range(e0, e0 + 2):
                    last = dve.tensor_tensor_reduce(out=junk[:, t * E + e, :],
                                                    in0=bank[7 - j % 2][:, (e - e0) * D:(e - e0 + 1) * D],
                                                    in1=h2[:, t, :], scale=1.0, scalar=0.0, op0=ALU.mult,
                                                    op1=ALU.add, accum_out=var[:, t, e:e + 1])
                last.then_inc(s_var, 1)

            def std_parts(n, at):
                wait(dve, s_sd, n + 1)
                wait(dve, s_ST, n)
                at(dve.tensor_copy(s12[:, :, 0:E], sds[:, :, :]))
                dve.tensor_tensor(s12[:, :, E:2 * E], sds[:, :, :], s12[:, :, 0:E], ALU.subtract)
                dve.tensor_copy(s12[:, :, 2 * E:3 * E], s12[:, :, 0:E]).then_inc(s_s12, 1)

            def relu_low(n, e, m):
                a = e * HC + m
                wait(dve, s_Rh, NA * n + (a + 1))
                if m == 0:
                    wait(dve, s_O, NO * n + (e * TB - TB))
                dve.scalar_tensor_tensor(out=Rl[:, e % 2, m, :], in0=bank[m][:, :], scalar=0.0,
                                         in1=Rh[:, e % 2, m, :], op0=ALU.max, op1=ALU.subtract).then_inc(s_Rl, 1)

            def accumulate(n, par, e, t):
                o = e * TB + t
                if o == 0:
                    wait(dve, s_coef, n + 1)
                wait(dve, s_O, NO * n + (o + 1))
                src = bank[4 + t % 2][:, 0:D]
                if e == 0:
                    wait(dve, s_z, TB * (n - 1) + (t + 1))
                    ins = dve.tensor_scalar(acc[:, t, :], src, coef[:, par, t, e:e + 1], None, ALU.mult)
                else:
                    wait(dve, s_acc, NO * n + (o - TB + 1))
                    ins = dve.scalar_tensor_tensor(out=acc[:, t, :], in0=src, scalar=coef[:, par, t, e:e + 1],
                                                   in1=acc[:, t, :], op0=ALU.mult, op1=ALU.add)
                ins.then_inc(s_acc, 1)

            def acc_stats(n):
                wait(dve, s_acc, NO * (n + 1))
                wait(dve, s_ars, n)
                for t in range(TB):
                    last = dve.bn_stats(ast[:, t, :], acc[:, t, :])
                last.then_inc(s_amv, 1)

            def guard(n):
                wait(dve, s_var, NU * n + NU)
                wait(dve, s_rsd, n)
                dve.tensor_scalar(vare[:, :, :], var[:, :, :], 0.0, epsq, ALU.max, ALU.add).then_inc(s_vare, 1)

            def choose(n, at):
                wait(dve, s_E, n + 1)
                other = ex[:, :, :].unsqueeze(2).to_broadcast([P, TB, E, E])
                own = ex[:, :, :].unsqueeze(3).to_broadcast([P, TB, E, E])
                dve.tensor_tensor(gt[:, :, :, :], other, own, ALU.is_gt)
                at(dve.tensor_tensor(ge[:, :, :, :], other, own, ALU.is_ge))
                for m, mask in ((gt, after), (ge, before)):
                    last = dve.tensor_tensor(m[:, :, :, :], m[:, :, :, :],
                                             mask[:, :, :].unsqueeze(1).to_broadcast([P, TB, E, E]), ALU.mult)
                at(last)
                at(dve.tensor_tensor(gt[:, :, :, :], gt[:, :, :, :], ge[:, :, :, :], ALU.add))
                at(dve.tensor_reduce(rank[:, :, :], gt[:, :, :, :], AX.X, ALU.add))
                at(dve.scalar_tensor_tensor(out=es[:, :, :], in0=rank[:, :, :], scalar=1.5, in1=ex[:, :, :],
                                            op0=ALU.is_lt, op1=ALU.mult))

            def weigh(n, par, at):
                dve.tensor_reduce(tot[:, 0], es[:, :, :], AX.X, ALU.add)
                at(dve.tensor_reduce(tot[:, 1], ex[:, :, :], AX.X, ALU.add))
                at(dve.scalar_tensor_tensor(out=den[:, :], in0=tot[:, 1], scalar=EPS_GATE, in1=tot[:, 0],
                                            op0=ALU.mult, op1=ALU.add))
                at(dve.reciprocal(rden[:, :], den[:, :]))
                at(dve.tensor_tensor(ws[:, :, :], es[:, :, :], rden[:, :].unsqueeze(2).to_broadcast([P, TB, E]),
                                     ALU.mult))
                wait(dve, s_rsd, n + 1)
                wait(dve, s_acc, NO * (n - 1))
                dve.scalar_tensor_tensor(out=coef[:, par], in0=ws[:, :, :], scalar=kappa, in1=rsd[:, :, :],
                                         op0=ALU.mult, op1=ALU.mult).then_inc(s_coef, 1)

            def ffn(f):
                n0 = f * NBLK
                g0 = 2 * f * NBLK
                at = Steps(dve, dve_done, step.at)
                x_stats(g0, 0)
                hT_low(g0, 0)
                h_twice(n0)
                logits_copy(n0)
                for j in range(NU // 2):
                    variance(n0, j)
                logits_max(n0)
                for j in range(NU // 2, NU):
                    variance(n0, j)
                guard(n0)
                std_parts(n0, at)
                choose(n0, at)
                weigh(n0, 0, at)
                start = at.at
                per = 10

                def body(n, par, last):
                    first = isinstance(n, int) and n == n0
                    at = Steps(dve, dve_done, start if first else (n - n0) * per + start)
                    if not first:
                        acc_stats(n - 1)
                    if not last:
                        x_stats(n + (1 + g0 - n0), tile0(n + 1, n0, 1 - par))
                    for m in range(HC):
                        relu_low(n, 0, m)
                    for m in range(HC):
                        relu_low(n, 1, m)
                    if not last:
                        hT_low(n + (1 + g0 - n0), 1 - par)
                        h_twice(n + 1)
                    for t in range(TB):
                        accumulate(n, par, 0, t)
                    if not last:
                        logits_copy(n + 1)
                    for m in range(HC):
                        relu_low(n, 2, m)
                        if not last:
                            variance(n + 1, m)
                    if not last:
                        logits_max(n + 1)
                    for t in range(TB):
                        accumulate(n, par, 1, t)
                    for m in range(HC):
                        relu_low(n, 3, m)
                        if not last:
                            variance(n + 1, 4 + m)
                    if not last:
                        guard(n + 1)
                    for t in range(TB):
                        accumulate(n, par, 2, t)
                        if t == 1 and not last:
                            std_parts(n + 1, at)
                    for t in range(TB):
                        accumulate(n, par, 3, t)
                        if t == 0 and not last:
                            choose(n + 1, at)
                        if t == 1 and not last:
                            weigh(n + 1, 1 - par, at)
                    return at

                at = blocks(dve, n0, body)
                acc_stats(n0 + NBLK - 1)
                step.at = at.at

            def attention():
                dve.wait_ge(s_x, TB * NBLK)

                def query_low(n, par):
                    wait(dve, a_qh, n + 1)
                    for half in range(2):
                        wait(dve, a_qx[half], NX * n)
                    dve.tensor_tensor(qp[:, :, 1], qf[:, par], qp[:, :, 0], ALU.subtract).then_inc(a_qp, 1)

                def ktok_low(n, par):
                    for j in range(2):
                        wait(dve, a_kth, 2 * n + (j + 1))
                        rows = slice(2 * j, 2 * j + 2)
                        dve.tensor_tensor(ktok[:, par, 1, rows].rearrange("p t d -> p (t d)"), bank[6 + j][:, :],
                                          ktok[:, par, 0, rows].rearrange("p t d -> p (t d)"),
                                          ALU.subtract).then_inc(a_ktl, 1)

                def values(n):
                    wait(dve, a_kt, 2 * n + 2)
                    wait(dve, a_kl, n + 1)
                    for j in range(2):
                        wait(dve, a_v, 2 * n + (j + 1))
                        dve.scalar_tensor_tensor(out=vf[:, 2 * j:2 * j + 2],
                                                 in0=bank[6 + j][:, :].rearrange("p (t d) -> p t d", t=2), scalar=aev,
                                                 in1=bvB[:, :].unsqueeze(1).to_broadcast([P, 2, D]),
                                                 op0=ALU.mult, op1=ALU.add).then_inc(a_vf, 1)

                def value_low(n, par):
                    wait(dve, a_vh, n + 1)
                    dve.tensor_tensor(vtok[:, par, 1], vf, vtok[:, par, 0], ALU.subtract).then_inc(a_vl, 1)

                def mask_scores(c, g):
                    wait(dve, a_s, NG * c + (g + 1))
                    if g < NG - 1:
                        wait(dve, a_sl, (NG - 1) * (c - 1) + (g + 1))
                    else:
                        wait(dve, a_sll, c)
                    dve.scalar_tensor_tensor(out=sm[:, g], in0=bank[g][:, :].rearrange("p (j t) -> p j t", j=4),
                                             scalar=S_SHIFT, in1=causal[:, :].unsqueeze(1).to_broadcast([P, 4, P]),
                                             op0=ALU.mult, op1=ALU.mult).then_inc(a_sm, 1)

                def last_score_low(c, cp):
                    wait(dve, a_sh, NG * c + NG)
                    wait(dve, a_y, c - 1)
                    dve.tensor_tensor(shl[:, cp, 1, NG - 1], sm[:, NG - 1], shl[:, cp, 0, NG - 1],
                                      ALU.subtract).then_inc(a_sll, 1)

                def update_x(c, tile):
                    wait(dve, a_wo, c + 1)
                    dve.tensor_tensor(X[:, tile, :], bank[5][:, 0:D], X[:, tile, :], ALU.add).then_inc(a_x, 1)

                def mask_kv(c):
                    wait(dve, a_dz, c + 1)
                    wait(dve, a_z, c)
                    dve.scalar_tensor_tensor(out=dz, in0=bank[5][:, 0:D].rearrange("p (c v) -> p c v", c=KC),
                                             scalar=S_SHIFT, in1=sameh[:, :].unsqueeze(1).to_broadcast([P, KC, P]),
                                             op0=ALU.mult, op1=ALU.mult).then_inc(a_dzm, 1)

                x_stats(NBLK, 0)
                hT_low(NBLK, 0)
                query_low(0, 0)
                ktok_low(0, 0)
                values(0)
                value_low(0, 0)
                for g in range(NG):
                    mask_scores(0, g)
                last_score_low(0, 0)

                def body(n, par, last):
                    for t in range(TB):
                        c = n * TB + t
                        more = not (last and t == TB - 1)
                        if t == 0 and not last:
                            x_stats(n + (NBLK + 1), tile0(n + 1, 0, 1 - par))
                        if more:
                            mask_scores(c + 1, 0)
                            mask_scores(c + 1, 1)
                        if t > 0:
                            if t == 1:
                                wait(dve, a_xb, n + 1)
                            update_x(c - 1, tile0(n, 0, par) + (t - 1))
                        elif not (isinstance(n, int) and n == 0):
                            update_x(c - 1, tile0(n - 1, 0, 1 - par) + (TB - 1))
                        if more:
                            mask_scores(c + 1, 2)
                            mask_scores(c + 1, 3)
                        if not last:
                            if t == 1:
                                hT_low(n + (NBLK + 1), 1 - par)
                            if t == 2:
                                ktok_low(n + 1, 1 - par)
                            if t == 3:
                                value_low(n + 1, 1 - par)
                        if more:
                            last_score_low(c + 1, (t + 1) % 2)
                        mask_kv(c)
                        if t == 1 and not last:
                            query_low(n + 1, 1 - par)
                        if t == 2 and not last:
                            values(n + 1)

                blocks(dve, 0, body)
                update_x(TB * NBLK - 1, NT - 1)

            ffn(0)
            attention()
            dve.wait_ge(a_x, TB * NBLK)
            ffn(1)

        @block.scalar
        def _(act):
            act.dma_start(gamB[:, :, :].rearrange("p e n -> p (e n)"),
                          ln_g.rearrange("(a e) n -> a (e n)", a=1).to_broadcast([P, E * H])).then_inc(l_gam, 16)
            act.dma_start(rw[:, :], router_w).then_inc(l_rw, 16)
            act.dma_start(rngc[:, :], rn_g.rearrange("(c p) -> p c", p=P), allow_slow_non_contiguous=True).then_inc(l_rw, 16)
            act.dma_start(rnbc[:, :], rn_b.rearrange("(c p) -> p c", p=P), allow_slow_non_contiguous=True).then_inc(l_rw, 16)
            for k, v in enumerate((bq, bk)):
                act.dma_start(bqk[:, k, :], v.rearrange("(c p) -> p c", p=P),
                              allow_slow_non_contiguous=True).then_inc(l_att, 16)
            for d, v in ((bvB, bv), (boB, bo)):
                act.dma_start(d[:, :], v.rearrange("(a n) -> a n", a=1).to_broadcast([P, D])).then_inc(l_att, 16)
            act.dma_start(ong[:, :], on_g.rearrange("(a n) -> a n", a=1).to_broadcast([P, D])).then_inc(l_on, 16)
            act.dma_start(onb[:, :], on_b.rearrange("(a n) -> a n", a=1).to_broadcast([P, D])).then_inc(l_on, 16)
            act.wait_ge(p_q, 1)
            for e in range(E):
                for b in range(2):
                    act.wait_ge(p_wt, 2 * e + b + 1)
                    if e >= 2 and b == 0:
                        act.wait_ge(p_g, e - 1)
                    act.activation(w1T[:, e % 2, 2 * b:2 * b + 2, :].rearrange("p c n -> p (c n)"),
                                   bank[2 * (e % 2) + b][:, :], ACT.Copy, scale=qc).then_inc(p_wtc, 1)
                act.activation(w1h[:, e].rearrange("p c n -> p (c n)"), w1g[:, e].rearrange("p c n -> p (c n)"),
                               ACT.Copy, scale=q1).then_inc(p_hi, 1)
                act.wait_ge(p_g, e + 1)
                act.activation(gramh[:, :, e, :], bank[4 + e % 2][:, :].rearrange("p (c n) -> p c n", c=KC),
                               ACT.Copy, scale=1.0 / H).then_inc(p_gh, 1)
            for e in range(E):
                act.activation(w2h[:, e].rearrange("p c n -> p (c n)"), w2r[:, e].rearrange("p c n -> p (c n)"),
                               ACT.Copy, scale=q2).then_inc(p_hi, 1)
            for k in range(3):
                act.wait_ge(a_w, k + 1)
                act.activation(wTh[:, k].rearrange("p c n -> p (c n)"), bank[k][:, :], ACT.Copy,
                               scale=qa).then_inc(a_wh, 1)
            act.wait_ge(a_w, 4)
            act.activation(woT[:, :, :].rearrange("p c n -> p (c n)"), bank[3][:, :], ACT.Copy).then_inc(a_wh, 1)

            def h_rows(g, t0, used):
                wait(act, s_rs, g + 1)
                wait(act, s_T, KC * g)
                wait(act, s_h2, used)
                for t in range(TB):
                    last = act.activation(h[:, t, :], X[:, t0 + t, :], ACT.Identity,
                                          bias=xnr[:, t:t + 1], scale=xrs[:, t:t + 1])
                last.then_inc(s_h, 1)

            def h_round(g):
                act.wait_ge(s_h, g + 1)
                act.activation(hr.rearrange("p t d -> p (t d)"), h[:, :, :].rearrange("p t d -> p (t d)"),
                               ACT.Copy).then_inc(s_hr, 1)

            def hT_high(g, par):
                for c in range(KC):
                    wait(act, s_T, KC * g + (c + 1))
                    act.activation(hTh[:, par, c, :], bank[6 + c][:, :], ACT.Copy).then_inc(s_hTh, 1)

            def exps(n):
                wait(act, s_lgm, n + 1)
                wait(act, s_coef, n)
                act.activation(ex[:, :, :], lgd[:, :, :], ACT.Exp).then_inc(s_E, 1)

            def std_T(n, par):
                wait(act, s_ST, n + 1)
                act.activation(sdT[:, par, :], bank[7][0:NSTD, 0:BT // 2].bitcast(F16), ACT.Copy).then_inc(s_sdT, 1)

            def relu_high(n, e, m):
                a = e * HC + m
                wait(act, s_A, NA * n + (a + 1))
                if m == 0:
                    wait(act, s_O, NO * n + (e * TB - TB))
                act.activation(Rh[:, e % 2, m, :], bank[m][:, :], ACT.Relu).then_inc(s_Rh, 1)

            def z_rows(n):
                for t in range(TB):
                    wait(act, s_ars, n + 1)
                    wait(act, s_x, TB * (n - 1) + (t + 1))
                    act.activation(z[:, t, :], acc[:, t, :], ACT.Identity,
                                   bias=anr[:, t:t + 1], scale=ars[:, t:t + 1]).then_inc(s_z, 1)

            def ffn(f):
                n0 = f * NBLK
                dg = n0 + 1
                h_rows(2 * n0, 0, n0)
                h_round(2 * n0)
                hT_high(2 * n0, 0)
                exps(n0)
                std_T(n0, 0)

                def body(n, par, last):
                    for m in range(HC):
                        relu_high(n, 0, m)
                    if not (isinstance(n, int) and n == n0):
                        z_rows(n - 1)
                    if not last:
                        h_rows(n + dg, tile0(n + 1, n0, 1 - par), n + 1)
                        h_round(n + dg)
                    for m in range(HC):
                        relu_high(n, 1, m)
                    if not last:
                        wait(act, s_A, NA * n)
                        hT_high(n + dg, 1 - par)
                    for m in range(HC):
                        relu_high(n, 2, m)
                    if not last:
                        exps(n + 1)
                    for m in range(HC):
                        relu_high(n, 3, m)
                    if not last:
                        std_T(n + 1, 1 - par)

                blocks(act, n0, body)
                z_rows(n0 + NBLK - 1)

            def attention():
                act.wait_ge(s_x, TB * NBLK)

                def qk_copy(n, par, k, dst):
                    if k == 1:
                        wait(act, a_vl, n)
                    for c in range(KC):
                        wait(act, a_qk, 4 * n + (2 * k + c + 1))
                        act.activation(dst[:, c], bank[6 + c][:, :], ACT.Identity, bias=bqk[:, k, c:c + 1],
                                       scale=aev).then_inc(a_qf, 1)

                def query_high(n, par):
                    for half in range(2):
                        wait(act, a_qx[half], NX * n)
                    wait(act, a_qf, 4 * n + 2)
                    act.activation(qp[:, :, 0], qf[:, par], ACT.Copy).then_inc(a_qh, 1)

                def key_high(n, par):
                    wait(act, a_qf, 4 * n + 4)
                    act.activation(kp[:, par, :, 0], kf, ACT.Copy).then_inc(a_kh, 1)

                def ktok_high(n, par):
                    for j in range(2):
                        wait(act, a_kt, 2 * n + (j + 1))
                        act.activation(ktok[:, par, 0, 2 * j:2 * j + 2].rearrange("p t d -> p (t d)"),
                                       bank[6 + j][:, :], ACT.Copy).then_inc(a_kth, 1)

                def value_high(n, par):
                    wait(act, a_vf, 2 * n + 2)
                    act.activation(vtok[:, par, 0], vf, ACT.Copy).then_inc(a_vh, 1)

                def score_high(c, cp, g):
                    wait(act, a_sm, NG * c + (g + 1))
                    wait(act, a_y, c - 1)
                    act.activation(shl[:, cp, 0, g], sm[:, g], ACT.Copy).then_inc(a_sh, 1)

                def y_copy(c):
                    wait(act, a_y, c + 1)
                    wait(act, a_yt, c)
                    act.activation(ysb, bank[4][:, 0:D], ACT.Copy, scale=iys).then_inc(a_ysb, 1)

                def yT_copy(c):
                    wait(act, a_yt, c + 1)
                    wait(act, a_wo, c)
                    act.activation(yT, bank[4][:, 0:D].rearrange("p (c t) -> p c t", c=KC),
                                   ACT.Copy).then_inc(a_ytc, 1)

                h_rows(NBLK, 0, NBLK)
                hT_high(NBLK, 0)
                qk_copy(0, 0, 0, qf[:, 0])
                query_high(0, 0)
                qk_copy(0, 0, 1, kf)
                key_high(0, 0)
                ktok_high(0, 0)
                value_high(0, 0)
                for g in range(NG):
                    score_high(0, 0, g)

                def body(n, par, last):
                    for t in range(TB):
                        c = n * TB + t
                        if t > 0 or not (isinstance(n, int) and n == 0):
                            yT_copy(c - 1)
                        if t == 1 and not last:
                            h_rows(n + (NBLK + 1), tile0(n + 1, 0, 1 - par), NBLK)
                        if t == 2 and not last:
                            key_high(n + 1, 1 - par)
                        if t == 3 and not last:
                            value_high(n + 1, 1 - par)
                        if not (last and t == TB - 1):
                            for g in range(NG):
                                score_high(c + 1, (t + 1) % 2, g)
                        if t == 1 and not last:
                            hT_high(n + (NBLK + 1), 1 - par)
                        if t == 2 and not last:
                            ktok_high(n + 1, 1 - par)
                        y_copy(c)
                        if t == 1 and not last:
                            qk_copy(n + 1, 1 - par, 0, qf[:, 1 - par])
                            query_high(n + 1, 1 - par)
                            qk_copy(n + 1, 1 - par, 1, kf)

                blocks(act, 0, body)
                yT_copy(TB * NBLK - 1)

            ffn(0)
            attention()
            act.wait_ge(a_x, TB * NBLK)
            ffn(1)

        @block.tensor
        def _(pe):
            pe.wait_ge(p_id, 1)
            pe.wait_ge(l_rw, 48)
            for c in range(KC):
                last = pe.transpose(bank[6][:, c * E:(c + 1) * E], rw[:, c * P:(c + 1) * P], identf[0:E, 0:E])
            last.then_inc(p_rt, 1)
            pe.wait_ge(p_rc, 1)
            for c in range(KC):
                last = pe.matmul(bank[7][:, 0:E], rnbB[:, c, :], rwT[:, c, :], start=(c == 0), stop=(c == KC - 1))
            last.then_inc(p_rt, 1)
            pe.wait_ge(p_c, 1)
            for e in range(E + 1):
                if e < E:
                    for b in range(2):
                        if e >= 2:
                            pe.wait_ge(p_wtc, 2 * (e - 2) + b + 1)
                        for j in range(2):
                            for c in range(KC):
                                last = pe.transpose(bank[2 * (e % 2) + b][:, j * D + c * P:j * D + (c + 1) * P],
                                                    w1r[:, e, c, (2 * b + j) * P:(2 * b + j + 1) * P], identf[:, :])
                        last.then_inc(p_wt, 1)
                if e >= 1:
                    g = e - 1
                    pe.wait_ge(p_wtc, 2 * g + 2)
                    if g >= 2:
                        pe.wait_ge(p_gl, g - 1)
                    for c in range(KC):
                        for k in range(HC):
                            last = pe.matmul(bank[4 + g % 2][:, c * D:(c + 1) * D], w1T[:, g % 2, k, c * P:(c + 1) * P],
                                             w1T[:, g % 2, k, :], start=(k == 0), stop=(k == HC - 1))
                    last.then_inc(p_g, 1)
            pe.wait_ge(p_gl, E + 1)
            pe.wait_ge(l_att, 16 * 8)
            for k in range(4):
                for c in range(KC):
                    for o in range(KC):
                        last = pe.transpose(bank[k][:, c * D + o * P:c * D + (o + 1) * P],
                                            wqkv[:, k, o, c * P:(c + 1) * P], identf[:, :])
                last.then_inc(a_w, 1)
            pe.wait_ge(a_wl, 3)
            pe.wait_ge(a_wh, 4)

            def h_T(g):
                wait(pe, s_h, g + 1)
                for c in range(KC):
                    for t in range(TB):
                        last = pe.transpose(bank[6 + c][:, t * P:(t + 1) * P], h[:, t, c * P:(c + 1) * P], identf[:, :])
                    last.then_inc(s_T, 1)

            def router(n, g, par):
                wait(pe, s_hTl, KC * g + KC)
                for t in range(TB):
                    rows = slice(t * P, (t + 1) * P)
                    o = bank[6][:, t * 2 * E:(t + 1) * 2 * E]
                    pe.matmul(o, hTh[:, par, 0, rows], routw[:, 0, :], start=True, stop=False)
                    pe.matmul(o, hTh[:, par, 1, rows], routw[:, 1, :], start=False, stop=False)
                    pe.matmul(o[:, 0:E], hTl[:, par, 0, rows], routw[:, 0, 0:E], start=False, stop=False)
                    last = pe.matmul(o[:, 0:E], hTl[:, par, 1, rows], routw[:, 1, 0:E], start=False, stop=True)
                last.then_inc(s_L, 1)

            def gram(n, par, j):
                t, e0 = j // 2, 2 * (j % 2)
                if j == 1:
                    wait(pe, s_lg, n + 1)
                if j >= 2:
                    wait(pe, s_var, NU * n + (j - 1))
                for c in range(KC):
                    for part, g in enumerate((gramh, graml)):
                        last = pe.matmul(bank[7 - j % 2][:, :], hTh[:, par, c, t * P:(t + 1) * P],
                                         g[:, c, e0:e0 + 2, :].rearrange("p e n -> p (e n)"),
                                         start=(c == 0 and part == 0), stop=(c == KC - 1 and part == 1))
                last.then_inc(s_U, 1)

            def std_rows(n):
                wait(pe, s_s12, n + 1)
                o = bank[7][0:NSTD, 0:BT // 2].bitcast(F16)
                for t in range(TB):
                    last = pe.transpose(o[:, t * P:(t + 1) * P], s12[:, t, :], ident16[:, :])
                last.then_inc(s_ST, 1)

            def layer1(n, par, e, m):
                a = e * HC + m
                wait(pe, s_Rl, NA * n + (a - HC + 1))
                cols = slice(m * P, (m + 1) * P)
                o = bank[m][:, :]
                for c in range(KC):
                    pe.matmul(o, w1h[:, e, c, cols], hTh[:, par, c, :], start=(c == 0), stop=False)
                    pe.matmul(o, w1h[:, e, c, cols], hTl[:, par, c, :], start=False, stop=False)
                    pe.matmul(o, w1l[:, e, c, cols], hTh[:, par, c, :], start=False, stop=False)
                if a == 0:
                    wait(pe, s_sdT, n + 1)
                pe.matmul(o, betas[:, e, cols], sdT[:, par, :], start=False, stop=True).then_inc(s_A, 1)

            def layer2(n, e, t):
                o = e * TB + t
                if t == 0:
                    wait(pe, s_Rl, NA * n + (e + 1) * HC)
                wait(pe, s_acc, NO * n + (o - 1))
                rows = slice(t * P, (t + 1) * P)
                dst = bank[4 + t % 2][:, 0:D]
                for k in range(HC):
                    pe.matmul(dst, Rh[:, e % 2, k, rows], w2h[:, e, k, :], start=(k == 0), stop=False)
                    pe.matmul(dst, Rh[:, e % 2, k, rows], w2l[:, e, k, :], start=False, stop=False)
                    last = pe.matmul(dst, Rl[:, e % 2, k, rows], w2h[:, e, k, :], start=False, stop=(k == HC - 1))
                last.then_inc(s_O, 1)

            def ffn(f):
                n0 = f * NBLK
                dg = n0 + 1
                h_T(2 * n0)
                router(n0, 2 * n0, 0)
                for j in range(NU):
                    gram(n0, 0, j)
                std_rows(n0)

                def body(n, par, last):
                    for m in range(HC):
                        layer1(n, par, 0, m)
                    for m in range(HC):
                        layer1(n, par, 1, m)
                    if not last:
                        wait(pe, s_var, NU * (n + 1))
                        wait(pe, s_sdT, n + 1)
                        h_T(n + dg)
                    for t in range(TB):
                        layer2(n, 0, t)
                    if not last:
                        router(n + 1, n + dg, 1 - par)
                    for m in range(HC):
                        layer1(n, par, 2, m)
                        if not last:
                            gram(n + 1, 1 - par, m)
                    for t in range(TB):
                        layer2(n, 1, t)
                    for m in range(HC):
                        layer1(n, par, 3, m)
                        if not last:
                            gram(n + 1, 1 - par, 4 + m)
                    for t in range(TB):
                        layer2(n, 2, t)
                    for t in range(TB):
                        layer2(n, 3, t)
                        if t == 0 and not last:
                            std_rows(n + 1)

                blocks(pe, n0, body)

            def attention():
                pe.wait_ge(s_x, TB * NBLK)

                def split_product(o, lhs, rhs, start, stop, **kw):
                    (lh, ll), (rh, rl) = lhs, rhs
                    pe.matmul(o, lh, rh, start=start, stop=False, **kw)
                    pe.matmul(o, lh, rl, start=False, stop=False, **kw)
                    return pe.matmul(o, ll, rh, start=False, stop=stop, **kw)

                def rows_T(n):
                    wait(pe, a_vf, 2 * n)
                    h_T(n + NBLK)

                def queries_keys(n, par):
                    for k in range(2):
                        for m in range(KC):
                            if k == 0:
                                wait(pe, s_hTl, KC * n + (KC * NBLK + m + 1))
                                if m == 0:
                                    wait(pe, s_hTl, KC * n + (KC * NBLK + KC))
                            else:
                                wait(pe, a_qf, 4 * n + (m + 1))
                            cols = slice(m * P, (m + 1) * P)
                            for c in range(KC):
                                last = split_product(bank[6 + m][:, :],
                                                     (wTh[:, k, c, cols], wTl[:, k, c, cols]),
                                                     (hTh[:, par, c, :], hTl[:, par, c, :]),
                                                     c == 0, c == KC - 1)
                            last.then_inc(a_qk, 1)

                def keys_T(n):
                    wait(pe, a_qf, 4 * n + 4)
                    for j in range(2):
                        for t in range(2 * j, 2 * j + 2):
                            for m in range(KC):
                                last = pe.transpose(bank[6 + j][:, (t % 2) * D + m * P:(t % 2) * D + (m + 1) * P],
                                                    kf[:, m, t * P:(t + 1) * P], identf[:, :])
                        last.then_inc(a_kt, 1)

                def values(n, par):
                    for j in range(2):
                        wait(pe, a_ktl, 2 * n + (j + 1))
                        for t in range(2 * j, 2 * j + 2):
                            rows = slice(t * P, (t + 1) * P)
                            for c in range(KC):
                                last = split_product(bank[6 + j][:, (t % 2) * D:(t % 2 + 1) * D],
                                                     (hTh[:, par, c, rows], hTl[:, par, c, rows]),
                                                     (wTh[:, 2, c, :], wTl[:, 2, c, :]),
                                                     c == 0, c == KC - 1)
                        last.then_inc(a_v, 1)

                def scores(c, n, par, t, g):
                    if g == 0:
                        if t == 0:
                            wait(pe, a_kl, n + 1)
                        if t % 2 == 0:
                            wait(pe, a_qx[t // 2], NX * n + NX)
                    wait(pe, a_sm, NG * (c - 1) + (g + 1))
                    m, j0 = g // 2, 4 * (g % 2)
                    cols = slice(t * P, (t + 1) * P)
                    split_product(bank[g][:, :].rearrange("p (j t) -> p j t", j=4),
                                  (kp[:, par, m, 0, cols], kp[:, par, m, 1, cols]),
                                  (qx[:, j0:j0 + 4, m, 0, cols], qx[:, j0:j0 + 4, m, 1, cols]),
                                  True, True).then_inc(a_s, 1)

                def outputs(c, n, par, t):
                    wait(pe, a_z, c)
                    wait(pe, a_ytc, c)
                    cols = slice(t * P, (t + 1) * P)
                    for m in range(KC):
                        pe.matmul(bank[4][:, m * P:(m + 1) * P], qf[:, par, m, cols], zst[:, par, m, :],
                                  start=(m == 0), stop=False, skip_group_check=True)
                    wait(pe, a_sl, (NG - 1) * c + (NG - 1))
                    wait(pe, a_sll, c + 1)
                    if t == 0:
                        wait(pe, a_vl, n + 1)
                    for hd in range(4 * NG):
                        vs = slice(hd * HD, (hd + 1) * HD)
                        g, j = hd // 4, hd % 4
                        last = split_product(bank[4][:, vs], (shl[:, t % 2, 0, g, j], shl[:, t % 2, 1, g, j]),
                                             (vtok[:, par, 0, t, vs], vtok[:, par, 1, t, vs]),
                                             False, hd == 4 * NG - 1, skip_group_check=True)
                    last.then_inc(a_y, 1)

                def keys_values(c, par, t):
                    wait(pe, a_x, c)
                    for m in range(KC):
                        cols = slice(m * P, (m + 1) * P)
                        last = split_product(bank[5][:, cols], (ktok[:, par, 0, t, cols], ktok[:, par, 1, t, cols]),
                                             (vtok[:, par, 0, t, cols], vtok[:, par, 1, t, cols]),
                                             True, True)
                    last.then_inc(a_dz, 1)

                def y_T(c):
                    wait(pe, a_ysb, c + 1)
                    for m in range(KC):
                        last = pe.transpose(bank[4][:, m * P:(m + 1) * P], ysb[:, m * P:(m + 1) * P], identf[:, :])
                    last.then_inc(a_yt, 1)

                def project(c):
                    wait(pe, a_ytc, c + 1)
                    wait(pe, a_dzm, c + 1)
                    for m in range(KC):
                        last = pe.matmul(bank[5][:, 0:D], yT[:, m, :], woT[:, m, :], start=(m == 0), stop=(m == KC - 1))
                    last.then_inc(a_wo, 1)

                rows_T(0)
                queries_keys(0, 0)
                keys_T(0)
                values(0, 0)
                for g in range(NG):
                    scores(0, 0, 0, 0, g)

                def body(n, par, last):
                    for t in range(TB):
                        c = n * TB + t
                        first = t == 0 and isinstance(n, int) and n == 0
                        more = not (last and t == TB - 1)
                        nn, np_ = (n, par) if t < TB - 1 else (n + 1, 1 - par)
                        for g in range(NG):
                            if more:
                                scores(c + 1, nn, np_, (t + 1) % TB, g)
                            if g == 0 and not first:
                                y_T(c - 1)
                            if g == 1 and not first:
                                project(c - 1)
                        if t == 1 and not last:
                            rows_T(n + 1)
                        if t == 2 and not last:
                            keys_T(n + 1)
                        outputs(c, n, par, t)
                        keys_values(c, par, t)
                        if t == 1 and not last:
                            queries_keys(n + 1, 1 - par)
                        if t == 2 and not last:
                            values(n + 1, 1 - par)

                blocks(pe, 0, body)
                y_T(TB * NBLK - 1)
                project(TB * NBLK - 1)

            ffn(0)
            attention()
            pe.wait_ge(a_x, TB * NBLK)
            ffn(1)


_INS = ['L0_attn_x', 'L0_attn_Wq', 'L0_attn_bq', 'L0_attn_Wk', 'L0_attn_bk', 'L0_attn_Wv', 'L0_attn_bv', 'L0_attn_Wo',
        'L0_attn_bo', 'L0_ffn_router_w', 'L0_ffn_rn_g', 'L0_ffn_rn_b', 'L0_ffn_w1', 'L0_ffn_ln_g', 'L0_ffn_ln_b',
        'L0_ffn_w2', 'L0_ffn_on_g', 'L0_ffn_on_b']
_OUTS = [((2, 2048, 256), 'float32')]


def kernel(**inputs):
    import numpy as _np
    import concourse.bacc as _bacc
    from concourse import mybir as _mybir
    from concourse.bass_utils import run_bass_kernel_spmd as _run

    nc = _bacc.Bacc("TRN2", target_bir_lowering=False, num_devices=1)
    arrays, args = {}, []
    for name in _INS:
        a = _np.ascontiguousarray(inputs[name])
        arrays[f"in_{name}_dram"] = a
        args.append(nc.dram_tensor(f"in_{name}_dram", a.shape, _mybir.dt.from_np(a.dtype), kind="ExternalInput").ap())
    for i, (shape, dtype) in enumerate(_OUTS):
        dt = _mybir.dt.from_np(_np.dtype(dtype))
        args.append(nc.dram_tensor(f"out_{i}_dram", shape, dt, kind="ExternalOutput").ap())
    macaron_kernel(nc, *args)
    r = _run(nc, [arrays], core_ids=[0])
    return r.results[0]["out_0_dram"]
```

```python
from contextlib import ExitStack

import concourse.bass as bass
from concourse import mybir

ALU = mybir.AluOpType
ACT = mybir.ActivationFunctionType
AX = mybir.AxisListType
F32 = mybir.dt.float32
F16 = mybir.dt.float16
U32 = mybir.dt.uint32
RMAX = bass.bass_isa.ReduceOp.max

P = 128
EPS = 1e-5
EPS_GATE = 1e-8
EXPONENT = 0x7F800000
TINY = 2.0 ** -40
TINY_ATT = 2.0 ** -16
S_SHIFT = 2.0 ** -19
STD_SHIFT = 64.0


def macaron_kernel(nc, x, Wq, bq, Wk, bk, Wv, bv, Wo, bo, router_w, rn_g, rn_b, w1, ln_g, ln_b, w2, on_g, on_b, out):
    NB, T, D = x.shape
    E, _, H = w1.shape
    NT = NB * T // P
    KC = D // P
    HC = H // P
    TB = 4
    BT = TB * P
    NBLK = NT // TB
    NSTD = 2 * E
    NV = 4
    NU = TB * E // 2
    NA = E * HC
    NO = E * TB
    HD = 16
    HPC = P // HD
    NG = D // HD // 4
    NX = 16 * HPC

    x_t = x.rearrange("b (n p) d -> p (b n) d", p=P)
    out_t = out.rearrange("b (n p) d -> p (b n) d", p=P)

    with ExitStack() as ctx:
        def sb(name, shape, dt=F32):
            return ctx.enter_context(nc.sbuf_tensor(name, shape, dt))

        def sem(name):
            return ctx.enter_context(nc.semaphore(name))

        bank = [ctx.enter_context(nc.psum_tensor(f"bank{i}", [P, 512], F32)) for i in range(8)]

        X = sb("X", [P, NT, D])
        w1h = sb("w1h", [P, E, KC, H], F16)
        w1l = sb("w1l", [P, E, KC, H], F16)
        w2h = sb("w2h", [P, E, HC, D], F16)
        w2l = sb("w2l", [P, E, HC, D], F16)
        gramh = sb("gramh", [P, KC, E, D], F16)
        graml = sb("graml", [P, KC, E, D], F16)
        betas = sb("betas", [P, E, HC])
        sel = sb("sel", [NSTD, E, P], F16)
        routw = sb("routw", [P, KC, 2 * E], F16)
        routc = sb("routc", [P, E])
        ong = sb("ong", [P, D])
        onb = sb("onb", [P, D])
        identf = sb("identf", [P, P])
        ident16 = sb("ident16", [P, P], F16)
        nhalf = sb("nhalf", [P, TB, E])
        phalf = sb("phalf", [P, TB, E])
        inv_std = sb("inv_std", [P, TB, E])
        consts = sb("consts", [P, 5, TB])
        half_, inv_d, eps_, mone = (consts[:, k] for k in range(4))
        before = sb("before", [P, E, E])
        after = sb("after", [P, E, E])

        area = sb("area", [P, 101 * 256])

        def at_kb(kb, shape, dt=F32):
            n = 1
            for k in shape:
                n *= k
            words = n if dt == F32 else n // 2
            assert 256 * kb + words <= 101 * 256
            v = area[:, int(256 * kb):int(256 * kb) + words]
            v = v if dt == F32 else v.bitcast(dt)
            names = "abcdef"[:len(shape)]
            if len(shape) == 1:
                return v
            return v.rearrange(f"p ({' '.join(names)}) -> p {' '.join(names)}", **dict(zip(names, shape)))

        Rh = at_kb(0, [2, HC, BT], F16)
        Rl = at_kb(8, [2, HC, BT], F16)
        junk = at_kb(84, [TB * E, D], F16)
        h2 = at_kb(24, [TB, D])
        hr = at_kb(32, [TB, D], F16)
        sdT = at_kb(34, [BT], F16)[0:NSTD]
        sdB = at_kb(16, [E, BT])
        V = at_kb(76, [NV, BT])
        acc = at_kb(28, [TB, D])
        z = at_kb(36, [TB, D])
        gamB = at_kb(0, [E, H])
        w1T = at_kb(8, [2, HC, D])
        wqkv = at_kb(16, [4, KC, D])
        w1r = at_kb(40, [E, KC, H])
        w1g = at_kb(56, [E, KC, H])
        w2r = at_kb(72, [E, HC, D])
        rnbB = at_kb(88, [KC, P])
        ones = at_kb(89, [P])
        sm = at_kb(0, [NG, 4, P])
        shl = at_kb(8, [2, 2, NG, 4, P], F16)
        ktok = at_kb(24, [2, 2, TB, D], F16)
        vtok = at_kb(32, [2, 2, TB, D], F16)
        qx = at_kb(40, [HPC, KC, 2, BT], F16)
        qf = at_kb(72, [2, KC, BT])
        kf = at_kb(80, [KC, BT])
        vf = at_kb(80, [TB, D])
        qp = at_kb(84, [KC, 2, BT], F16)
        kp = at_kb(88, [2, KC, 2, BT], F16)
        ysb = at_kb(96, [D])
        yT = at_kb(97, [KC, P])
        dz = at_kb(98, [KC, P])
        zst = at_kb(99, [2, KC, P])

        pick = sb("pick", [NSTD, E])
        rw = sb("rw", [E, D])
        rwT = sb("rwT", [P, KC, E])
        rwg = sb("rwg", [P, KC, E])
        rngc = sb("rngc", [P, KC])
        rnbc = sb("rnbc", [P, KC])
        rsum = sb("rsum", [P, E * KC])
        rmean = sb("rmean", [P, E * KC])
        NMX = 7
        mx = sb("mx", [P, NMX + 3])
        mxa = sb("mxa", [P, NMX + 3])
        big = sb("big", [P, 6])
        capn = sb("capn", [P, 6])
        q = sb("q", [P, 6])
        qi = sb("qi", [P, 6])
        sc = sb("sc", [P, 8])
        epsq, bscale, kappa, aev, iys = sc[:, 0:1], sc[:, 1:2], sc[:, 2:3], sc[:, 4:5], sc[:, 5:6]
        qc, q1, q2, qr, qri = q[:, 0:1], q[:, 1:2], q[:, 2:3], q[:, 3:4], qi[:, 3:4]
        qa, sa = q[:, 4:5], q[:, 5:6]
        wTh = sb("wTh", [P, 3, KC, D], F16)
        wTl = sb("wTl", [P, 3, KC, D], F16)
        woT = sb("woT", [P, KC, D])
        bqk = sb("bqk", [P, 2, KC])
        bvB = sb("bvB", [P, D])
        boB = sb("boB", [P, D])
        causal = sb("causal", [P, P])
        sameh = sb("sameh", [P, P])

        xst = sb("xst", [P, TB, 6])
        xf = sb("xf", [P, 12, TB])
        xrs, xnr = xf[:, 10], xf[:, 11]
        r2a = sb("r2a", [P, TB])
        r2b = sb("r2b", [P, TB])
        r2c = sb("r2c", [P, TB])
        r2d = sb("r2d", [P, TB])
        r2 = sb("r2", [P, TB])
        h = sb("h", [P, TB, D])
        hTh = sb("hTh", [P, 2, KC, BT], F16)
        hTl = sb("hTl", [P, 2, KC, BT], F16)
        lsb = sb("lsb", [P, TB, 2 * E])
        lga = sb("lga", [P, TB, E])
        lgb = sb("lgb", [P, TB, E])
        lgc = sb("lgc", [P, TB, E])
        lgd = sb("lgd", [P, TB, E])
        lmax = sb("lmax", [P, TB])
        ex = sb("ex", [P, TB, E])
        var = sb("var", [P, TB, E])
        vare = sb("vare", [P, TB, E])
        sd = sb("sd", [P, TB, E])
        sds = sb("sds", [P, TB, E])
        rsd = sb("rsd", [P, TB, E])
        s12 = sb("s12", [P, TB, NSTD], F16)
        gt = sb("gt", [P, TB, E, E])
        ge = sb("ge", [P, TB, E, E])
        rank = sb("rank", [P, TB, E])
        es = sb("es", [P, TB, E])
        ws = sb("ws", [P, TB, E])
        wr = sb("wr", [P, TB, E])
        tot = sb("tot", [P, 2, TB])
        den = sb("den", [P, TB])
        rden = sb("rden", [P, TB])
        coef = sb("coef", [P, 2, TB, E])
        ast = sb("ast", [P, TB, 6])
        af = sb("af", [P, 12, TB])
        ars, anr = af[:, 10], af[:, 11]

        l_att = sem("l_att")
        l_w1, l_w2, l_gam, l_bet, l_rw, l_on, l_x = (sem(n) for n in (
            "l_w1", "l_w2", "l_gam", "l_bet", "l_rw", "l_on", "l_x"))
        p_id = sem("p_id")
        p_c = sem("p_c")
        p_mx = sem("p_mx")
        p_mxa = sem("p_mxa")
        p_q = sem("p_q")
        p_hi = sem("p_hi")
        p_wt = sem("p_wt")
        p_wtc = sem("p_wtc")
        p_g = sem("p_g")
        p_gh = sem("p_gh")
        p_gl = sem("p_gl")
        p_rt = sem("p_rt")
        p_rc = sem("p_rc")
        (s_mv, s_rs, s_h, s_hr, s_T, s_hTh, s_hTl, s_h2, s_L, s_lg, s_lgl, s_lmax, s_lgm, s_E, s_U, s_var, s_sd,
         s_rsd, s_vare, s_s12, s_ST, s_sdT, s_coef, s_A, s_SB, s_sdB, s_V, s_Rh, s_Rl, s_O, s_acc, s_amv, s_ars, s_z, s_x, s_out) = (sem(n) for n in (
            "x_stats", "x_rstd", "h_ready", "h_rounded", "hT_psum", "hT_high", "hT_low", "h2_ready", "logits_psum",
            "logits_copied", "logits_ready", "logits_max", "logits_less_max", "exp_ready", "gram_psum", "var_ready",
            "std_ready", "rstd_ready", "var_guarded", "std_parts", "stdT_psum", "stdT_ready", "coef_ready", "hid_psum", "stdB_psum", "stdB_ready", "hid_ready", "relu_high", "relu_low",
            "out_psum", "acc_ready", "acc_stats", "acc_rstd", "z_ready", "x_updated", "stored"))
        (a_zero, a_mask, a_w, a_wh, a_wl, a_qk, a_qf, a_qh, a_kh, a_qp, a_kl, a_kt, a_kth, a_ktl, a_v, a_vf,
         a_vh, a_vl, a_xb, a_s, a_sm, a_sh, a_sl, a_sll, a_y, a_ysb, a_yt, a_ytc, a_wo, a_x, a_dz, a_dzm, a_z) = (
            sem("a_" + n) for n in (
            "queries_cleared", "masks", "weights_T_psum", "weights_high", "weights_low", "qk_psum", "qk_copied",
            "q_high", "k_high", "q_parts", "k_parts", "ktok_psum", "ktok_high", "ktok_low", "v_psum",
            "v_copied", "v_high", "v_low", "bias_added", "scores_psum", "scores_masked", "scores_high", "scores_low",
            "last_scores_low",
            "y_psum", "y_copied", "yT_psum", "yT_copied", "proj_psum", "x_updated", "kv_psum", "kv_masked",
            "kv_added"))
        a_qx = [sem(f"a_q_expanded{half}") for half in range(2)]
        dve_done = sem("dve_done")
        pool_done = sem("pool_done")

        block = ctx.enter_context(nc.Block())

        def wait(eng, s, value):
            if isinstance(value, int) and value <= 0:
                return
            eng.wait_ge(s, value)

        def tile0(n, n0, par):
            return (n - par - n0) * (TB // 2) + par * (NT // 2)

        def two_ahead(n, n0):
            return not isinstance(n, int) or n < n0 + NBLK - 2

        def att_ahead(n):
            return isinstance(n, int) and n == NBLK - 2

        class Steps:
            def __init__(self, eng, s, at=0):
                self.eng, self.s, self.at = eng, s, at

            def __call__(self, ins):
                ins.then_inc(self.s, 1)
                self.at = self.at + 1
                self.eng.wait_ge(self.s, self.at)

        def blocks(eng, n0, body):
            body(n0, 0, False)
            body(n0 + 1, 1, False)
            with eng.Fori(n0 // 2 + 1, (n0 + NBLK) // 2 - 1, 1) as pair:
                body(2 * pair, 0, False)
                body(2 * pair + 1, 1, False)
            body(n0 + NBLK - 2, 0, False)
            return body(n0 + NBLK - 1, 1, True)

        @block.sync
        def _(sp):
            for e in range(E):
                sp.dma_start(w1r[:, e], w1[e].rearrange("(c p) n -> p c n", p=P)).then_inc(l_w1, 16)
            for e in range(E):
                sp.dma_start(w2r[:, e], w2[e].rearrange("(c p) n -> p c n", p=P)).then_inc(l_w2, 16)
            for k, w in enumerate((Wq, Wk, Wv, Wo)):
                sp.dma_start(wqkv[:, k], w.rearrange("(c p) n -> p c n", p=P)).then_inc(l_att, 16)
            for b in range(NBLK):
                sp.dma_start(X[:, b * TB:(b + 1) * TB, :], x_t[:, b * TB:(b + 1) * TB, :]).then_inc(l_x, 16)

            def expand(n):
                wait(sp, a_qp, n + 1)
                for half in range(2):
                    cols = slice(half * BT // 2, (half + 1) * BT // 2)
                    wait(sp, a_s, NG * TB * (n - 1) + NG * 2 * (half + 1))
                    for j in range(HPC):
                        rows = slice(j * HD, (j + 1) * HD)
                        sp.dma_start(qx[rows, j, :, :, cols], qp[rows, :, :, cols]).then_inc(a_qx[half], 16)

            sp.wait_ge(a_zero, 1)
            expand(0)
            with sp.Fori(1, NBLK, 1) as n:
                expand(n)

            def store(n):
                for par in range(2):
                    sp.wait_ge(s_x, TB * (n + par + 1))
                    t0 = tile0(n + par, NBLK, par)
                    sp.dma_start(out_t[:, bass.ds(t0, TB), :], X[:, bass.ds(t0, TB), :]).then_inc(s_out, 16)

            with sp.Fori(NBLK // 2, NBLK, 1) as pair:
                store(2 * pair)
            sp.wait_ge(s_out, 16 * NBLK)

        @block.gpsimd
        def _(pool):
            step = Steps(pool, pool_done)
            step(pool.memset(identf[:, :], 0.0))
            step(pool.affine_select(out=identf[:, :], in_=identf[:, :], compare_op=ALU.not_equal, fill=1.0,
                                    base=0, pattern=[[-1, P]], channel_multiplier=1))
            step(pool.tensor_copy(ident16[:, :], identf[:, :]))
            step(pool.memset(nhalf[:, :, :], -0.5))
            step(pool.memset(phalf[:, :, :], 0.5))
            step(pool.memset(inv_std[:, :, :], 1.0 / STD_SHIFT))
            for k, v in enumerate((0.5, 1.0 / D, EPS, -1.0)):
                step(pool.memset(consts[:, k], v))
            step(pool.memset(ones, 1.0))
            step(pool.memset(before[:, :, :], 1.0))
            step(pool.affine_select(out=before[:, :, :], in_=before[:, :, :], compare_op=ALU.is_ge, fill=0.0,
                                    base=-1, pattern=[[1, E], [-1, E]], channel_multiplier=0))
            step(pool.tensor_scalar(after[:, :, :], before[:, :, :], -1.0, 1.0, ALU.mult, ALU.add))
            step(pool.memset(causal[:, :], 1.0))
            step(pool.affine_select(out=causal[:, :], in_=causal[:, :], compare_op=ALU.is_ge, fill=0.0,
                                    base=0, pattern=[[1, P]], channel_multiplier=-1))
            step(pool.memset(sameh[:, :], 1.0))
            sameh_v = sameh[:, :].rearrange("p (j d) -> p j d", d=HD)
            for base, jd, cm in ((0, -HD, 1), (HD - 1, HD, -1)):
                step(pool.affine_select(out=sameh_v, in_=sameh_v, compare_op=ALU.is_ge, fill=0.0,
                                        base=base, pattern=[[jd, HPC], [0, HD]], channel_multiplier=cm))
            for j, c in enumerate((128.0, 128.0, 32768.0, 1024.0, 1024.0, 32768.0)):
                step(pool.memset(capn[:, j:j + 1], c))
            pool.memset(mx[:, :], 0.0).then_inc(p_id, 1)
            pool.wait_ge(p_mx, 1)
            pool.partition_all_reduce(mxa[:, :], mx[:, :], P, RMAX).then_inc(p_mxa, 1)
            pool.wait_ge(p_q, 1)
            def bc(a):
                return a.unsqueeze(2).to_broadcast([P, TB, E])

            def norm_factors(stats, f, at, done):
                me, qe, mo, qo = (stats[:, :, k] for k in (1, 2, 4, 5))
                pool.tensor_tensor(f[:, 0], me, mo, ALU.add)
                pool.tensor_tensor(f[:, 1], me, mo, ALU.subtract)
                at(pool.tensor_tensor(f[:, 2], qe, qo, ALU.add))
                pool.tensor_tensor(f[:, 3], f[:, 0], half_, ALU.mult)
                pool.tensor_tensor(f[:, 4], f[:, 1], half_, ALU.mult)
                at(pool.tensor_tensor(f[:, 5], f[:, 2], inv_d, ALU.mult))
                at(pool.tensor_tensor(f[:, 6], f[:, 4], f[:, 4], ALU.mult))
                at(pool.tensor_tensor(f[:, 8], f[:, 5], f[:, 6], ALU.add))
                at(pool.tensor_tensor(f[:, 9], f[:, 8], eps_, ALU.add))
                at(pool.tensor_tensor(f[:, 10], f[:, 9], nhalf[:, :, 0], ALU.pow))
                at(pool.tensor_tensor(f[:, 7], f[:, 3], f[:, 10], ALU.mult))
                pool.tensor_tensor(f[:, 11], f[:, 7], mone, ALU.mult).then_inc(done, 1)

            def rs(g, at, router):
                wait(pool, s_mv, g + 1)
                wait(pool, s_h, g)
                norm_factors(xst, xf, at, s_rs)
                if not router:
                    return
                at(pool.tensor_tensor(r2a[:, :], xf[:, 8], xrs, ALU.mult))
                at(pool.tensor_tensor(r2b[:, :], r2a[:, :], xrs, ALU.mult))
                at(pool.tensor_tensor(r2c[:, :], r2b[:, :], eps_, ALU.add))
                at(pool.tensor_tensor(r2d[:, :], r2c[:, :], nhalf[:, :, 0], ALU.pow))
                at(pool.tensor_tensor(r2[:, :], r2d[:, :], qri.to_broadcast([P, TB]), ALU.mult))

            def logits(n, at):
                wait(pool, s_lg, n + 1)
                at(pool.tensor_tensor(lga[:, :, :], lsb[:, :, 0:E], lsb[:, :, E:2 * E], ALU.add))
                at(pool.tensor_tensor(lgb[:, :, :], lga[:, :, :], bc(r2[:, :]), ALU.mult))
                pool.tensor_tensor(lgc[:, :, :], lgb[:, :, :], routc[:, :].unsqueeze(1).to_broadcast([P, TB, E]),
                                   ALU.add).then_inc(s_lgl, 1)

            def less_max(n, at):
                wait(pool, s_lmax, n + 1)
                pool.tensor_tensor(lgd[:, :, :], lgc[:, :, :], bc(lmax[:, :]), ALU.subtract).then_inc(s_lgm, 1)

            def std(n, at):
                wait(pool, s_vare, n + 1)
                wait(pool, s_s12, n)
                wait(pool, s_coef, n)
                at(pool.tensor_tensor(sd[:, :, :], vare[:, :, :], phalf[:, :, :], ALU.pow))
                pool.tensor_tensor(sds[:, :, :], sd[:, :, :], inv_std[:, :, :], ALU.mult).then_inc(s_sd, 1)
                pool.tensor_tensor(rsd[:, :, :], vare[:, :, :], nhalf[:, :, :], ALU.pow).then_inc(s_rsd, 1)

            def post_stats(n, at):
                wait(pool, s_amv, TB * n + TB)
                wait(pool, s_z, TB * n)
                norm_factors(ast, af, at, s_ars)

            def post_tile(n, par, f, t, at):
                xt = X[:, tile0(n, f * NBLK, par) + t, :]
                wait(pool, s_z, TB * n + (t + 1))
                at(pool.tensor_tensor(z[:, t, :], z[:, t, :], ong[:, :], ALU.mult))
                at(pool.tensor_tensor(z[:, t, :], z[:, t, :], onb[:, :], ALU.add))
                pool.tensor_tensor(xt, xt, z[:, t, :], ALU.add).then_inc(s_x, 1)

            def post(n, par, f, at):
                for t in range(TB):
                    post_tile(n, par, f, t, at)

            def add_bias(n, par):
                t0 = tile0(n, 0, par)
                wait(pool, s_h, n + (NBLK + 1))
                xt = X[:, bass.ds(t0, TB), :]
                pool.tensor_tensor(xt, xt, boB[:, :].unsqueeze(1).to_broadcast([P, TB, D]),
                                   ALU.add).then_inc(a_xb, 1)

            def key_low(n, par):
                wait(pool, a_kh, n + 1)
                pool.tensor_tensor(kp[:, par, :, 1], kf, kp[:, par, :, 0], ALU.subtract).then_inc(a_kl, 1)

            def score_low(c, cp, g):
                wait(pool, a_sh, NG * c + (g + 1))
                wait(pool, a_y, c - 1)
                pool.tensor_tensor(shl[:, cp, 1, g], sm[:, g], shl[:, cp, 0, g], ALU.subtract).then_inc(a_sl, 1)

            def add_state(c, par):
                wait(pool, a_dzm, c + 1)
                wait(pool, a_y, c + 1)
                pool.tensor_tensor(zst[:, par], zst[:, par], dz, ALU.add).then_inc(a_z, 1)

            def ffn(f):
                n0 = f * NBLK
                g0 = 2 * f * NBLK
                at = Steps(pool, pool_done, step.at)
                if f == 0:
                    rs(g0, at, True)
                    logits(n0, at)
                    less_max(n0, at)
                    std(n0, at)
                    rs(g0 + 1, at, True)
                start = at.at
                n_post = 7 + 2 * TB
                n_rs = 12
                per = 3 + n_rs + n_post

                def body(n, par, last):
                    first = isinstance(n, int) and n == n0
                    at = Steps(pool, pool_done, start if first else (n - n0) * per + (start - n_post))
                    if last:
                        at.at = at.at - (n_rs - (7 if f == 0 else 0))
                    if not first:
                        post_stats(n - 1, at)
                        post(n - 1, 1 - par, f, at)
                    if not last:
                        logits(n + 1, at)
                        less_max(n + 1, at)
                    if two_ahead(n, n0):
                        rs(n + (2 + g0 - n0), at, True)
                    elif att_ahead(n):
                        rs(NBLK, at, False)
                    if not last:
                        std(n + 1, at)
                    if f == 0 and first:
                        pool.wait_ge(p_gl, E + 1)
                        pool.wait_ge(p_g, E)
                        pool.memset(qx.rearrange("p a b c d -> p (a b c d)").bitcast(F32), 0.0).then_inc(a_zero, 1)
                    return at

                at = blocks(pool, n0, body)
                if f == 0:
                    add_bias(0, 0)
                    key_low(0, 0)
                post_stats(n0 + NBLK - 1, at)
                if f == 1:
                    post(n0 + NBLK - 1, 1, f, at)
                step.at = at.at

            def attention():
                at = Steps(pool, pool_done, step.at)
                pool.memset(zst, 0.0).then_inc(a_mask, 1)
                pool.wait_ge(a_mask, 1)
                for g in range(NG - 1):
                    score_low(0, 0, g)
                post_tile(NBLK - 1, 1, 0, 0, at)
                start = at.at
                per = 7
                extra = 2 * (TB - 1)

                def body(n, par, last):
                    first = isinstance(n, int) and n == 0
                    at = Steps(pool, pool_done, start if first else n * per + (start + extra))
                    for t in range(TB):
                        c = n * TB + t
                        if t == 0 and not last:
                            rs(n + (NBLK + 1), at, False)
                        if t == 0 and last:
                            rs(2 * NBLK, at, True)
                        for g in range(NG - 1):
                            if not (last and t == TB - 1):
                                score_low(c + 1, (t + 1) % 2, g)
                            if t == 2 and g == 0 and not last:
                                key_low(n + 1, 1 - par)
                        if t == 1 and not last:
                            add_bias(n + 1, 1 - par)
                        if first and t < TB - 1:
                            post_tile(NBLK - 1, 1, 0, t + 1, at)
                        if last and t == 3:
                            std(NBLK, at)
                        add_state(c, par)
                        if last and t == 1:
                            logits(NBLK, at)
                        if last and t == 2:
                            less_max(NBLK, at)
                    if last:
                        rs(2 * NBLK + 1, at, True)
                    return at

                at = blocks(pool, 0, body)
                step.at = at.at

            ffn(0)
            attention()
            ffn(1)

        @block.vector
        def _(dve):
            step = Steps(dve, dve_done)
            dve.wait_ge(l_w1, 16 * E)
            w1v = w1r[:, :, :, :].rearrange("p e c n -> p (e c) n")
            step(dve.tensor_reduce(rsum[:, :], w1v, AX.X, ALU.add))
            step(dve.tensor_scalar(rmean[:, :], rsum[:, :], 1.0 / H, None, ALU.mult))
            for k in range(E * KC):
                last = dve.tensor_scalar(w1v[:, k, :], w1v[:, k, :], rmean[:, k:k + 1], None, ALU.subtract)
            last.then_inc(p_c, 1)
            dve.wait_ge(p_c, 1)
            dve.wait_ge(l_gam, 16)
            for c in range(KC):
                last = dve.tensor_tensor(w1g[:, :, c, :], w1r[:, :, c, :], gamB[:, :, :], ALU.mult)
            step(last)
            dve.wait_ge(l_rw, 48)
            dve.wait_ge(p_id, 1)
            for c in range(KC):
                last = dve.tensor_scalar(rnbB[:, c, :], ones[:, :], rnbc[:, c:c + 1], None, ALU.mult)
            dve.wait_ge(p_rt, 1)
            step(dve.tensor_copy(rwT[:, :, :], bank[6][:, 0:KC * E].rearrange("p (c e) -> p c e", c=KC)))
            for c in range(KC):
                last = dve.tensor_scalar(rwg[:, c, :], rwT[:, c, :], rngc[:, c:c + 1], None, ALU.mult)
            last.then_inc(p_rc, 1)
            dve.wait_ge(p_rc, 1)
            dve.wait_ge(l_bet, 16 * E)
            dve.wait_ge(l_w2, 16 * E)
            dve.wait_ge(l_att, 16 * 8)
            for j, a, axis in ((0, w1r[:, :, :, :].rearrange("p e c n -> p (e c n)"), AX.X),
                               (1, w1g[:, :, :, :].rearrange("p e c n -> p (e c n)"), AX.X),
                               (2, w2r[:, :, :, :].rearrange("p e c n -> p (e c n)"), AX.X),
                               (4, rwg[:, :, :].rearrange("p c e -> p (c e)"), AX.X),
                               (3, betas[:, :, :].rearrange("p e m -> p (e m)"), AX.X),
                               (5, wqkv[:, 0:3].rearrange("p k c n -> p (k c n)"), AX.X),
                               (6, bqk[:, :, :].rearrange("p k c -> p (k c)"), AX.X),
                               (7, bvB[:, :], AX.X)):
                last = dve.tensor_reduce(mx[:, j:j + 1], a, axis, ALU.max, apply_absolute_value=True)
            last.then_inc(p_mx, 1)
            dve.wait_ge(p_mxa, 1)
            step(dve.tensor_scalar(big[:, 0:1], mxa[:, 0:1], TINY, None, ALU.max))
            step(dve.scalar_tensor_tensor(out=big[:, 1:2], in0=mxa[:, 3:4], scalar=big[:, 0:1], in1=mxa[:, 1:2],
                                          op0=ALU.mult, op1=ALU.add))
            step(dve.tensor_copy(big[:, 2:3], mxa[:, 2:3]))
            step(dve.tensor_copy(big[:, 3:4], mxa[:, 4:5]))
            step(dve.tensor_scalar(big[:, 1:4], big[:, 1:4], TINY, None, ALU.max))
            step(dve.tensor_scalar(big[:, 4:5], mxa[:, 5:6], TINY_ATT, None, ALU.max))
            step(dve.tensor_tensor(mxa[:, 6:7], mxa[:, 6:7], mxa[:, 7:8], ALU.max))
            step(dve.scalar_tensor_tensor(out=big[:, 5:6], in0=big[:, 4:5], scalar=float(D), in1=mxa[:, 6:7],
                                          op0=ALU.mult, op1=ALU.add))
            step(dve.reciprocal(q[:, :], big[:, :]))
            step(dve.tensor_tensor(q[:, :], q[:, :], capn[:, :], ALU.mult))
            step(dve.tensor_scalar(q[:, :].bitcast(U32), q[:, :].bitcast(U32), EXPONENT, None, ALU.bitwise_and))
            step(dve.reciprocal(qi[:, :], q[:, :]))
            step(dve.tensor_scalar(epsq, qc, qc, EPS, ALU.mult, ALU.mult))
            step(dve.tensor_scalar(bscale, q1, qi[:, 0:1], STD_SHIFT, ALU.mult, ALU.mult))
            step(dve.tensor_scalar(sc[:, 3:4], qc, qi[:, 1:2], None, ALU.mult))
            step(dve.tensor_scalar(aev, sa, qi[:, 4:5], None, ALU.mult))
            step(dve.tensor_scalar(sc[:, 6:7], qi[:, 5:6], qi[:, 5:6], None, ALU.mult))
            step(dve.tensor_scalar(iys, sc[:, 6:7], qi[:, 5:6], 1.0 / S_SHIFT, ALU.mult, ALU.mult))
            step(dve.tensor_scalar(bqk[:, :, :], bqk[:, :, :], sa, None, ALU.mult))
            step(dve.tensor_scalar(bvB[:, :], bvB[:, :], sa, None, ALU.mult))
            dve.tensor_scalar(kappa, sc[:, 3:4], qi[:, 2:3], None, ALU.mult).then_inc(p_q, 1)
            dve.wait_ge(p_q, 1)
            step(dve.tensor_scalar(routw[:, :, 0:E], rwg[:, :, :], qr, None, ALU.mult))
            step(dve.scalar_tensor_tensor(out=routw[:, :, E:2 * E], in0=rwg[:, :, :], scalar=qr,
                                          in1=routw[:, :, 0:E], op0=ALU.mult, op1=ALU.subtract))
            step(dve.tensor_scalar(betas[:, :, :], betas[:, :, :], bscale, None, ALU.mult))
            step(dve.tensor_tensor(pick[:, 0:E], identf[0:NSTD, 0:E], identf[0:NSTD, E:2 * E], ALU.add))
            step(dve.tensor_copy(sel[:, :, :], pick[:, :].unsqueeze(2).to_broadcast([NSTD, E, P])))
            dve.wait_ge(p_rt, 2)
            step(dve.tensor_copy(routc[:, :], bank[7][:, 0:E]))
            dve.wait_ge(l_on, 32)
            step(dve.tensor_scalar(ong[:, :], ong[:, :], 0.5, None, ALU.mult))
            step(dve.tensor_scalar(onb[:, :], onb[:, :], 0.5, None, ALU.mult))
            for e in range(E):
                dve.wait_ge(p_hi, e + 1)
                dve.scalar_tensor_tensor(out=w1l[:, e].rearrange("p c n -> p (c n)"),
                                         in0=w1g[:, e].rearrange("p c n -> p (c n)"), scalar=q1,
                                         in1=w1h[:, e].rearrange("p c n -> p (c n)"),
                                         op0=ALU.mult, op1=ALU.subtract)
                dve.wait_ge(p_gh, e + 1)
                dve.scalar_tensor_tensor(out=graml[:, :, e, :],
                                         in0=bank[4 + e % 2][:, :].rearrange("p (c n) -> p c n", c=KC),
                                         scalar=1.0 / H, in1=gramh[:, :, e, :],
                                         op0=ALU.mult, op1=ALU.subtract).then_inc(p_gl, 1)
            for e in range(E):
                dve.wait_ge(p_hi, E + e + 1)
                last = dve.scalar_tensor_tensor(out=w2l[:, e].rearrange("p c n -> p (c n)"),
                                                in0=w2r[:, e].rearrange("p c n -> p (c n)"), scalar=q2,
                                                in1=w2h[:, e].rearrange("p c n -> p (c n)"),
                                                op0=ALU.mult, op1=ALU.subtract)
            last.then_inc(p_gl, 1)
            for k in range(3):
                dve.wait_ge(a_wh, k + 1)
                dve.scalar_tensor_tensor(out=wTl[:, k].rearrange("p c n -> p (c n)"), in0=bank[k][:, :], scalar=qa,
                                         in1=wTh[:, k].rearrange("p c n -> p (c n)"),
                                         op0=ALU.mult, op1=ALU.subtract).then_inc(a_wl, 1)
            dve.wait_ge(l_x, 16 * NBLK)

            def x_stats(g, t0):
                wait(dve, s_rs, g)
                for t in range(TB):
                    last = dve.bn_stats(xst[:, t, :], X[:, t0 + t, :])
                last.then_inc(s_mv, 1)

            def hT_low(g, par):
                for c in range(KC):
                    wait(dve, s_hTh, KC * g + (c + 1))
                    dve.tensor_tensor(hTl[:, par, c, :], bank[6 + c][:, :], hTh[:, par, c, :],
                                      ALU.subtract).then_inc(s_hTl, 1)

            def h_twice(n):
                wait(dve, s_hr, n + 1)
                wait(dve, s_var, NU * n)
                dve.scalar_tensor_tensor(out=h2.rearrange("p t d -> p (t d)"),
                                         in0=h[:, :, :].rearrange("p t d -> p (t d)"), scalar=2.0,
                                         in1=hr.rearrange("p t d -> p (t d)"),
                                         op0=ALU.mult, op1=ALU.subtract).then_inc(s_h2, 1)

            def logits_copy(n):
                wait(dve, s_L, n + 1)
                wait(dve, s_lgl, n)
                dve.tensor_copy(lsb[:, :, :].rearrange("p t e -> p (t e)"),
                                bank[6][:, 0:TB * 2 * E]).then_inc(s_lg, 1)

            def logits_max(n):
                wait(dve, s_lgl, n + 1)
                wait(dve, s_lgm, n)
                dve.tensor_reduce(lmax[:, :], lgc[:, :, :], AX.X, ALU.max).then_inc(s_lmax, 1)

            def variance(n, j):
                t, e0 = j // 2, 2 * (j % 2)
                if j == 0:
                    wait(dve, s_h2, n + 1)
                    wait(dve, s_sd, n)
                wait(dve, s_U, NU * n + (j + 1))
                for e in range(e0, e0 + 2):
                    last = dve.tensor_tensor_reduce(out=junk[:, t * E + e, :],
                                                    in0=bank[7 - j % 2][:, (e - e0) * D:(e - e0 + 1) * D],
                                                    in1=h2[:, t, :], scale=1.0, scalar=0.0, op0=ALU.mult,
                                                    op1=ALU.add, accum_out=var[:, t, e:e + 1])
                last.then_inc(s_var, 1)

            def std_parts(n, at):
                wait(dve, s_sd, n + 1)
                wait(dve, s_ST, n)
                at(dve.tensor_copy(s12[:, :, 0:E], sds[:, :, :]))
                dve.tensor_tensor(s12[:, :, E:2 * E], sds[:, :, :], s12[:, :, 0:E], ALU.subtract).then_inc(s_s12, 1)

            def hidden(n, e, m):
                a = e * HC + m
                if m == 0:
                    wait(dve, s_sdB, E * n + (e + 1))
                wait(dve, s_A, NA * n + (a + 1))
                wait(dve, s_Rl, NA * n + (a - NV + 1))
                dve.scalar_tensor_tensor(out=V[:, a % NV], in0=sdB[:, e], scalar=betas[:, e, m:m + 1],
                                         in1=bank[m][:, :], op0=ALU.mult, op1=ALU.add).then_inc(s_V, 1)

            def relu_low(n, e, m):
                a = e * HC + m
                wait(dve, s_Rh, NA * n + (a + 1))
                if m == 0:
                    wait(dve, s_O, NO * n + (e * TB - TB))
                dve.scalar_tensor_tensor(out=Rl[:, e % 2, m, :], in0=V[:, a % NV], scalar=0.0,
                                         in1=Rh[:, e % 2, m, :], op0=ALU.max, op1=ALU.subtract).then_inc(s_Rl, 1)

            def accumulate(n, par, e, t):
                o = e * TB + t
                if o == 0:
                    wait(dve, s_coef, n + 1)
                wait(dve, s_O, NO * n + (o + 1))
                src = bank[4 + t % 2][:, 0:D]
                if e == 0:
                    wait(dve, s_z, TB * (n - 1) + (t + 1))
                    ins = dve.tensor_scalar(acc[:, t, :], src, coef[:, par, t, e:e + 1], None, ALU.mult)
                else:
                    wait(dve, s_acc, NO * n + (o - TB + 1))
                    ins = dve.scalar_tensor_tensor(out=acc[:, t, :], in0=src, scalar=coef[:, par, t, e:e + 1],
                                                   in1=acc[:, t, :], op0=ALU.mult, op1=ALU.add)
                ins.then_inc(s_acc, 1)

            def acc_stats(n, t):
                wait(dve, s_acc, NO * n + (NO - TB + t + 1))
                if t == 0:
                    wait(dve, s_ars, n)
                dve.bn_stats(ast[:, t, :], acc[:, t, :]).then_inc(s_amv, 1)

            def guard(n):
                wait(dve, s_var, NU * n + NU)
                wait(dve, s_rsd, n)
                dve.tensor_scalar(vare[:, :, :], var[:, :, :], 0.0, epsq, ALU.max, ALU.add).then_inc(s_vare, 1)

            def choose(n, at):
                wait(dve, s_E, n + 1)
                other = ex[:, :, :].unsqueeze(2).to_broadcast([P, TB, E, E])
                own = ex[:, :, :].unsqueeze(3).to_broadcast([P, TB, E, E])
                dve.tensor_tensor(gt[:, :, :, :], other, own, ALU.is_gt)
                at(dve.tensor_tensor(ge[:, :, :, :], other, own, ALU.is_ge))
                for m, mask in ((gt, after), (ge, before)):
                    last = dve.tensor_tensor(m[:, :, :, :], m[:, :, :, :],
                                             mask[:, :, :].unsqueeze(1).to_broadcast([P, TB, E, E]), ALU.mult)
                at(last)
                at(dve.tensor_tensor(gt[:, :, :, :], gt[:, :, :, :], ge[:, :, :, :], ALU.add))
                at(dve.tensor_reduce(rank[:, :, :], gt[:, :, :, :], AX.X, ALU.add))
                at(dve.scalar_tensor_tensor(out=es[:, :, :], in0=rank[:, :, :], scalar=1.5, in1=ex[:, :, :],
                                            op0=ALU.is_lt, op1=ALU.mult))

            def weigh(at):
                dve.tensor_reduce(tot[:, 0], es[:, :, :], AX.X, ALU.add)
                at(dve.tensor_reduce(tot[:, 1], ex[:, :, :], AX.X, ALU.add))
                at(dve.scalar_tensor_tensor(out=den[:, :], in0=tot[:, 1], scalar=EPS_GATE, in1=tot[:, 0],
                                            op0=ALU.mult, op1=ALU.add))
                at(dve.reciprocal(rden[:, :], den[:, :]))
                at(dve.tensor_tensor(ws[:, :, :], es[:, :, :], rden[:, :].unsqueeze(2).to_broadcast([P, TB, E]),
                                     ALU.mult))

            def coefs(n, par):
                wait(dve, s_rsd, n + 1)
                wait(dve, s_acc, NO * (n - 1))
                dve.scalar_tensor_tensor(out=coef[:, par], in0=ws[:, :, :], scalar=kappa, in1=rsd[:, :, :],
                                         op0=ALU.mult, op1=ALU.mult).then_inc(s_coef, 1)

            def query_low(n, par):
                wait(dve, a_qh, n + 1)
                for half in range(2):
                    wait(dve, a_qx[half], NX * n)
                dve.tensor_tensor(qp[:, :, 1], qf[:, par], qp[:, :, 0], ALU.subtract).then_inc(a_qp, 1)

            def ktok_low(n, par):
                for j in range(2):
                    wait(dve, a_kth, 2 * n + (j + 1))
                    rows = slice(2 * j, 2 * j + 2)
                    dve.tensor_tensor(ktok[:, par, 1, rows].rearrange("p t d -> p (t d)"), bank[6 + j][:, :],
                                      ktok[:, par, 0, rows].rearrange("p t d -> p (t d)"),
                                      ALU.subtract).then_inc(a_ktl, 1)

            def values(n):
                wait(dve, a_kt, 2 * n + 2)
                wait(dve, a_kl, n + 1)
                for j in range(2):
                    wait(dve, a_v, 2 * n + (j + 1))
                    dve.scalar_tensor_tensor(out=vf[:, 2 * j:2 * j + 2],
                                             in0=bank[6 + j][:, :].rearrange("p (t d) -> p t d", t=2), scalar=aev,
                                             in1=bvB[:, :].unsqueeze(1).to_broadcast([P, 2, D]),
                                             op0=ALU.mult, op1=ALU.add).then_inc(a_vf, 1)

            def value_low(n, par):
                wait(dve, a_vh, n + 1)
                dve.tensor_tensor(vtok[:, par, 1], vf, vtok[:, par, 0], ALU.subtract).then_inc(a_vl, 1)

            def mask_scores(c, g):
                wait(dve, a_s, NG * c + (g + 1))
                if g < NG - 1:
                    wait(dve, a_sl, (NG - 1) * (c - 1) + (g + 1))
                else:
                    wait(dve, a_sll, c)
                dve.scalar_tensor_tensor(out=sm[:, g], in0=bank[g][:, :].rearrange("p (j t) -> p j t", j=4),
                                         scalar=S_SHIFT, in1=causal[:, :].unsqueeze(1).to_broadcast([P, 4, P]),
                                         op0=ALU.mult, op1=ALU.mult).then_inc(a_sm, 1)

            def last_score_low(c, cp):
                wait(dve, a_sh, NG * c + NG)
                wait(dve, a_y, c - 1)
                dve.tensor_tensor(shl[:, cp, 1, NG - 1], sm[:, NG - 1], shl[:, cp, 0, NG - 1],
                                  ALU.subtract).then_inc(a_sll, 1)

            def update_x(c, tile):
                wait(dve, a_wo, c + 1)
                dve.tensor_tensor(X[:, tile, :], bank[5][:, 0:D], X[:, tile, :], ALU.add).then_inc(a_x, 1)

            def mask_kv(c):
                wait(dve, a_dz, c + 1)
                wait(dve, a_z, c)
                dve.scalar_tensor_tensor(out=dz, in0=bank[5][:, 0:D].rearrange("p (c v) -> p c v", c=KC),
                                         scalar=S_SHIFT, in1=sameh[:, :].unsqueeze(1).to_broadcast([P, KC, P]),
                                         op0=ALU.mult, op1=ALU.mult).then_inc(a_dzm, 1)

            def ffn(f):
                n0 = f * NBLK
                g0 = 2 * f * NBLK
                at = Steps(dve, dve_done, step.at)
                if f == 0:
                    x_stats(g0, 0)
                    hT_low(g0, 0)
                    h_twice(n0)
                    logits_copy(n0)
                    for j in range(NU // 2):
                        variance(n0, j)
                    logits_max(n0)
                    x_stats(g0 + 1, tile0(n0 + 1, n0, 1))
                    for j in range(NU // 2, NU):
                        variance(n0, j)
                    guard(n0)
                    std_parts(n0, at)
                    choose(n0, at)
                    weigh(at)
                    coefs(n0, 0)
                start = at.at
                per = 10

                def body(n, par, last):
                    first = isinstance(n, int) and n == n0
                    at = Steps(dve, dve_done, start if first else (n - n0) * per + start)
                    for a in range(2 * HC):
                        hidden(n, a // HC, a % HC)
                        if a >= 1:
                            relu_low(n, (a - 1) // HC, (a - 1) % HC)
                    relu_low(n, 1, HC - 1)
                    if not last or f == 0:
                        hT_low(n + (1 + g0 - n0), 1 - par)
                    for t in range(TB):
                        accumulate(n, par, 0, t)
                        if t == 1 and not last:
                            h_twice(n + 1)
                    if not last:
                        logits_copy(n + 1)
                    for m in range(HC):
                        hidden(n, 2, m)
                        if not last:
                            if m >= 1:
                                variance(n + 1, m - 1)
                            relu_low(n, 2, m)
                        elif m >= 1:
                            relu_low(n, 2, m - 1)
                    if last:
                        relu_low(n, 2, HC - 1)
                    if not last:
                        variance(n + 1, HC - 1)
                    if not last:
                        logits_max(n + 1)
                    for t in range(TB):
                        accumulate(n, par, 1, t)
                        if t == 1 and not last:
                            choose(n + 1, at)
                        if t == 2 and not last:
                            weigh(at)
                    if two_ahead(n, n0):
                        x_stats(n + (2 + g0 - n0), tile0(n + 2, n0, par))
                    elif att_ahead(n):
                        wait(dve, s_x, TB)
                        x_stats(NBLK, 0)
                    for m in range(HC):
                        hidden(n, 3, m)
                        if not last:
                            if m >= 1:
                                variance(n + 1, HC + m - 1)
                            relu_low(n, 3, m)
                        elif m >= 1:
                            relu_low(n, 3, m - 1)
                    if last:
                        relu_low(n, 3, HC - 1)
                    if not last:
                        variance(n + 1, 2 * HC - 1)
                    if not last:
                        guard(n + 1)
                    for t in range(TB):
                        accumulate(n, par, 2, t)
                        if t == TB - 1 and not last:
                            std_parts(n + 1, at)
                        if t == 1 and last and f == 0:
                            query_low(0, 0)
                    if last and f == 0:
                        ktok_low(0, 0)
                    for t in range(TB):
                        accumulate(n, par, 3, t)
                        acc_stats(n, t)
                        if t == 1 and not last:
                            coefs(n + 1, 1 - par)
                    return at

                at = blocks(dve, n0, body)
                step.at = at.at

            def attention():
                values(0)
                value_low(0, 0)
                for g in range(NG):
                    mask_scores(0, g)
                last_score_low(0, 0)

                def body(n, par, last):
                    for t in range(TB):
                        c = n * TB + t
                        more = not (last and t == TB - 1)
                        if t == 0 and not last:
                            wait(dve, s_x, TB * (n + 2))
                            x_stats(n + (NBLK + 1), tile0(n + 1, 0, 1 - par))
                        if t == 0 and last:
                            wait(dve, a_x, TB)
                            x_stats(2 * NBLK, 0)
                        if more:
                            mask_scores(c + 1, 0)
                            mask_scores(c + 1, 1)
                        if t > 0:
                            if t == 1:
                                wait(dve, a_xb, n + 1)
                            update_x(c - 1, tile0(n, 0, par) + (t - 1))
                        elif not (isinstance(n, int) and n == 0):
                            update_x(c - 1, tile0(n - 1, 0, 1 - par) + (TB - 1))
                        if more:
                            mask_scores(c + 1, 2)
                            mask_scores(c + 1, 3)
                        if not last:
                            if t == 1:
                                hT_low(n + (NBLK + 1), 1 - par)
                            if t == 2:
                                ktok_low(n + 1, 1 - par)
                            if t == 3:
                                value_low(n + 1, 1 - par)
                        if more:
                            last_score_low(c + 1, (t + 1) % 2)
                        if t == 1 and last:
                            hT_low(2 * NBLK, 0)
                        if t == 2 and last:
                            for j in range(4):
                                variance(NBLK, j)
                        if t == 3 and last:
                            for j in range(5, NU):
                                variance(NBLK, j)
                            guard(NBLK)
                        mask_kv(c)
                        if t == 1 and not last:
                            query_low(n + 1, 1 - par)
                        if t == 2 and not last:
                            values(n + 1)
                        if t == 1 and last:
                            h_twice(NBLK)
                            logits_copy(NBLK)
                        if t == 2 and last:
                            variance(NBLK, 4)
                            logits_max(NBLK)

                blocks(dve, 0, body)
                update_x(TB * NBLK - 1, NT - 1)
                at = Steps(dve, dve_done, step.at)
                std_parts(NBLK, at)
                choose(NBLK, at)
                weigh(at)
                coefs(NBLK, 0)
                x_stats(2 * NBLK + 1, tile0(1, 0, 1))
                step.at = at.at

            ffn(0)
            attention()
            dve.wait_ge(a_x, TB * NBLK)
            ffn(1)

        @block.scalar
        def _(act):
            act.dma_start(gamB[:, :, :].rearrange("p e n -> p (e n)"),
                          ln_g.rearrange("(a e) n -> a (e n)", a=1).to_broadcast([P, E * H])).then_inc(l_gam, 16)
            act.dma_start(rw[:, :], router_w).then_inc(l_rw, 16)
            act.dma_start(rngc[:, :], rn_g.rearrange("(c p) -> p c", p=P), allow_slow_non_contiguous=True).then_inc(l_rw, 16)
            act.dma_start(rnbc[:, :], rn_b.rearrange("(c p) -> p c", p=P), allow_slow_non_contiguous=True).then_inc(l_rw, 16)
            for k, v in enumerate((bq, bk)):
                act.dma_start(bqk[:, k, :], v.rearrange("(c p) -> p c", p=P),
                              allow_slow_non_contiguous=True).then_inc(l_att, 16)
            for d, v in ((bvB, bv), (boB, bo)):
                act.dma_start(d[:, :], v.rearrange("(a n) -> a n", a=1).to_broadcast([P, D])).then_inc(l_att, 16)
            for e in range(E):
                act.dma_start(betas[:, e, :], ln_b[e].rearrange("(m p) -> p m", p=P),
                              allow_slow_non_contiguous=True).then_inc(l_bet, 16)
            act.dma_start(ong[:, :], on_g.rearrange("(a n) -> a n", a=1).to_broadcast([P, D])).then_inc(l_on, 16)
            act.dma_start(onb[:, :], on_b.rearrange("(a n) -> a n", a=1).to_broadcast([P, D])).then_inc(l_on, 16)
            act.wait_ge(p_q, 1)
            for e in range(E):
                for b in range(2):
                    act.wait_ge(p_wt, 2 * e + b + 1)
                    if e >= 2 and b == 0:
                        act.wait_ge(p_g, e - 1)
                    act.activation(w1T[:, e % 2, 2 * b:2 * b + 2, :].rearrange("p c n -> p (c n)"),
                                   bank[2 * (e % 2) + b][:, :], ACT.Copy, scale=qc).then_inc(p_wtc, 1)
                act.activation(w1h[:, e].rearrange("p c n -> p (c n)"), w1g[:, e].rearrange("p c n -> p (c n)"),
                               ACT.Copy, scale=q1).then_inc(p_hi, 1)
                act.wait_ge(p_g, e + 1)
                act.activation(gramh[:, :, e, :], bank[4 + e % 2][:, :].rearrange("p (c n) -> p c n", c=KC),
                               ACT.Copy, scale=1.0 / H).then_inc(p_gh, 1)
            for e in range(E):
                act.activation(w2h[:, e].rearrange("p c n -> p (c n)"), w2r[:, e].rearrange("p c n -> p (c n)"),
                               ACT.Copy, scale=q2).then_inc(p_hi, 1)
            for k in range(3):
                act.wait_ge(a_w, k + 1)
                act.activation(wTh[:, k].rearrange("p c n -> p (c n)"), bank[k][:, :], ACT.Copy,
                               scale=qa).then_inc(a_wh, 1)
            act.wait_ge(a_w, 4)
            act.activation(woT[:, :, :].rearrange("p c n -> p (c n)"), bank[3][:, :], ACT.Copy).then_inc(a_wh, 1)

            def h_rows(g, t0, used):
                wait(act, s_rs, g + 1)
                wait(act, s_T, KC * g)
                wait(act, s_h2, used)
                for t in range(TB):
                    last = act.activation(h[:, t, :], X[:, t0 + t, :], ACT.Identity,
                                          bias=xnr[:, t:t + 1], scale=xrs[:, t:t + 1])
                last.then_inc(s_h, 1)

            def h_round(g):
                act.wait_ge(s_h, g + 1)
                act.activation(hr.rearrange("p t d -> p (t d)"), h[:, :, :].rearrange("p t d -> p (t d)"),
                               ACT.Copy).then_inc(s_hr, 1)

            def hT_high(g, par):
                for c in range(KC):
                    wait(act, s_T, KC * g + (c + 1))
                    act.activation(hTh[:, par, c, :], bank[6 + c][:, :], ACT.Copy).then_inc(s_hTh, 1)

            def exps(n):
                wait(act, s_lgm, n + 1)
                wait(act, s_coef, n)
                act.activation(ex[:, :, :], lgd[:, :, :], ACT.Exp).then_inc(s_E, 1)

            def std_T(n):
                wait(act, s_ST, n + 1)
                act.activation(sdT, bank[7][0:NSTD, 0:BT // 2].bitcast(F16), ACT.Copy).then_inc(s_sdT, 1)
                for e in range(E):
                    wait(act, s_SB, E * n + (e + 1))
                    act.activation(sdB[:, e], bank[6 + e % 2][:, :], ACT.Copy).then_inc(s_sdB, 1)

            def relu_high(n, e, m):
                a = e * HC + m
                wait(act, s_V, NA * n + (a + 1))
                if m == 0:
                    wait(act, s_O, NO * n + (e * TB - TB))
                act.activation(Rh[:, e % 2, m, :], V[:, a % NV], ACT.Relu).then_inc(s_Rh, 1)

            def z_row(n, t):
                wait(act, s_ars, n + 1)
                wait(act, s_x, TB * (n - 1) + (t + 1))
                act.activation(z[:, t, :], acc[:, t, :], ACT.Identity,
                               bias=anr[:, t:t + 1], scale=ars[:, t:t + 1]).then_inc(s_z, 1)

            def z_rows(n):
                for t in range(TB):
                    z_row(n, t)

            def qk_copy(n, par, k, dst):
                if k == 1:
                    wait(act, a_vl, n)
                for c in range(KC):
                    wait(act, a_qk, 4 * n + (2 * k + c + 1))
                    act.activation(dst[:, c], bank[6 + c][:, :], ACT.Identity, bias=bqk[:, k, c:c + 1],
                                   scale=aev).then_inc(a_qf, 1)

            def query_high(n, par):
                for half in range(2):
                    wait(act, a_qx[half], NX * n)
                wait(act, a_qf, 4 * n + 2)
                act.activation(qp[:, :, 0], qf[:, par], ACT.Copy).then_inc(a_qh, 1)

            def key_high(n, par):
                wait(act, a_qf, 4 * n + 4)
                act.activation(kp[:, par, :, 0], kf, ACT.Copy).then_inc(a_kh, 1)

            def ktok_high(n, par):
                for j in range(2):
                    wait(act, a_kt, 2 * n + (j + 1))
                    act.activation(ktok[:, par, 0, 2 * j:2 * j + 2].rearrange("p t d -> p (t d)"),
                                   bank[6 + j][:, :], ACT.Copy).then_inc(a_kth, 1)

            def value_high(n, par):
                wait(act, a_vf, 2 * n + 2)
                act.activation(vtok[:, par, 0], vf, ACT.Copy).then_inc(a_vh, 1)

            def score_high(c, cp, g):
                wait(act, a_sm, NG * c + (g + 1))
                wait(act, a_y, c - 1)
                act.activation(shl[:, cp, 0, g], sm[:, g], ACT.Copy).then_inc(a_sh, 1)

            def y_copy(c):
                wait(act, a_y, c + 1)
                wait(act, a_yt, c)
                act.activation(ysb, bank[4][:, 0:D], ACT.Copy, scale=iys).then_inc(a_ysb, 1)

            def yT_copy(c):
                wait(act, a_yt, c + 1)
                wait(act, a_wo, c)
                act.activation(yT, bank[4][:, 0:D].rearrange("p (c t) -> p c t", c=KC),
                               ACT.Copy).then_inc(a_ytc, 1)

            def ffn(f):
                n0 = f * NBLK
                dg = n0 + 1
                if f == 0:
                    h_rows(0, 0, 0)
                    h_round(0)
                    hT_high(0, 0)
                    exps(0)
                    std_T(0)
                    h_rows(1, tile0(1, 0, 1), 1)
                    h_round(1)

                def body(n, par, last):
                    for m in range(HC):
                        relu_high(n, 0, m)
                    for m in range(HC):
                        relu_high(n, 1, m)
                        if not (isinstance(n, int) and n == n0) and m < TB - 1:
                            z_row(n - 1, m)
                    if not last or f == 0:
                        wait(act, s_A, NA * n)
                        hT_high(n + dg, 1 - par)
                    if not (isinstance(n, int) and n == n0):
                        z_row(n - 1, TB - 1)
                    for m in range(HC):
                        relu_high(n, 2, m)
                    if not last:
                        exps(n + 1)
                    for m in range(HC):
                        relu_high(n, 3, m)
                    if two_ahead(n, n0):
                        h_rows(n + (dg + 1), tile0(n + 2, n0, par), n + 2)
                        h_round(n + (dg + 1))
                    elif att_ahead(n):
                        h_rows(NBLK, 0, NBLK)
                    if not last:
                        std_T(n + 1)

                blocks(act, n0, body)
                if f == 1:
                    z_rows(n0 + NBLK - 1)

            def attention():
                qk_copy(0, 0, 0, qf[:, 0])
                query_high(0, 0)
                act.wait_ge(s_Rl, NA * NBLK)
                qk_copy(0, 0, 1, kf)
                key_high(0, 0)
                ktok_high(0, 0)
                value_high(0, 0)
                for g in range(NG):
                    score_high(0, 0, g)
                z_rows(NBLK - 1)

                def body(n, par, last):
                    for t in range(TB):
                        c = n * TB + t
                        if t > 0 or not (isinstance(n, int) and n == 0):
                            yT_copy(c - 1)
                        if t == 1 and not last:
                            h_rows(n + (NBLK + 1), tile0(n + 1, 0, 1 - par), NBLK)
                        if t == 2 and not last:
                            key_high(n + 1, 1 - par)
                        if t == 3 and not last:
                            if isinstance(n, int) and n == 0:
                                act.wait_ge(s_x, TB * NBLK)
                            value_high(n + 1, 1 - par)
                        if t == 1 and last:
                            h_rows(2 * NBLK, 0, NBLK)
                            h_round(2 * NBLK)
                        if not (last and t == TB - 1):
                            for g in range(NG):
                                score_high(c + 1, (t + 1) % 2, g)
                        if t == 1:
                            hT_high(n + (NBLK + 1), 1 - par)
                        if t == 2 and not last:
                            ktok_high(n + 1, 1 - par)
                        y_copy(c)
                        if t == 2 and last:
                            exps(NBLK)
                        if t == 1 and not last:
                            qk_copy(n + 1, 1 - par, 0, qf[:, 1 - par])
                            query_high(n + 1, 1 - par)
                            qk_copy(n + 1, 1 - par, 1, kf)

                blocks(act, 0, body)
                yT_copy(TB * NBLK - 1)
                std_T(NBLK)
                h_rows(2 * NBLK + 1, tile0(1, 0, 1), NBLK + 1)
                h_round(2 * NBLK + 1)

            ffn(0)
            attention()
            ffn(1)

        @block.tensor
        def _(pe):
            pe.wait_ge(p_id, 1)
            pe.wait_ge(l_rw, 48)
            for c in range(KC):
                last = pe.transpose(bank[6][:, c * E:(c + 1) * E], rw[:, c * P:(c + 1) * P], identf[0:E, 0:E])
            last.then_inc(p_rt, 1)
            pe.wait_ge(p_rc, 1)
            for c in range(KC):
                last = pe.matmul(bank[7][:, 0:E], rnbB[:, c, :], rwT[:, c, :], start=(c == 0), stop=(c == KC - 1))
            last.then_inc(p_rt, 1)
            pe.wait_ge(p_c, 1)
            for e in range(E + 1):
                if e < E:
                    for b in range(2):
                        if e >= 2:
                            pe.wait_ge(p_wtc, 2 * (e - 2) + b + 1)
                        for j in range(2):
                            for c in range(KC):
                                last = pe.transpose(bank[2 * (e % 2) + b][:, j * D + c * P:j * D + (c + 1) * P],
                                                    w1r[:, e, c, (2 * b + j) * P:(2 * b + j + 1) * P], identf[:, :])
                        last.then_inc(p_wt, 1)
                if e >= 1:
                    g = e - 1
                    pe.wait_ge(p_wtc, 2 * g + 2)
                    if g >= 2:
                        pe.wait_ge(p_gl, g - 1)
                    for c in range(KC):
                        for k in range(HC):
                            last = pe.matmul(bank[4 + g % 2][:, c * D:(c + 1) * D], w1T[:, g % 2, k, c * P:(c + 1) * P],
                                             w1T[:, g % 2, k, :], start=(k == 0), stop=(k == HC - 1))
                    last.then_inc(p_g, 1)
            pe.wait_ge(p_gl, E + 1)
            pe.wait_ge(l_att, 16 * 8)
            for k in range(4):
                for c in range(KC):
                    for o in range(KC):
                        last = pe.transpose(bank[k][:, c * D + o * P:c * D + (o + 1) * P],
                                            wqkv[:, k, o, c * P:(c + 1) * P], identf[:, :])
                last.then_inc(a_w, 1)
            pe.wait_ge(a_wl, 3)
            pe.wait_ge(a_wh, 4)

            def h_T(g):
                wait(pe, s_h, g + 1)
                for c in range(KC):
                    for t in range(TB):
                        last = pe.transpose(bank[6 + c][:, t * P:(t + 1) * P], h[:, t, c * P:(c + 1) * P], identf[:, :])
                    last.then_inc(s_T, 1)

            def router(n, g, par):
                wait(pe, s_hTl, KC * g + KC)
                for t in range(TB):
                    rows = slice(t * P, (t + 1) * P)
                    o = bank[6][:, t * 2 * E:(t + 1) * 2 * E]
                    pe.matmul(o, hTh[:, par, 0, rows], routw[:, 0, :], start=True, stop=False)
                    pe.matmul(o, hTh[:, par, 1, rows], routw[:, 1, :], start=False, stop=False)
                    pe.matmul(o[:, 0:E], hTl[:, par, 0, rows], routw[:, 0, 0:E], start=False, stop=False)
                    last = pe.matmul(o[:, 0:E], hTl[:, par, 1, rows], routw[:, 1, 0:E], start=False, stop=True)
                last.then_inc(s_L, 1)

            def gram(n, par, j):
                t, e0 = j // 2, 2 * (j % 2)
                if j == 1:
                    wait(pe, s_lg, n + 1)
                if j >= 2:
                    wait(pe, s_var, NU * n + (j - 1))
                for c in range(KC):
                    for part, g in enumerate((gramh, graml)):
                        last = pe.matmul(bank[7 - j % 2][:, :], hTh[:, par, c, t * P:(t + 1) * P],
                                         g[:, c, e0:e0 + 2, :].rearrange("p e n -> p (e n)"),
                                         start=(c == 0 and part == 0), stop=(c == KC - 1 and part == 1))
                last.then_inc(s_U, 1)

            def std_rows(n):
                wait(pe, s_s12, n + 1)
                o = bank[7][0:NSTD, 0:BT // 2].bitcast(F16)
                for t in range(TB):
                    last = pe.transpose(o[:, t * P:(t + 1) * P], s12[:, t, :], ident16[:, :])
                last.then_inc(s_ST, 1)

            def std_spread(n, e):
                if e == 0:
                    wait(pe, s_sdT, n + 1)
                if e >= 2:
                    wait(pe, s_sdB, E * n + (e - 1))
                pe.matmul(bank[6 + e % 2][:, :], sel[:, e, :], sdT, start=True, stop=True).then_inc(s_SB, 1)

            def layer1(n, par, e, m):
                a = e * HC + m
                wait(pe, s_V, NA * n + (a - HC + 1))
                cols = slice(m * P, (m + 1) * P)
                o = bank[m][:, :]
                for c in range(KC):
                    pe.matmul(o, w1h[:, e, c, cols], hTh[:, par, c, :], start=(c == 0), stop=False)
                    pe.matmul(o, w1h[:, e, c, cols], hTl[:, par, c, :], start=False, stop=False)
                    last = pe.matmul(o, w1l[:, e, c, cols], hTh[:, par, c, :], start=False, stop=(c == KC - 1))
                last.then_inc(s_A, 1)

            def layer2(n, e, t):
                o = e * TB + t
                if t == 0:
                    wait(pe, s_Rl, NA * n + (e + 1) * HC)
                wait(pe, s_acc, NO * n + (o - 1))
                rows = slice(t * P, (t + 1) * P)
                dst = bank[4 + t % 2][:, 0:D]
                for k in range(HC):
                    pe.matmul(dst, Rh[:, e % 2, k, rows], w2h[:, e, k, :], start=(k == 0), stop=False)
                    pe.matmul(dst, Rh[:, e % 2, k, rows], w2l[:, e, k, :], start=False, stop=False)
                    last = pe.matmul(dst, Rl[:, e % 2, k, rows], w2h[:, e, k, :], start=False, stop=(k == HC - 1))
                last.then_inc(s_O, 1)

            def split_product(o, lhs, rhs, start, stop, **kw):
                (lh, ll), (rh, rl) = lhs, rhs
                pe.matmul(o, lh, rh, start=start, stop=False, **kw)
                pe.matmul(o, lh, rl, start=False, stop=False, **kw)
                return pe.matmul(o, ll, rh, start=False, stop=stop, **kw)

            def rows_T(n):
                wait(pe, a_vf, 2 * n)
                h_T(n + NBLK)

            def queries_keys(n, par):
                for k in range(2):
                    for m in range(KC):
                        if k == 0:
                            wait(pe, s_hTl, KC * n + (KC * NBLK + m + 1))
                            if m == 0:
                                wait(pe, s_hTl, KC * n + (KC * NBLK + KC))
                        else:
                            wait(pe, a_qf, 4 * n + (m + 1))
                        cols = slice(m * P, (m + 1) * P)
                        for c in range(KC):
                            last = split_product(bank[6 + m][:, :],
                                                 (wTh[:, k, c, cols], wTl[:, k, c, cols]),
                                                 (hTh[:, par, c, :], hTl[:, par, c, :]),
                                                 c == 0, c == KC - 1)
                        last.then_inc(a_qk, 1)

            def keys_T(n):
                wait(pe, a_qf, 4 * n + 4)
                for j in range(2):
                    for t in range(2 * j, 2 * j + 2):
                        for m in range(KC):
                            last = pe.transpose(bank[6 + j][:, (t % 2) * D + m * P:(t % 2) * D + (m + 1) * P],
                                                kf[:, m, t * P:(t + 1) * P], identf[:, :])
                    last.then_inc(a_kt, 1)

            def values(n, par):
                for j in range(2):
                    wait(pe, a_ktl, 2 * n + (j + 1))
                    for t in range(2 * j, 2 * j + 2):
                        rows = slice(t * P, (t + 1) * P)
                        for c in range(KC):
                            last = split_product(bank[6 + j][:, (t % 2) * D:(t % 2 + 1) * D],
                                                 (hTh[:, par, c, rows], hTl[:, par, c, rows]),
                                                 (wTh[:, 2, c, :], wTl[:, 2, c, :]),
                                                 c == 0, c == KC - 1)
                    last.then_inc(a_v, 1)

            def scores(c, n, par, t, g):
                if g == 0:
                    if t == 0:
                        wait(pe, a_kl, n + 1)
                    if t % 2 == 0:
                        wait(pe, a_qx[t // 2], NX * n + NX)
                wait(pe, a_sm, NG * (c - 1) + (g + 1))
                m, j0 = g // 2, 4 * (g % 2)
                cols = slice(t * P, (t + 1) * P)
                split_product(bank[g][:, :].rearrange("p (j t) -> p j t", j=4),
                              (kp[:, par, m, 0, cols], kp[:, par, m, 1, cols]),
                              (qx[:, j0:j0 + 4, m, 0, cols], qx[:, j0:j0 + 4, m, 1, cols]),
                              True, True).then_inc(a_s, 1)

            def outputs(c, n, par, t):
                wait(pe, a_z, c)
                wait(pe, a_ytc, c)
                cols = slice(t * P, (t + 1) * P)
                for m in range(KC):
                    pe.matmul(bank[4][:, m * P:(m + 1) * P], qf[:, par, m, cols], zst[:, par, m, :],
                              start=(m == 0), stop=False, skip_group_check=True)
                wait(pe, a_sl, (NG - 1) * c + (NG - 1))
                wait(pe, a_sll, c + 1)
                if t == 0:
                    wait(pe, a_vl, n + 1)
                for hd in range(4 * NG):
                    vs = slice(hd * HD, (hd + 1) * HD)
                    g, j = hd // 4, hd % 4
                    last = split_product(bank[4][:, vs], (shl[:, t % 2, 0, g, j], shl[:, t % 2, 1, g, j]),
                                         (vtok[:, par, 0, t, vs], vtok[:, par, 1, t, vs]),
                                         False, hd == 4 * NG - 1, skip_group_check=True)
                last.then_inc(a_y, 1)

            def keys_values(c, par, t):
                wait(pe, a_x, c)
                for m in range(KC):
                    cols = slice(m * P, (m + 1) * P)
                    last = split_product(bank[5][:, cols], (ktok[:, par, 0, t, cols], ktok[:, par, 1, t, cols]),
                                         (vtok[:, par, 0, t, cols], vtok[:, par, 1, t, cols]),
                                         True, True)
                last.then_inc(a_dz, 1)

            def y_T(c):
                wait(pe, a_ysb, c + 1)
                for m in range(KC):
                    last = pe.transpose(bank[4][:, m * P:(m + 1) * P], ysb[:, m * P:(m + 1) * P], identf[:, :])
                last.then_inc(a_yt, 1)

            def project(c):
                wait(pe, a_ytc, c + 1)
                wait(pe, a_dzm, c + 1)
                for m in range(KC):
                    last = pe.matmul(bank[5][:, 0:D], yT[:, m, :], woT[:, m, :], start=(m == 0), stop=(m == KC - 1))
                last.then_inc(a_wo, 1)

            def ffn(f):
                n0 = f * NBLK
                dg = n0 + 1
                if f == 0:
                    h_T(0)
                    router(0, 0, 0)
                    for j in range(NU):
                        gram(0, 0, j)

                def body(n, par, last):
                    for m in range(HC):
                        layer1(n, par, 0, m)
                        if isinstance(n, int) and n == n0 and m >= 1:
                            if m == 1:
                                std_rows(n)
                            else:
                                std_spread(n, 2 * m - 4)
                                std_spread(n, 2 * m - 3)
                    for m in range(HC):
                        layer1(n, par, 1, m)
                    if not last or f == 0:
                        wait(pe, s_sdB, E * (n + 1))
                        h_T(n + dg)
                    if f == 1 and isinstance(n, int) and n == n0:
                        pe.wait_ge(a_x, TB * NBLK)
                    for t in range(TB):
                        layer2(n, 0, t)
                    if not last:
                        router(n + 1, n + dg, 1 - par)
                    for m in range(HC):
                        layer1(n, par, 2, m)
                        if not last:
                            gram(n + 1, 1 - par, m)
                    for t in range(TB):
                        layer2(n, 1, t)
                    for m in range(HC):
                        layer1(n, par, 3, m)
                        if not last:
                            gram(n + 1, 1 - par, 4 + m)
                    if last and f == 0:
                        queries_keys(0, 0)
                    for t in range(TB):
                        layer2(n, 2, t)
                    if last and f == 0:
                        keys_T(0)
                    for t in range(TB):
                        layer2(n, 3, t)
                        if t == 1 and not last:
                            std_rows(n + 1)
                        if t >= 2 and not last:
                            std_spread(n + 1, 2 * t - 4)
                            std_spread(n + 1, 2 * t - 3)

                blocks(pe, n0, body)

            def attention():
                values(0, 0)
                pe.wait_ge(s_V, NA * NBLK)
                for g in range(NG):
                    scores(0, 0, 0, 0, g)

                def body(n, par, last):
                    for t in range(TB):
                        c = n * TB + t
                        first = t == 0 and isinstance(n, int) and n == 0
                        more = not (last and t == TB - 1)
                        nn, np_ = (n, par) if t < TB - 1 else (n + 1, 1 - par)
                        for g in range(NG):
                            if more:
                                scores(c + 1, nn, np_, (t + 1) % TB, g)
                            if g == 0 and not first:
                                y_T(c - 1)
                            if g == 1 and not first:
                                project(c - 1)
                        if t == 1 and not last:
                            rows_T(n + 1)
                        if t == 2 and not last:
                            keys_T(n + 1)
                        if t == 1 and last:
                            wait(pe, a_vf, 2 * NBLK)
                            h_T(2 * NBLK)
                        if t >= 2 and last:
                            gram(NBLK, 0, 6 * (t - 2))
                            gram(NBLK, 0, 6 * (t - 2) + 1)
                        if t == 0 and isinstance(n, int) and n == 0:
                            pe.wait_ge(s_acc, NO * NBLK)
                            pe.wait_ge(a_mask, 1)
                        outputs(c, n, par, t)
                        if t == 2 and last:
                            gram(NBLK, 0, 2)
                            gram(NBLK, 0, 3)
                        keys_values(c, par, t)
                        if t == 1 and last:
                            router(NBLK, 2 * NBLK, 0)
                        if t == 2 and last:
                            gram(NBLK, 0, 4)
                            gram(NBLK, 0, 5)
                        if t == 1 and not last:
                            queries_keys(n + 1, 1 - par)
                        if t == 2 and not last:
                            values(n + 1, 1 - par)

                blocks(pe, 0, body)
                y_T(TB * NBLK - 1)
                project(TB * NBLK - 1)
                pe.wait_ge(a_sm, NG * TB * NBLK)

            ffn(0)
            attention()
            ffn(1)


_INS = ['L0_attn_x', 'L0_attn_Wq', 'L0_attn_bq', 'L0_attn_Wk', 'L0_attn_bk', 'L0_attn_Wv', 'L0_attn_bv', 'L0_attn_Wo',
        'L0_attn_bo', 'L0_ffn_router_w', 'L0_ffn_rn_g', 'L0_ffn_rn_b', 'L0_ffn_w1', 'L0_ffn_ln_g', 'L0_ffn_ln_b',
        'L0_ffn_w2', 'L0_ffn_on_g', 'L0_ffn_on_b']
_OUTS = [((2, 2048, 256), 'float32')]


def kernel(**inputs):
    import numpy as _np
    import concourse.bacc as _bacc
    from concourse import mybir as _mybir
    from concourse.bass_utils import run_bass_kernel_spmd as _run

    nc = _bacc.Bacc("TRN2", target_bir_lowering=False, num_devices=1)
    arrays, args = {}, []
    for name in _INS:
        a = _np.ascontiguousarray(inputs[name])
        arrays[f"in_{name}_dram"] = a
        args.append(nc.dram_tensor(f"in_{name}_dram", a.shape, _mybir.dt.from_np(a.dtype), kind="ExternalInput").ap())
    for i, (shape, dtype) in enumerate(_OUTS):
        dt = _mybir.dt.from_np(_np.dtype(dtype))
        args.append(nc.dram_tensor(f"out_{i}_dram", shape, dt, kind="ExternalOutput").ap())
    macaron_kernel(nc, *args)
    r = _run(nc, [arrays], core_ids=[0])
    return r.results[0]["out_0_dram"]
```

```python
from contextlib import ExitStack

import concourse.bass as bass
from concourse import mybir

ALU = mybir.AluOpType
ACT = mybir.ActivationFunctionType
AX = mybir.AxisListType
F32 = mybir.dt.float32
F16 = mybir.dt.float16
U32 = mybir.dt.uint32
RMAX = bass.bass_isa.ReduceOp.max

P = 128
EPS = 1e-5
EPS_GATE = 1e-8
EXPONENT = 0x7F800000
TINY = 2.0 ** -40
TINY_ATT = 2.0 ** -16
S_SHIFT = 2.0 ** -19
STD_SHIFT = 64.0


def macaron_kernel(nc, x, Wq, bq, Wk, bk, Wv, bv, Wo, bo, router_w, rn_g, rn_b, w1, ln_g, ln_b, w2, on_g, on_b, out):
    NB, T, D = x.shape
    E, _, H = w1.shape
    NT = NB * T // P
    KC = D // P
    HC = H // P
    TB = 4
    BT = TB * P
    NBLK = NT // TB
    NSTD = 2 * E
    NV = 4
    NU = TB * E // 2
    NA = E * HC
    NO = E * TB
    HD = 16
    HPC = P // HD
    NG = D // HD // 4
    N_RS, N_RS_ATT = 12, 7
    NX = 16 * HPC

    x_t = x.rearrange("b (n p) d -> p (b n) d", p=P)
    out_t = out.rearrange("b (n p) d -> p (b n) d", p=P)

    with ExitStack() as ctx:
        def sb(name, shape, dt=F32):
            return ctx.enter_context(nc.sbuf_tensor(name, shape, dt))

        def sem(name):
            return ctx.enter_context(nc.semaphore(name))

        bank = [ctx.enter_context(nc.psum_tensor(f"bank{i}", [P, 512], F32)) for i in range(8)]

        X = sb("X", [P, NT, D])
        w1h = sb("w1h", [P, E, KC, H], F16)
        w1l = sb("w1l", [P, E, KC, H], F16)
        w2h = sb("w2h", [P, E, HC, D], F16)
        w2l = sb("w2l", [P, E, HC, D], F16)
        gramh = sb("gramh", [P, KC, E, D], F16)
        graml = sb("graml", [P, KC, E, D], F16)
        betas = sb("betas", [P, E, HC])
        sel = sb("sel", [NSTD, E, P], F16)
        routw = sb("routw", [P, KC, 2 * E], F16)
        routc = sb("routc", [P, E])
        ong = sb("ong", [P, D])
        onb = sb("onb", [P, D])
        identf = sb("identf", [P, P])
        ident16 = sb("ident16", [P, P], F16)
        nhalf = sb("nhalf", [P, TB, E])
        phalf = sb("phalf", [P, TB, E])
        inv_std = sb("inv_std", [P, TB, E])
        consts = sb("consts", [P, 4, TB])
        half_, inv_d, eps_, mone = (consts[:, k] for k in range(4))
        before = sb("before", [P, E, E])
        after = sb("after", [P, E, E])

        area = sb("area", [P, 101 * 256])

        def at_kb(kb, shape, dt=F32):
            n = 1
            for k in shape:
                n *= k
            words = n if dt == F32 else n // 2
            assert 256 * kb + words <= 101 * 256
            v = area[:, int(256 * kb):int(256 * kb) + words]
            v = v if dt == F32 else v.bitcast(dt)
            names = "abcdef"[:len(shape)]
            if len(shape) == 1:
                return v
            return v.rearrange(f"p ({' '.join(names)}) -> p {' '.join(names)}", **dict(zip(names, shape)))

        Rh = at_kb(0, [2, HC, BT], F16)
        Rl = at_kb(8, [2, HC, BT], F16)
        junk = at_kb(84, [TB * E, D], F16)
        h2 = at_kb(24, [TB, D])
        hr = at_kb(32, [TB, D], F16)
        sdT = at_kb(34, [BT], F16)[0:NSTD]
        sdB = at_kb(16, [E, BT])
        V = at_kb(76, [NV, BT])
        acc = at_kb(28, [TB, D])
        z = at_kb(36, [TB, D])
        gamB = at_kb(0, [E, H])
        w1T = at_kb(8, [2, HC, D])
        w1r = at_kb(40, [E, KC, H])
        w1g = at_kb(56, [E, KC, H])
        rnbB = at_kb(72, [KC, P])
        ones = at_kb(73, [P])
        wqkv = at_kb(92, [4, KC, D])
        stage = [X[:, 8:16], X[:, 24:32]]
        w2r = [stage[e // 2][:, e % 2 * HC:e % 2 * HC + HC, :] for e in range(E)]
        sm = at_kb(0, [NG, 4, P])
        shl = at_kb(8, [2, 2, NG, 4, P], F16)
        ktok = at_kb(24, [2, 2, TB, D], F16)
        vtok = at_kb(32, [2, 2, TB, D], F16)
        qx = at_kb(40, [HPC, KC, 2, BT], F16)
        qf = at_kb(72, [2, KC, BT])
        kf = at_kb(80, [KC, BT])
        vf = at_kb(80, [TB, D])
        qp = at_kb(84, [KC, 2, BT], F16)
        kp = at_kb(88, [2, KC, 2, BT], F16)
        ysb = at_kb(96, [D])
        yT = at_kb(97, [KC, P])
        dz = at_kb(98, [KC, P])
        zst = at_kb(99, [2, KC, P])

        pick = sb("pick", [NSTD, E])
        rw = sb("rw", [E, D])
        rwT = sb("rwT", [P, KC, E])
        rwg = sb("rwg", [P, KC, E])
        rngc = sb("rngc", [P, KC])
        rnbc = sb("rnbc", [P, KC])
        gamc = sb("gamc", [P, E, HC])
        rsum = sb("rsum", [P, E * KC])
        nmean = sb("nmean", [P, E * KC])
        mxw = sb("mxw", [P, E])
        mx = sb("mx", [P, 4])
        mx2 = sb("mx2", [P, 1])
        mx3 = sb("mx3", [P, 3])
        mxa = sb("mxa", [P, 4])
        mxa2 = sb("mxa2", [P, 1])
        mxa3 = sb("mxa3", [P, 3])
        sumgb = sb("sumgb", [P, 1])
        big = sb("big", [P, 6])
        capn = sb("capn", [P, 6])
        q = sb("q", [P, 6])
        qi = sb("qi", [P, 6])
        sc = sb("sc", [P, 8])
        epsq, bscale, kappa, aev, iys, gscale = (sc[:, k:k + 1] for k in (0, 1, 2, 4, 5, 7))
        qc, q1, qr, q2, qa, sa = (q[:, k:k + 1] for k in range(6))
        wTh = sb("wTh", [P, 3, KC, D], F16)
        wTl = sb("wTl", [P, 3, KC, D], F16)
        woT = sb("woT", [P, KC, D])
        bqk = sb("bqk", [P, 2, KC])
        bvB = sb("bvB", [P, D])
        boB = sb("boB", [P, D])
        causal = sb("causal", [P, P])
        sameh = sb("sameh", [P, P])

        xst = sb("xst", [P, TB, 6])
        xf = sb("xf", [P, 12, TB])
        xrs, xnr = xf[:, 10], xf[:, 11]
        r2a = sb("r2a", [P, TB])
        r2b = sb("r2b", [P, TB])
        r2c = sb("r2c", [P, TB])
        r2d = sb("r2d", [P, TB])
        r2 = sb("r2", [P, TB])
        h = sb("h", [P, TB, D])
        hTh = sb("hTh", [P, 2, KC, BT], F16)
        hTl = sb("hTl", [P, 2, KC, BT], F16)
        lsb = sb("lsb", [P, TB, 2 * E])
        lga = sb("lga", [P, TB, E])
        lgb = sb("lgb", [P, TB, E])
        lgc = sb("lgc", [P, TB, E])
        lgd = sb("lgd", [P, TB, E])
        lmax = sb("lmax", [P, TB])
        ex = sb("ex", [P, TB, E])
        var = sb("var", [P, TB, E])
        vare = sb("vare", [P, TB, E])
        sd = sb("sd", [P, TB, E])
        sds = sb("sds", [P, TB, E])
        rsd = sb("rsd", [P, TB, E])
        s12 = sb("s12", [P, TB, NSTD], F16)
        gt = sb("gt", [P, TB, E, E])
        ge = sb("ge", [P, TB, E, E])
        rank = sb("rank", [P, TB, E])
        es = sb("es", [P, TB, E])
        ws = sb("ws", [P, TB, E])
        tot = sb("tot", [P, 2, TB])
        den = sb("den", [P, TB])
        rden = sb("rden", [P, TB])
        coef = sb("coef", [P, 2, TB, E])
        ast = sb("ast", [P, TB, 6])
        af = sb("af", [P, 12, TB])
        ars, anr = af[:, 10], af[:, 11]

        l_att = sem("l_att")
        l_w1 = [sem(f"l_w1_{e}") for e in range(E)]
        l_x = [sem(f"l_x{b}") for b in range(2)] + [sem("l_x_next"), sem("l_x_staged")]
        l_w2, l_gam, l_bet, l_rw, l_on = (sem(n) for n in ("l_w2", "l_gam", "l_bet", "l_rw", "l_on"))
        p_id = sem("p_id")
        p_m = sem("p_m")
        p_c = sem("p_c")
        p_mx = sem("p_mx")
        p_mxa = sem("p_mxa")
        p_q = sem("p_q")
        p_gam = sem("p_gam")
        p_w1g = sem("p_w1g")
        p_w1h = sem("p_w1h")
        p_w1l = sem("p_w1l")
        p_w2s = sem("p_w2s")
        p_w2h = sem("p_w2h")
        p_w2l = sem("p_w2l")
        p_wt = sem("p_wt")
        p_wtc = sem("p_wtc")
        p_g = sem("p_g")
        p_gh = sem("p_gh")
        p_gl = sem("p_gl")
        p_rt = sem("p_rt")
        p_rc = sem("p_rc")
        p_rw = sem("p_rw")
        p_sel = sem("p_sel")
        p_as = sem("p_as")
        (s_mv, s_rs, s_h, s_hr, s_T, s_hTh, s_hTl, s_h2, s_L, s_lg, s_lgl, s_lmax, s_lgm, s_E, s_U, s_var, s_sd,
         s_rsd, s_vare, s_s12, s_ST, s_sdT, s_coef, s_A, s_SB, s_sdB, s_V, s_Rh, s_Rl, s_O, s_acc, s_amv, s_ars, s_z,
         s_x, s_xb, s_zg, s_out) = (sem(n) for n in (
            "x_stats", "x_rstd", "h_ready", "h_rounded", "hT_psum", "hT_high", "hT_low", "h2_ready", "logits_psum",
            "logits_copied", "logits_ready", "logits_max", "logits_less_max", "exp_ready", "gram_psum", "var_ready",
            "std_ready", "rstd_ready", "var_guarded", "std_parts", "stdT_psum", "stdT_ready", "coef_ready", "hid_psum",
            "stdB_psum", "stdB_ready", "hid_ready", "relu_high", "relu_low", "out_psum", "acc_ready", "acc_stats",
            "acc_rstd", "z_ready", "x_updated", "last_x_with_bias", "last_z_scaled", "stored"))
        (a_zero, a_mask, a_w, a_wh, a_wl, a_qk, a_qf, a_qh, a_kh, a_qp, a_kl, a_kt, a_kth, a_ktl, a_v, a_vf,
         a_vh, a_vl, a_xb, a_s, a_sm, a_sh, a_sl, a_sll, a_y, a_ysb, a_yt, a_ytc, a_wo, a_x, a_dz, a_dzm, a_z) = (
            sem("a_" + n) for n in (
            "queries_cleared", "state_cleared", "weights_T_psum", "weights_high", "weights_low", "qk_psum", "qk_copied",
            "q_high", "k_high", "q_parts", "k_parts", "ktok_psum", "ktok_high", "ktok_low", "v_psum",
            "v_copied", "v_high", "v_low", "bias_added", "scores_psum", "scores_masked", "scores_high", "scores_low",
            "last_scores_low",
            "y_psum", "y_copied", "yT_psum", "yT_copied", "proj_psum", "x_updated", "kv_psum", "kv_masked",
            "kv_added"))
        a_qx = [sem(f"a_q_expanded{half}") for half in range(2)]
        dve_done = sem("dve_done")
        pool_done = sem("pool_done")

        block = ctx.enter_context(nc.Block())

        def wait(eng, s, value):
            if isinstance(value, int) and value <= 0:
                return
            eng.wait_ge(s, value)

        def tile0(n, n0, par):
            return (n - par - n0) * (TB // 2) + par * (NT // 2)

        def two_ahead(n, n0):
            return not isinstance(n, int) or n < n0 + NBLK - 2

        def att_ahead(n):
            return isinstance(n, int) and n == NBLK - 2

        class Steps:
            def __init__(self, eng, s, at=0):
                self.eng, self.s, self.at = eng, s, at

            def __call__(self, ins):
                ins.then_inc(self.s, 1)
                self.at = self.at + 1
                self.eng.wait_ge(self.s, self.at)

        def blocks(eng, n0, body):
            body(n0, 0, False)
            body(n0 + 1, 1, False)
            with eng.Fori(n0 // 2 + 1, (n0 + NBLK) // 2 - 1, 1) as pair:
                body(2 * pair, 0, False)
                body(2 * pair + 1, 1, False)
            body(n0 + NBLK - 2, 0, False)
            return body(n0 + NBLK - 1, 1, True)

        @block.sync
        def _(sp):
            def load_x(b, done):
                sp.dma_start(X[:, b * TB:(b + 1) * TB, :], x_t[:, b * TB:(b + 1) * TB, :]).then_inc(done, 16)

            load_x(0, l_x[0])
            for e in range(E):
                sp.dma_start(w1r[:, e], w1[e].rearrange("(c p) n -> p c n", p=P)).then_inc(l_w1[e], 16)
            for e in range(0, E, 2):
                sp.dma_start(stage[e // 2], w2[e:e + 2].rearrange("e (c p) n -> p (e c) n", p=P)).then_inc(l_w2, 16)
            load_x(NBLK // 2, l_x[1])
            for b in (1, NBLK // 2 + 1):
                load_x(b, l_x[2])
            for k, w in enumerate((Wq, Wk, Wv, Wo)):
                sp.dma_start(wqkv[:, k], w.rearrange("(c p) n -> p c n", p=P)).then_inc(l_att, 16)
            for k, v in enumerate((bq, bk)):
                sp.dma_start(bqk[:, k, :], v.rearrange("(c p) -> p c", p=P),
                             allow_slow_non_contiguous=True).then_inc(l_att, 16)
            for d, v, done in ((bvB, bv, l_att), (boB, bo, l_att), (ong, on_g, l_on), (onb, on_b, l_on)):
                sp.dma_start(d[:, :], v.rearrange("(a n) -> a n", a=1).to_broadcast([P, D])).then_inc(done, 16)
            sp.wait_ge(p_w2l, E)
            for b in (2, 3, NBLK - 2, NBLK - 1):
                load_x(b, l_x[3])

            def expand(n):
                wait(sp, a_qp, n + 1)
                for half in range(2):
                    cols = slice(half * BT // 2, (half + 1) * BT // 2)
                    wait(sp, a_s, NG * TB * (n - 1) + NG * 2 * (half + 1))
                    for j in range(HPC):
                        rows = slice(j * HD, (j + 1) * HD)
                        sp.dma_start(qx[rows, j, :, :, cols], qp[rows, :, :, cols]).then_inc(a_qx[half], 16)

            sp.wait_ge(a_zero, 1)
            expand(0)
            with sp.Fori(1, NBLK, 1) as n:
                expand(n)

            def store(n):
                for par in range(2):
                    t0 = tile0(n + par, NBLK, par)
                    if isinstance(n, int) and par == 1:
                        for t in range(TB):
                            sp.wait_ge(s_x, TB * (n + par) + t + 1)
                            sp.dma_start(out_t[:, t0 + t, :], X[:, t0 + t, :]).then_inc(s_out, 16)
                    else:
                        sp.wait_ge(s_x, TB * (n + par + 1))
                        sp.dma_start(out_t[:, bass.ds(t0, TB), :], X[:, bass.ds(t0, TB), :]).then_inc(s_out, 16)

            with sp.Fori(NBLK // 2, NBLK - 1, 1) as pair:
                store(2 * pair)
            store(2 * NBLK - 2)
            sp.wait_ge(s_out, 16 * (NBLK - 1 + TB))

        @block.gpsimd
        def _(pool):
            step = Steps(pool, pool_done)
            step(pool.memset(identf[:, :], 0.0))
            step(pool.affine_select(out=identf[:, :], in_=identf[:, :], compare_op=ALU.not_equal, fill=1.0,
                                    base=0, pattern=[[-1, P]], channel_multiplier=1))
            pool.memset(ones, 1.0).then_inc(p_id, 1)
            for k, v in enumerate((0.5, 1.0 / D, EPS, -1.0)):
                step(pool.memset(consts[:, k], v))
            step(pool.memset(nhalf[:, :, :], -0.5))
            step(pool.memset(phalf[:, :, :], 0.5))
            def bc(a):
                return a.unsqueeze(2).to_broadcast([P, TB, E])

            def norm_factors(stats, f, at, done):
                me, qe, mo, qo = (stats[:, :, k] for k in (1, 2, 4, 5))
                pool.tensor_tensor(f[:, 0], me, mo, ALU.add)
                pool.tensor_tensor(f[:, 1], me, mo, ALU.subtract)
                at(pool.tensor_tensor(f[:, 2], qe, qo, ALU.add))
                pool.tensor_tensor(f[:, 3], f[:, 0], half_, ALU.mult)
                pool.tensor_tensor(f[:, 4], f[:, 1], half_, ALU.mult)
                at(pool.tensor_tensor(f[:, 5], f[:, 2], inv_d, ALU.mult))
                at(pool.tensor_tensor(f[:, 6], f[:, 4], f[:, 4], ALU.mult))
                at(pool.tensor_tensor(f[:, 8], f[:, 5], f[:, 6], ALU.add))
                at(pool.tensor_tensor(f[:, 9], f[:, 8], eps_, ALU.add))
                at(pool.tensor_tensor(f[:, 10], f[:, 9], nhalf[:, :, 0], ALU.pow))
                at(pool.tensor_tensor(f[:, 7], f[:, 3], f[:, 10], ALU.mult))
                pool.tensor_tensor(f[:, 11], f[:, 7], mone, ALU.mult).then_inc(done, 1)

            def rs(g, at, router):
                wait(pool, s_mv, g + 1)
                wait(pool, s_h, g)
                norm_factors(xst, xf, at, s_rs)
                if router:
                    second_norm(at)

            def second_norm(at):
                at(pool.tensor_tensor(r2a[:, :], xf[:, 8], xrs, ALU.mult))
                at(pool.tensor_tensor(r2b[:, :], r2a[:, :], xrs, ALU.mult))
                at(pool.tensor_tensor(r2c[:, :], r2b[:, :], eps_, ALU.add))
                at(pool.tensor_tensor(r2d[:, :], r2c[:, :], nhalf[:, :, 0], ALU.pow))
                at(pool.tensor_tensor(r2[:, :], r2d[:, :], qi[:, 2:3].to_broadcast([P, TB]), ALU.mult))

            rs(0, step, False)
            for j, c in enumerate((128.0, 128.0, 1024.0, 32768.0, 1024.0, 32768.0)):
                pool.memset(capn[:, j:j + 1], c).then_inc(p_id, 1)
            step(pool.tensor_copy(ident16[:, :], identf[:, :]))
            step(pool.memset(inv_std[:, :, :], 1.0 / STD_SHIFT))
            step(pool.memset(before[:, :, :], 1.0))
            step(pool.affine_select(out=before[:, :, :], in_=before[:, :, :], compare_op=ALU.is_ge, fill=0.0,
                                    base=-1, pattern=[[1, E], [-1, E]], channel_multiplier=0))
            step(pool.tensor_scalar(after[:, :, :], before[:, :, :], -1.0, 1.0, ALU.mult, ALU.add))
            step(pool.memset(causal[:, :], 1.0))
            step(pool.affine_select(out=causal[:, :], in_=causal[:, :], compare_op=ALU.is_ge, fill=0.0,
                                    base=0, pattern=[[1, P]], channel_multiplier=-1))
            step(pool.memset(sameh[:, :], 1.0))
            sameh_v = sameh[:, :].rearrange("p (j d) -> p j d", d=HD)
            for base, jd, cm in ((0, -HD, 1), (HD - 1, HD, -1)):
                step(pool.affine_select(out=sameh_v, in_=sameh_v, compare_op=ALU.is_ge, fill=0.0,
                                        base=base, pattern=[[jd, HPC], [0, HD]], channel_multiplier=cm))
            pool.wait_ge(p_mx, 1)
            pool.partition_all_reduce(mxa[:, :], mx[:, :], P, RMAX).then_inc(p_mxa, 1)
            pool.wait_ge(p_q, 1)
            second_norm(step)

            def logits(n, at):
                wait(pool, s_lg, n + 1)
                at(pool.tensor_tensor(lga[:, :, :], lsb[:, :, 0:E], lsb[:, :, E:2 * E], ALU.add))
                at(pool.tensor_tensor(lgb[:, :, :], lga[:, :, :], bc(r2[:, :]), ALU.mult))
                pool.tensor_tensor(lgc[:, :, :], lgb[:, :, :], routc[:, :].unsqueeze(1).to_broadcast([P, TB, E]),
                                   ALU.add).then_inc(s_lgl, 1)

            def less_max(n, at):
                wait(pool, s_lmax, n + 1)
                pool.tensor_tensor(lgd[:, :, :], lgc[:, :, :], bc(lmax[:, :]), ALU.subtract).then_inc(s_lgm, 1)

            def std(n, at):
                wait(pool, s_vare, n + 1)
                wait(pool, s_s12, n)
                wait(pool, s_coef, n)
                at(pool.tensor_tensor(sd[:, :, :], vare[:, :, :], phalf[:, :, :], ALU.pow))
                pool.tensor_tensor(sds[:, :, :], sd[:, :, :], inv_std[:, :, :], ALU.mult).then_inc(s_sd, 1)
                pool.tensor_tensor(rsd[:, :, :], vare[:, :, :], nhalf[:, :, :], ALU.pow).then_inc(s_rsd, 1)

            def post_stats(n, at):
                wait(pool, s_amv, TB * n + TB)
                wait(pool, s_z, TB * n)
                norm_factors(ast, af, at, s_ars)

            def post_tile(n, par, f, t, at):
                xt = X[:, tile0(n, f * NBLK, par) + t, :]
                wait(pool, s_z, TB * n + (t + 1))
                at(pool.tensor_tensor(z[:, t, :], z[:, t, :], ong[:, :], ALU.mult))
                at(pool.tensor_tensor(z[:, t, :], z[:, t, :], onb[:, :], ALU.add))
                pool.tensor_tensor(xt, xt, z[:, t, :], ALU.add).then_inc(s_x, 1)

            def post(n, par, f, at):
                for t in range(TB):
                    post_tile(n, par, f, t, at)

            def add_bias(n, par):
                t0 = tile0(n, 0, par)
                wait(pool, s_h, n + (NBLK + 1))
                xt = X[:, bass.ds(t0, TB), :]
                pool.tensor_tensor(xt, xt, boB[:, :].unsqueeze(1).to_broadcast([P, TB, D]),
                                   ALU.add).then_inc(a_xb, 1)

            def key_low(n, par):
                wait(pool, a_kh, n + 1)
                pool.tensor_tensor(kp[:, par, :, 1], kf, kp[:, par, :, 0], ALU.subtract).then_inc(a_kl, 1)

            def score_low(c, cp, g):
                wait(pool, a_sh, NG * c + (g + 1))
                wait(pool, a_y, c - 1)
                pool.tensor_tensor(shl[:, cp, 1, g], sm[:, g], shl[:, cp, 0, g], ALU.subtract).then_inc(a_sl, 1)

            def add_state(c, par):
                wait(pool, a_dzm, c + 1)
                wait(pool, a_y, c + 1)
                pool.tensor_tensor(zst[:, par], zst[:, par], dz, ALU.add).then_inc(a_z, 1)

            def ffn(f):
                n0 = f * NBLK
                g0 = 2 * f * NBLK
                at = Steps(pool, pool_done, step.at)
                if f == 0:
                    def w1_low(e):
                        pool.wait_ge(p_w1h, e + 1)
                        pool.tensor_tensor(w1l[:, e], w1g[:, e], w1h[:, e], ALU.subtract).then_inc(p_w1l, 1)

                    def w2_low(e):
                        pool.wait_ge(p_w2h, e + 1)
                        pool.tensor_tensor(w2l[:, e], w2r[e], w2h[:, e], ALU.subtract).then_inc(p_w2l, 1)

                    w1_low(0)
                    logits(n0, at)
                    w1_low(1)
                    pool.wait_ge(p_mx, 2)
                    pool.partition_all_reduce(mxa2[:, :], mx2[:, :], P, RMAX).then_inc(p_mxa, 1)
                    w1_low(2)
                    w1_low(3)
                    less_max(n0, at)
                    std(n0, at)
                    rs(g0 + 1, at, True)
                    for e in range(E):
                        w2_low(e)
                start = at.at
                n_post = N_RS_ATT + 2 * TB
                per = 3 + N_RS + n_post

                def body(n, par, last):
                    first = isinstance(n, int) and n == n0
                    at = Steps(pool, pool_done, start if first else (n - n0) * per + (start - n_post))
                    if last:
                        at.at = at.at - (N_RS - (N_RS_ATT if f == 0 else 0))
                    if not first:
                        post_stats(n - 1, at)
                        post(n - 1, 1 - par, f, at)
                    if not last:
                        logits(n + 1, at)
                        less_max(n + 1, at)
                    if two_ahead(n, n0):
                        rs(n + (2 + g0 - n0), at, True)
                    elif att_ahead(n):
                        rs(NBLK, at, False)
                    if not last:
                        std(n + 1, at)
                    if f == 0 and first:
                        pool.wait_ge(p_w1l, E)
                        pool.wait_ge(p_g, E)
                        pool.wait_ge(p_mx, 3)
                        pool.partition_all_reduce(mxa3[:, :], mx3[:, :], P, RMAX).then_inc(p_mxa, 1)
                        pool.memset(qx.rearrange("p a b c d -> p (a b c d)").bitcast(F32), 0.0).then_inc(a_zero, 1)
                    return at

                at = blocks(pool, n0, body)
                if f == 0:
                    add_bias(0, 0)
                    key_low(0, 0)
                if f == 1:
                    xl = X[:, NT - TB:NT]
                    pool.tensor_tensor(xl, xl, onb[:, :].unsqueeze(1).to_broadcast([P, TB, D]),
                                       ALU.add).then_inc(s_xb, 1)
                post_stats(n0 + NBLK - 1, at)
                step.at = at.at

            def attention():
                at = Steps(pool, pool_done, step.at)
                pool.wait_ge(a_w, 4)
                pool.memset(zst, 0.0).then_inc(a_mask, 1)
                pool.wait_ge(a_mask, 1)
                for g in range(NG - 1):
                    score_low(0, 0, g)
                post_tile(NBLK - 1, 1, 0, 0, at)
                start = at.at
                per = N_RS_ATT
                extra = 2 * (TB - 1)

                def body(n, par, last):
                    first = isinstance(n, int) and n == 0
                    at = Steps(pool, pool_done, start if first else n * per + (start + extra))
                    for t in range(TB):
                        c = n * TB + t
                        if t == 0 and not last:
                            rs(n + (NBLK + 1), at, False)
                        if t == 0 and last:
                            rs(2 * NBLK, at, True)
                        for g in range(NG - 1):
                            if not (last and t == TB - 1):
                                score_low(c + 1, (t + 1) % 2, g)
                            if t == 2 and g == 0 and not last:
                                key_low(n + 1, 1 - par)
                        if t == 1 and not last:
                            add_bias(n + 1, 1 - par)
                        if first and t < TB - 1:
                            post_tile(NBLK - 1, 1, 0, t + 1, at)
                        if last and t == 3:
                            std(NBLK, at)
                        add_state(c, par)
                        if last and t == 1:
                            logits(NBLK, at)
                        if last and t == 2:
                            less_max(NBLK, at)
                    if last:
                        rs(2 * NBLK + 1, at, True)
                    return at

                at = blocks(pool, 0, body)
                step.at = at.at

            ffn(0)
            attention()
            ffn(1)

        @block.vector
        def _(dve):
            step = Steps(dve, dve_done)
            def x_stats(g, t0, tiles=range(TB)):
                if tiles[0] == 0:
                    wait(dve, s_rs, g)
                for t in tiles:
                    last = dve.bn_stats(xst[:, t, :], X[:, t0 + t, :])
                if tiles[-1] == TB - 1:
                    last.then_inc(s_mv, 1)

            def hT_low(g, par, chunks=range(KC)):
                for c in chunks:
                    wait(dve, s_hTh, KC * g + (c + 1))
                    dve.tensor_tensor(hTl[:, par, c, :], bank[6 + c][:, :], hTh[:, par, c, :],
                                      ALU.subtract).then_inc(s_hTl, 1)

            def h_twice(n):
                wait(dve, s_hr, n + 1)
                wait(dve, s_var, NU * n)
                dve.scalar_tensor_tensor(out=h2.rearrange("p t d -> p (t d)"),
                                         in0=h[:, :, :].rearrange("p t d -> p (t d)"), scalar=2.0,
                                         in1=hr.rearrange("p t d -> p (t d)"),
                                         op0=ALU.mult, op1=ALU.subtract).then_inc(s_h2, 1)

            def logits_copy(n):
                wait(dve, s_L, n + 1)
                wait(dve, s_lgl, n)
                dve.tensor_copy(lsb[:, :, :].rearrange("p t e -> p (t e)"),
                                bank[6][:, 0:TB * 2 * E]).then_inc(s_lg, 1)

            def logits_max(n):
                wait(dve, s_lgl, n + 1)
                wait(dve, s_lgm, n)
                dve.tensor_reduce(lmax[:, :], lgc[:, :, :], AX.X, ALU.max).then_inc(s_lmax, 1)

            def variance(n, j):
                t, e0 = j // 2, 2 * (j % 2)
                if j == 0:
                    wait(dve, s_h2, n + 1)
                    wait(dve, s_sd, n)
                wait(dve, s_U, NU * n + (j + 1))
                for e in range(e0, e0 + 2):
                    last = dve.tensor_tensor_reduce(out=junk[:, t * E + e, :],
                                                    in0=bank[7 - j % 2][:, (e - e0) * D:(e - e0 + 1) * D],
                                                    in1=h2[:, t, :], scale=1.0, scalar=0.0, op0=ALU.mult,
                                                    op1=ALU.add, accum_out=var[:, t, e:e + 1])
                last.then_inc(s_var, 1)

            def std_parts(n, at):
                wait(dve, s_sd, n + 1)
                wait(dve, s_ST, n)
                at(dve.tensor_copy(s12[:, :, 0:E], sds[:, :, :]))
                dve.tensor_tensor(s12[:, :, E:2 * E], sds[:, :, :], s12[:, :, 0:E], ALU.subtract).then_inc(s_s12, 1)

            def hidden(n, e, m):
                a = e * HC + m
                if m == 0:
                    wait(dve, s_sdB, E * n + (e + 1))
                wait(dve, s_A, NA * n + (a + 1))
                wait(dve, s_Rl, NA * n + (a - NV + 1))
                dve.scalar_tensor_tensor(out=V[:, a % NV], in0=sdB[:, e], scalar=betas[:, e, m:m + 1],
                                         in1=bank[m][:, :], op0=ALU.mult, op1=ALU.add).then_inc(s_V, 1)

            def relu_low(n, e, m):
                a = e * HC + m
                wait(dve, s_Rh, NA * n + (a + 1))
                if m == 0:
                    wait(dve, s_O, NO * n + (e * TB - TB))
                dve.scalar_tensor_tensor(out=Rl[:, e % 2, m, :], in0=V[:, a % NV], scalar=0.0,
                                         in1=Rh[:, e % 2, m, :], op0=ALU.max, op1=ALU.subtract).then_inc(s_Rl, 1)

            def accumulate(n, par, e, t):
                o = e * TB + t
                if o == 0:
                    wait(dve, s_coef, n + 1)
                wait(dve, s_O, NO * n + (o + 1))
                src = bank[4 + t % 2][:, 0:D]
                if e == 0:
                    wait(dve, s_z, TB * (n - 1) + (t + 1))
                    ins = dve.tensor_scalar(acc[:, t, :], src, coef[:, par, t, e:e + 1], None, ALU.mult)
                else:
                    wait(dve, s_acc, NO * n + (o - TB + 1))
                    ins = dve.scalar_tensor_tensor(out=acc[:, t, :], in0=src, scalar=coef[:, par, t, e:e + 1],
                                                   in1=acc[:, t, :], op0=ALU.mult, op1=ALU.add)
                ins.then_inc(s_acc, 1)

            def acc_stats(n, t):
                wait(dve, s_acc, NO * n + (NO - TB + t + 1))
                if t == 0:
                    wait(dve, s_ars, n)
                dve.bn_stats(ast[:, t, :], acc[:, t, :]).then_inc(s_amv, 1)

            def guard(n):
                wait(dve, s_var, NU * n + NU)
                wait(dve, s_rsd, n)
                dve.tensor_scalar(vare[:, :, :], var[:, :, :], 0.0, epsq, ALU.max, ALU.add).then_inc(s_vare, 1)

            def first_block_and_weights(at):
                def scales(lo, hi, at):
                    at(dve.tensor_scalar(big[:, lo:hi], big[:, lo:hi], TINY, None, ALU.max))
                    at(dve.reciprocal(q[:, lo:hi], big[:, lo:hi]))
                    at(dve.tensor_tensor(q[:, lo:hi], q[:, lo:hi], capn[:, lo:hi], ALU.mult))
                    at(dve.tensor_scalar(q[:, lo:hi].bitcast(U32), q[:, lo:hi].bitcast(U32), EXPONENT, None,
                                         ALU.bitwise_and))
                    at(dve.reciprocal(qi[:, lo:hi], q[:, lo:hi]))

                dve.wait_ge(l_x[0], 16)
                x_stats(0, 0)
                for e in range(E):
                    ks = slice(e * KC, (e + 1) * KC)
                    dve.wait_ge(l_w1[e], 16)
                    at(dve.tensor_reduce(rsum[:, ks], w1r[:, e], AX.X, ALU.add))
                    dve.tensor_scalar(nmean[:, ks], rsum[:, ks], -1.0 / H, None, ALU.mult).then_inc(p_m, 1)
                for e in range(E):
                    dve.wait_ge(p_c, KC * e + KC)
                    dve.tensor_reduce(mxw[:, e:e + 1], w1r[:, e].rearrange("p c n -> p (c n)"), AX.X, ALU.max,
                                      apply_absolute_value=True).then_inc(p_m, 1)
                dve.wait_ge(l_rw, 48)
                dve.wait_ge(p_id, 1)
                for c in range(KC):
                    last = dve.tensor_scalar(rnbB[:, c, :], ones[:, :], rnbc[:, c:c + 1], None, ALU.mult)
                dve.wait_ge(p_rt, 1)
                at(dve.tensor_copy(rwT[:, :, :], bank[5][:, 0:KC * E].rearrange("p (c e) -> p c e", c=KC)))
                for c in range(KC):
                    last = dve.tensor_scalar(rwg[:, c, :], rwT[:, c, :], rngc[:, c:c + 1], None, ALU.mult)
                last.then_inc(p_rc, 1)
                dve.wait_ge(p_rc, 1)
                dve.wait_ge(p_m, 2 * E)
                dve.wait_ge(l_bet, 16 * 2)
                for j, a in ((0, mxw[:, :]), (1, gamc[:, :, :].rearrange("p e m -> p (e m)")),
                             (2, betas[:, :, :].rearrange("p e m -> p (e m)")),
                             (3, rwg[:, :, :].rearrange("p c e -> p (c e)"))):
                    last = dve.tensor_reduce(mx[:, j:j + 1], a, AX.X, ALU.max, apply_absolute_value=True)
                last.then_inc(p_mx, 1)
                dve.wait_ge(p_id, 1 + 6)
                dve.wait_ge(p_mxa, 1)
                at(dve.tensor_scalar(big[:, 0:1], mxa[:, 0:1], TINY, None, ALU.max))
                at(dve.tensor_tensor(sumgb[:, :], mxa[:, 1:2], mxa[:, 2:3], ALU.add))
                at(dve.tensor_tensor(big[:, 1:2], big[:, 0:1], sumgb[:, :], ALU.mult))
                at(dve.tensor_copy(big[:, 2:3], mxa[:, 3:4]))
                scales(0, 3, at)
                at(dve.tensor_scalar(gscale, qc, qc, 1.0 / H, ALU.mult, ALU.mult))
                dve.tensor_scalar(epsq, qc, qc, EPS, ALU.mult, ALU.mult)
                dve.tensor_scalar(sc[:, 3:4], qc, qi[:, 1:2], None, ALU.mult)
                dve.tensor_scalar(bscale, q1, qi[:, 0:1], STD_SHIFT, ALU.mult, ALU.mult).then_inc(p_q, 1)
                dve.wait_ge(p_q, 1)
                at(dve.tensor_scalar(routw[:, :, 0:E], rwg[:, :, :], qr, None, ALU.mult))
                dve.scalar_tensor_tensor(out=routw[:, :, E:2 * E], in0=rwg[:, :, :], scalar=qr,
                                         in1=routw[:, :, 0:E], op0=ALU.mult, op1=ALU.subtract).then_inc(p_rw, 1)
                def with_gamma(e):
                    dve.wait_ge(p_c, KC * e + KC)
                    dve.wait_ge(p_gam, 1)
                    dve.tensor_tensor(w1g[:, e], w1r[:, e], gamB[:, e, :].unsqueeze(1).to_broadcast([P, KC, H]),
                                      ALU.mult).then_inc(p_w1g, 1)

                def gram_low(e):
                    dve.wait_ge(p_gh, e + 1)
                    dve.scalar_tensor_tensor(out=graml[:, :, e, :],
                                             in0=bank[4 + e % 2][:, :].rearrange("p (c n) -> p c n", c=KC),
                                             scalar=gscale, in1=gramh[:, :, e, :],
                                             op0=ALU.mult, op1=ALU.subtract).then_inc(p_gl, 1)

                hT_low(0, 0)
                gram_low(0)
                h_twice(0)
                gram_low(1)
                for e in range(E):
                    with_gamma(e)
                gram_low(2)
                dve.wait_ge(l_w2, 16 * 2)
                dve.tensor_reduce(mxw[:, 0:1], stage[0].rearrange("p t d -> p (t d)"), AX.X, ALU.max,
                                  apply_absolute_value=True)
                gram_low(3)
                dve.wait_ge(p_rt, 2)
                dve.tensor_copy(routc[:, :], bank[7][:, 0:E]).then_inc(p_rc, 1)
                logits_copy(0)
                at(dve.tensor_reduce(mxw[:, 1:2], stage[1].rearrange("p t d -> p (t d)"), AX.X, ALU.max,
                                     apply_absolute_value=True))
                dve.tensor_reduce(mx2[:, :], mxw[:, 0:2], AX.X, ALU.max).then_inc(p_mx, 1)
                variance(0, 0)
                variance(0, 1)
                dve.wait_ge(p_mxa, 2)
                at(dve.tensor_copy(big[:, 3:4], mxa2[:, :]))
                scales(3, 4, at)
                dve.tensor_scalar(kappa, sc[:, 3:4], qi[:, 3:4], None, ALU.mult).then_inc(p_q, 1)
                for j in range(2, NU // 2):
                    variance(0, j)
                logits_max(0)
                for j in range(NU // 2, NU):
                    variance(0, j)
                guard(0)
                dve.wait_ge(l_x[1], 16)
                x_stats(1, tile0(1, 0, 1))
                at(dve.tensor_scalar(betas[:, :, :], betas[:, :, :], bscale, None, ALU.mult))
                at(dve.tensor_tensor(pick[:, 0:E], identf[0:NSTD, 0:E], identf[0:NSTD, E:2 * E], ALU.add))
                dve.tensor_copy(sel[:, :, :], pick[:, :].unsqueeze(2).to_broadcast([NSTD, E, P])).then_inc(p_sel, 1)
                dve.wait_ge(l_on, 32)
                dve.tensor_scalar(ong[:, :], ong[:, :], 0.5, None, ALU.mult)
                at(dve.tensor_scalar(onb[:, :], onb[:, :], 0.5, None, ALU.mult))
                std_parts(0, at)
                choose(0, at)
                weigh(at)
                coefs(0, 0)

            def attention_maxima():
                dve.wait_ge(l_att, 16 * 8)
                for j, a in enumerate((wqkv[:, 0:3].rearrange("p k c n -> p (k c n)"),
                                       bqk[:, :, :].rearrange("p k c -> p (k c)"), bvB[:, :])):
                    last = dve.tensor_reduce(mx3[:, j:j + 1], a, AX.X, ALU.max, apply_absolute_value=True)
                last.then_inc(p_mx, 1)

            def attention_scales():
                at = Steps(dve, p_as)
                dve.wait_ge(p_mxa, 3)
                at(dve.tensor_scalar(big[:, 4:5], mxa3[:, 0:1], TINY_ATT, None, ALU.max))
                at(dve.tensor_tensor(sumgb[:, :], mxa3[:, 1:2], mxa3[:, 2:3], ALU.max))
                at(dve.scalar_tensor_tensor(out=big[:, 5:6], in0=big[:, 4:5], scalar=float(D), in1=sumgb[:, :],
                                            op0=ALU.mult, op1=ALU.add))
                at(dve.reciprocal(q[:, 4:6], big[:, 4:6]))
                at(dve.tensor_tensor(q[:, 4:6], q[:, 4:6], capn[:, 4:6], ALU.mult))
                at(dve.tensor_scalar(q[:, 4:6].bitcast(U32), q[:, 4:6].bitcast(U32), EXPONENT, None,
                                     ALU.bitwise_and))
                at(dve.reciprocal(qi[:, 4:6], q[:, 4:6]))
                dve.tensor_scalar(aev, sa, qi[:, 4:5], None, ALU.mult)
                at(dve.tensor_scalar(sc[:, 6:7], qi[:, 5:6], qi[:, 5:6], None, ALU.mult))
                dve.tensor_scalar(iys, sc[:, 6:7], qi[:, 5:6], 1.0 / S_SHIFT, ALU.mult, ALU.mult)
                dve.tensor_scalar(bqk[:, :, :], bqk[:, :, :], sa, None, ALU.mult)
                dve.tensor_scalar(bvB[:, :], bvB[:, :], sa, None, ALU.mult).then_inc(p_q, 1)

            def weight_low(k):
                dve.wait_ge(a_wh, k + 1)
                dve.scalar_tensor_tensor(out=wTl[:, k].rearrange("p c n -> p (c n)"), in0=bank[6 + k % 2][:, :],
                                         scalar=qa, in1=wTh[:, k].rearrange("p c n -> p (c n)"),
                                         op0=ALU.mult, op1=ALU.subtract).then_inc(a_wl, 1)

            def choose(n, at):
                wait(dve, s_E, n + 1)
                other = ex[:, :, :].unsqueeze(2).to_broadcast([P, TB, E, E])
                own = ex[:, :, :].unsqueeze(3).to_broadcast([P, TB, E, E])
                dve.tensor_tensor(gt[:, :, :, :], other, own, ALU.is_gt)
                at(dve.tensor_tensor(ge[:, :, :, :], other, own, ALU.is_ge))
                for m, mask in ((gt, after), (ge, before)):
                    last = dve.tensor_tensor(m[:, :, :, :], m[:, :, :, :],
                                             mask[:, :, :].unsqueeze(1).to_broadcast([P, TB, E, E]), ALU.mult)
                at(last)
                at(dve.tensor_tensor(gt[:, :, :, :], gt[:, :, :, :], ge[:, :, :, :], ALU.add))
                at(dve.tensor_reduce(rank[:, :, :], gt[:, :, :, :], AX.X, ALU.add))
                at(dve.scalar_tensor_tensor(out=es[:, :, :], in0=rank[:, :, :], scalar=1.5, in1=ex[:, :, :],
                                            op0=ALU.is_lt, op1=ALU.mult))

            def weigh(at):
                dve.tensor_reduce(tot[:, 0], es[:, :, :], AX.X, ALU.add)
                at(dve.tensor_reduce(tot[:, 1], ex[:, :, :], AX.X, ALU.add))
                at(dve.scalar_tensor_tensor(out=den[:, :], in0=tot[:, 1], scalar=EPS_GATE, in1=tot[:, 0],
                                            op0=ALU.mult, op1=ALU.add))
                at(dve.reciprocal(rden[:, :], den[:, :]))
                at(dve.tensor_tensor(ws[:, :, :], es[:, :, :], rden[:, :].unsqueeze(2).to_broadcast([P, TB, E]),
                                     ALU.mult))

            def coefs(n, par):
                wait(dve, s_rsd, n + 1)
                wait(dve, s_acc, NO * (n - 1))
                dve.scalar_tensor_tensor(out=coef[:, par], in0=ws[:, :, :], scalar=kappa, in1=rsd[:, :, :],
                                         op0=ALU.mult, op1=ALU.mult).then_inc(s_coef, 1)

            def query_low(n, par):
                wait(dve, a_qh, n + 1)
                for half in range(2):
                    wait(dve, a_qx[half], NX * n)
                dve.tensor_tensor(qp[:, :, 1], qf[:, par], qp[:, :, 0], ALU.subtract).then_inc(a_qp, 1)

            def ktok_low(n, par):
                for j in range(2):
                    wait(dve, a_kth, 2 * n + (j + 1))
                    rows = slice(2 * j, 2 * j + 2)
                    dve.tensor_tensor(ktok[:, par, 1, rows].rearrange("p t d -> p (t d)"), bank[6 + j][:, :],
                                      ktok[:, par, 0, rows].rearrange("p t d -> p (t d)"),
                                      ALU.subtract).then_inc(a_ktl, 1)

            def values(n):
                wait(dve, a_kt, 2 * n + 2)
                wait(dve, a_kl, n + 1)
                for j in range(2):
                    wait(dve, a_v, 2 * n + (j + 1))
                    dve.scalar_tensor_tensor(out=vf[:, 2 * j:2 * j + 2],
                                             in0=bank[6 + j][:, :].rearrange("p (t d) -> p t d", t=2), scalar=aev,
                                             in1=bvB[:, :].unsqueeze(1).to_broadcast([P, 2, D]),
                                             op0=ALU.mult, op1=ALU.add).then_inc(a_vf, 1)

            def value_low(n, par):
                wait(dve, a_vh, n + 1)
                dve.tensor_tensor(vtok[:, par, 1], vf, vtok[:, par, 0], ALU.subtract).then_inc(a_vl, 1)

            def mask_scores(c, g):
                wait(dve, a_s, NG * c + (g + 1))
                if g < NG - 1:
                    wait(dve, a_sl, (NG - 1) * (c - 1) + (g + 1))
                else:
                    wait(dve, a_sll, c)
                dve.scalar_tensor_tensor(out=sm[:, g], in0=bank[g][:, :].rearrange("p (j t) -> p j t", j=4),
                                         scalar=S_SHIFT, in1=causal[:, :].unsqueeze(1).to_broadcast([P, 4, P]),
                                         op0=ALU.mult, op1=ALU.mult).then_inc(a_sm, 1)

            def last_score_low(c, cp):
                wait(dve, a_sh, NG * c + NG)
                wait(dve, a_y, c - 1)
                dve.tensor_tensor(shl[:, cp, 1, NG - 1], sm[:, NG - 1], shl[:, cp, 0, NG - 1],
                                  ALU.subtract).then_inc(a_sll, 1)

            def update_x(c, tile):
                wait(dve, a_wo, c + 1)
                dve.tensor_tensor(X[:, tile, :], bank[5][:, 0:D], X[:, tile, :], ALU.add).then_inc(a_x, 1)

            def mask_kv(c):
                wait(dve, a_dz, c + 1)
                wait(dve, a_z, c)
                dve.scalar_tensor_tensor(out=dz, in0=bank[5][:, 0:D].rearrange("p (c v) -> p c v", c=KC),
                                         scalar=S_SHIFT, in1=sameh[:, :].unsqueeze(1).to_broadcast([P, KC, P]),
                                         op0=ALU.mult, op1=ALU.mult).then_inc(a_dzm, 1)

            def ffn(f):
                n0 = f * NBLK
                g0 = 2 * f * NBLK
                at = Steps(dve, dve_done, step.at)
                if f == 0:
                    first_block_and_weights(at)
                start = at.at
                per = 10

                def body(n, par, last):
                    first = isinstance(n, int) and n == n0
                    at = Steps(dve, dve_done, start if first else (n - n0) * per + start)
                    if f == 0 and isinstance(n, int) and n == 1:
                        attention_scales()
                    for a in range(2 * HC):
                        hidden(n, a // HC, a % HC)
                        if a >= 1:
                            relu_low(n, (a - 1) // HC, (a - 1) % HC)
                    relu_low(n, 1, HC - 1)
                    for t in range(TB):
                        if t < KC and (not last or f == 0):
                            hT_low(n + (1 + g0 - n0), 1 - par, [t])
                        accumulate(n, par, 0, t)
                        if t == 1 and not last:
                            h_twice(n + 1)
                    if f == 0 and last:
                        weight_low(0)
                        weight_low(1)
                    if not last:
                        logits_copy(n + 1)
                    for m in range(HC):
                        hidden(n, 2, m)
                        if not last:
                            if m >= 1:
                                variance(n + 1, m - 1)
                            relu_low(n, 2, m)
                        elif m >= 1:
                            relu_low(n, 2, m - 1)
                    if last:
                        relu_low(n, 2, HC - 1)
                    if last and f == 0:
                        weight_low(2)
                    if not last:
                        variance(n + 1, HC - 1)
                    if not last:
                        logits_max(n + 1)
                    for t in range(TB):
                        accumulate(n, par, 1, t)
                        if t == 1 and not last:
                            choose(n + 1, at)
                        if t == 2 and not last:
                            weigh(at)
                    def stats_ahead(tiles):
                        if two_ahead(n, n0):
                            x_stats(n + (2 + g0 - n0), tile0(n + 2, n0, par), tiles)
                        elif att_ahead(n):
                            x_stats(NBLK, 0, tiles)

                    if f == 0 and isinstance(n, int) and n < 2:
                        wait(dve, l_x[2 + n], 16 * (2 if n == 0 else 4))
                    if att_ahead(n):
                        wait(dve, s_x, TB)
                    stats_ahead(range(0, 2))
                    for m in range(HC):
                        hidden(n, 3, m)
                        if m == 0:
                            stats_ahead(range(2, TB))
                        if not last:
                            if m >= 1:
                                variance(n + 1, HC + m - 1)
                            relu_low(n, 3, m)
                        elif m >= 1:
                            relu_low(n, 3, m - 1)
                    if last:
                        relu_low(n, 3, HC - 1)
                    if not last:
                        variance(n + 1, 2 * HC - 1)
                    if not last:
                        guard(n + 1)
                    for t in range(TB):
                        accumulate(n, par, 2, t)
                        if t == TB - 1 and not last:
                            std_parts(n + 1, at)
                        if t == 0 and f == 0 and first:
                            attention_maxima()
                        if t == 1 and last and f == 0:
                            query_low(0, 0)
                    if last and f == 0:
                        ktok_low(0, 0)
                    for t in range(TB):
                        if t == TB // 2 and last and f == 0:
                            values(0)
                        accumulate(n, par, 3, t)
                        acc_stats(n, t)
                        if t == 1 and not last:
                            coefs(n + 1, 1 - par)
                    return at

                at = blocks(dve, n0, body)
                step.at = at.at

            def attention():
                value_low(0, 0)
                for g in range(NG):
                    mask_scores(0, g)
                last_score_low(0, 0)

                def body(n, par, last):
                    for t in range(TB):
                        c = n * TB + t
                        more = not (last and t == TB - 1)
                        if t == 0 and not last:
                            wait(dve, s_x, TB * (n + 2))
                            x_stats(n + (NBLK + 1), tile0(n + 1, 0, 1 - par))
                        if t == 0 and last:
                            wait(dve, a_x, TB)
                            x_stats(2 * NBLK, 0)
                        if more:
                            mask_scores(c + 1, 0)
                            mask_scores(c + 1, 1)
                        if t > 0:
                            if t == 1:
                                wait(dve, a_xb, n + 1)
                            update_x(c - 1, tile0(n, 0, par) + (t - 1))
                        elif not (isinstance(n, int) and n == 0):
                            update_x(c - 1, tile0(n - 1, 0, 1 - par) + (TB - 1))
                        if more:
                            mask_scores(c + 1, 2)
                            mask_scores(c + 1, 3)
                        if not last:
                            if t == 1:
                                hT_low(n + (NBLK + 1), 1 - par)
                            if t == 2:
                                ktok_low(n + 1, 1 - par)
                            if t == 3:
                                value_low(n + 1, 1 - par)
                        if more:
                            last_score_low(c + 1, (t + 1) % 2)
                        if t == 1 and last:
                            hT_low(2 * NBLK, 0)
                        if t == 2 and last:
                            for j in range(4):
                                variance(NBLK, j)
                        if t == 3 and last:
                            for j in range(5, NU):
                                variance(NBLK, j)
                            guard(NBLK)
                        mask_kv(c)
                        if t == 1 and not last:
                            query_low(n + 1, 1 - par)
                        if t == 2 and not last:
                            values(n + 1)
                        if t == 1 and last:
                            h_twice(NBLK)
                            logits_copy(NBLK)
                        if t == 2 and last:
                            variance(NBLK, 4)
                            logits_max(NBLK)

                blocks(dve, 0, body)
                update_x(TB * NBLK - 1, NT - 1)
                at = Steps(dve, dve_done, step.at)
                std_parts(NBLK, at)
                choose(NBLK, at)
                weigh(at)
                coefs(NBLK, 0)
                x_stats(2 * NBLK + 1, tile0(1, 0, 1))
                step.at = at.at

            ffn(0)
            attention()
            dve.wait_ge(a_x, TB * NBLK)
            ffn(1)
            dve.wait_ge(s_xb, 1)
            for t in range(TB):
                dve.wait_ge(s_z, TB * (2 * NBLK - 1) + t + 1)
                dve.tensor_tensor(z[:, t, :], z[:, t, :], ong[:, :], ALU.mult).then_inc(s_zg, 1)
                xt = X[:, NT - TB + t, :]
                dve.wait_ge(s_zg, t + 1)
                dve.tensor_tensor(xt, xt, z[:, t, :], ALU.add).then_inc(s_x, 1)

        @block.scalar
        def _(act):
            act.dma_start(gamB[:, :, :].rearrange("p e n -> p (e n)"),
                          ln_g.rearrange("(a e) n -> a (e n)", a=1).to_broadcast([P, E * H])).then_inc(l_gam, 16)
            act.dma_start(rw[:, :], router_w).then_inc(l_rw, 16)
            for d, v in ((rngc, rn_g), (rnbc, rn_b)):
                act.dma_start(d[:, :], v.rearrange("(c p) -> p c", p=P), allow_slow_non_contiguous=True).then_inc(l_rw, 16)
            for d, v in ((gamc, ln_g), (betas, ln_b)):
                act.dma_start(d[:, :, :].rearrange("p e m -> p (e m)"), v.rearrange("e (m p) -> p (e m)", p=P),
                              allow_slow_non_contiguous=True).then_inc(l_bet, 16)

            def h_rows(g, t0, used, tiles=range(TB)):
                if tiles[0] == 0:
                    wait(act, s_rs, g + 1)
                    wait(act, s_T, KC * g)
                    wait(act, s_h2, used)
                for t in tiles:
                    last = act.activation(h[:, t, :], X[:, t0 + t, :], ACT.Identity,
                                          bias=xnr[:, t:t + 1], scale=xrs[:, t:t + 1])
                if tiles[-1] == TB - 1:
                    last.then_inc(s_h, 1)

            def h_round(g):
                act.wait_ge(s_h, g + 1)
                act.activation(hr.rearrange("p t d -> p (t d)"), h[:, :, :].rearrange("p t d -> p (t d)"),
                               ACT.Copy).then_inc(s_hr, 1)

            def hT_high(g, par):
                for c in range(KC):
                    wait(act, s_T, KC * g + (c + 1))
                    act.activation(hTh[:, par, c, :], bank[6 + c][:, :], ACT.Copy).then_inc(s_hTh, 1)

            def w2_high(e):
                act.wait_ge(p_q, 2)
                act.activation(w2r[e], w2r[e], ACT.Copy, scale=q2).then_inc(p_w2s, 1)
                act.wait_ge(p_w2s, e + 1)
                act.activation(w2h[:, e], w2r[e], ACT.Copy).then_inc(p_w2h, 1)

            def first_block_and_weights():
                def centre(e):
                    act.wait_ge(p_m, e + 1)
                    for c in range(KC):
                        act.activation(w1r[:, e, c, :], w1r[:, e, c, :], ACT.Identity,
                                       bias=nmean[:, e * KC + c:e * KC + c + 1]).then_inc(p_c, 1)

                def w1T_copy(e):
                    for b in range(2):
                        act.wait_ge(p_wt, 2 * e + b + 1)
                        if e >= 2 and b == 0:
                            act.wait_ge(p_g, e - 1)
                        act.activation(w1T[:, e % 2, 2 * b:2 * b + 2, :].rearrange("p c n -> p (c n)"),
                                       bank[2 * (e % 2) + b][:, :], ACT.Copy).then_inc(p_wtc, 1)

                def gram_high(e):
                    act.wait_ge(p_g, e + 1)
                    act.activation(gramh[:, :, e, :], bank[4 + e % 2][:, :].rearrange("p (c n) -> p c n", c=KC),
                                   ACT.Copy, scale=gscale).then_inc(p_gh, 1)

                def w1_high(e):
                    act.wait_ge(p_w1g, e + 1)
                    act.activation(w1h[:, e].rearrange("p c n -> p (c n)"), w1g[:, e].rearrange("p c n -> p (c n)"),
                                   ACT.Copy).then_inc(p_w1h, 1)

                centre(0)
                centre(1)
                w1T_copy(0)
                centre(2)
                centre(3)
                w1T_copy(1)
                h_rows(0, 0, 0)
                h_round(0)
                hT_high(0, 0)
                act.wait_ge(l_gam, 16)
                act.wait_ge(p_q, 1)
                gram_high(0)
                act.activation(gamB[:, :, :], gamB[:, :, :], ACT.Copy, scale=q1).then_inc(p_gam, 1)
                w1T_copy(2)
                gram_high(1)
                w1T_copy(3)
                w1_high(0)
                w1_high(1)
                gram_high(2)
                w1_high(2)
                gram_high(3)
                w1_high(3)
                exps(0)
                w2_high(0)
                w2_high(1)
                std_T(0)

            def weight_high(k):
                act.wait_ge(a_w, k + 1)
                src = bank[6 + k % 2][:, :]
                if k < 3:
                    act.activation(wTh[:, k].rearrange("p c n -> p (c n)"), src, ACT.Copy, scale=qa).then_inc(a_wh, 1)
                else:
                    act.activation(woT[:, :, :].rearrange("p c n -> p (c n)"), src, ACT.Copy).then_inc(a_wh, 1)

            def exps(n):
                wait(act, s_lgm, n + 1)
                wait(act, s_coef, n)
                act.activation(ex[:, :, :], lgd[:, :, :], ACT.Exp).then_inc(s_E, 1)

            def std_T(n):
                wait(act, s_ST, n + 1)
                act.activation(sdT, bank[7][0:NSTD, 0:BT // 2].bitcast(F16), ACT.Copy).then_inc(s_sdT, 1)
                for e in range(E):
                    wait(act, s_SB, E * n + (e + 1))
                    act.activation(sdB[:, e], bank[6 + e % 2][:, :], ACT.Copy).then_inc(s_sdB, 1)

            def relu_high(n, e, m):
                a = e * HC + m
                wait(act, s_V, NA * n + (a + 1))
                if m == 0:
                    wait(act, s_O, NO * n + (e * TB - TB))
                act.activation(Rh[:, e % 2, m, :], V[:, a % NV], ACT.Relu).then_inc(s_Rh, 1)

            def z_row(n, t):
                wait(act, s_ars, n + 1)
                wait(act, s_x, TB * (n - 1) + (t + 1))
                act.activation(z[:, t, :], acc[:, t, :], ACT.Identity,
                               bias=anr[:, t:t + 1], scale=ars[:, t:t + 1]).then_inc(s_z, 1)

            def z_rows(n):
                for t in range(TB):
                    z_row(n, t)

            def qk_copy(n, par, k, dst):
                if k == 1:
                    wait(act, a_vl, n)
                for c in range(KC):
                    wait(act, a_qk, 4 * n + (2 * k + c + 1))
                    act.activation(dst[:, c], bank[6 + c][:, :], ACT.Identity, bias=bqk[:, k, c:c + 1],
                                   scale=aev).then_inc(a_qf, 1)

            def query_high(n, par):
                for half in range(2):
                    wait(act, a_qx[half], NX * n)
                wait(act, a_qf, 4 * n + 2)
                act.activation(qp[:, :, 0], qf[:, par], ACT.Copy).then_inc(a_qh, 1)

            def key_high(n, par):
                wait(act, a_qf, 4 * n + 4)
                act.activation(kp[:, par, :, 0], kf, ACT.Copy).then_inc(a_kh, 1)

            def ktok_high(n, par):
                for j in range(2):
                    wait(act, a_kt, 2 * n + (j + 1))
                    act.activation(ktok[:, par, 0, 2 * j:2 * j + 2].rearrange("p t d -> p (t d)"),
                                   bank[6 + j][:, :], ACT.Copy).then_inc(a_kth, 1)

            def value_high(n, par):
                wait(act, a_vf, 2 * n + 2)
                act.activation(vtok[:, par, 0], vf, ACT.Copy).then_inc(a_vh, 1)

            def score_high(c, cp, g):
                wait(act, a_sm, NG * c + (g + 1))
                wait(act, a_y, c - 1)
                act.activation(shl[:, cp, 0, g], sm[:, g], ACT.Copy).then_inc(a_sh, 1)

            def y_copy(c):
                wait(act, a_y, c + 1)
                wait(act, a_yt, c)
                act.activation(ysb, bank[4][:, 0:D], ACT.Copy, scale=iys).then_inc(a_ysb, 1)

            def yT_copy(c):
                wait(act, a_yt, c + 1)
                wait(act, a_wo, c)
                act.activation(yT, bank[4][:, 0:D].rearrange("p (c t) -> p c t", c=KC),
                               ACT.Copy).then_inc(a_ytc, 1)

            def ffn(f):
                n0 = f * NBLK
                dg = n0 + 1
                if f == 0:
                    first_block_and_weights()

                def body(n, par, last):
                    for m in range(HC):
                        relu_high(n, 0, m)
                    for m in range(HC):
                        relu_high(n, 1, m)
                        if isinstance(n, int) and n == n0 and m < 2:
                            h_rows(2 * n0 + 1, tile0(1, 0, 1), n0 + 1, [2 * m, 2 * m + 1])
                        if not (isinstance(n, int) and n == n0) and m < TB - 1:
                            z_row(n - 1, m)
                    if not last or f == 0:
                        wait(act, s_A, NA * n)
                        hT_high(n + dg, 1 - par)
                    if isinstance(n, int) and n == n0:
                        h_round(2 * n0 + 1)
                    if f == 0 and isinstance(n, int) and n == 0:
                        w2_high(2)
                        w2_high(3)
                    if not (isinstance(n, int) and n == n0):
                        z_row(n - 1, TB - 1)
                    if last and f == 0:
                        act.wait_ge(p_q, 3)
                        weight_high(0)
                        weight_high(1)
                    for m in range(HC):
                        relu_high(n, 2, m)
                    if last and f == 0:
                        weight_high(2)
                        weight_high(3)
                    if not last:
                        exps(n + 1)
                    for m in range(HC):
                        relu_high(n, 3, m)
                    if two_ahead(n, n0):
                        h_rows(n + (dg + 1), tile0(n + 2, n0, par), n + 2)
                        h_round(n + (dg + 1))
                    elif att_ahead(n):
                        h_rows(NBLK, 0, NBLK)
                    if not last:
                        std_T(n + 1)

                blocks(act, n0, body)
                if f == 1:
                    z_rows(n0 + NBLK - 1)

            def attention():
                qk_copy(0, 0, 0, qf[:, 0])
                query_high(0, 0)
                act.wait_ge(s_Rl, NA * NBLK)
                qk_copy(0, 0, 1, kf)
                key_high(0, 0)
                ktok_high(0, 0)
                value_high(0, 0)
                for g in range(NG):
                    score_high(0, 0, g)
                z_rows(NBLK - 1)

                def body(n, par, last):
                    for t in range(TB):
                        c = n * TB + t
                        if t > 0 or not (isinstance(n, int) and n == 0):
                            yT_copy(c - 1)
                        if t == 1 and not last:
                            h_rows(n + (NBLK + 1), tile0(n + 1, 0, 1 - par), NBLK, range(2, TB))
                        if t == 2 and not last:
                            key_high(n + 1, 1 - par)
                        if t == 3 and not last:
                            if isinstance(n, int) and n == 0:
                                act.wait_ge(s_x, TB * NBLK)
                            value_high(n + 1, 1 - par)
                        if t == 1 and last:
                            h_rows(2 * NBLK, 0, NBLK)
                            h_round(2 * NBLK)
                        for g in range(NG):
                            if t == 1 and g == NG - 1:
                                hT_high(n + (NBLK + 1), 1 - par)
                            if not (last and t == TB - 1):
                                score_high(c + 1, (t + 1) % 2, g)
                        if t == 2 and not last:
                            ktok_high(n + 1, 1 - par)
                        y_copy(c)
                        if t == 0 and not last:
                            h_rows(n + (NBLK + 1), tile0(n + 1, 0, 1 - par), NBLK, range(0, 2))
                        if t == 2 and last:
                            exps(NBLK)
                        if t == 1 and not last:
                            qk_copy(n + 1, 1 - par, 0, qf[:, 1 - par])
                            query_high(n + 1, 1 - par)
                            qk_copy(n + 1, 1 - par, 1, kf)

                blocks(act, 0, body)
                yT_copy(TB * NBLK - 1)
                std_T(NBLK)

            ffn(0)
            attention()
            ffn(1)

        @block.tensor
        def _(pe):
            def h_T(g):
                wait(pe, s_h, g + 1)
                for c in range(KC):
                    for t in range(TB):
                        last = pe.transpose(bank[6 + c][:, t * P:(t + 1) * P], h[:, t, c * P:(c + 1) * P], identf[:, :])
                    last.then_inc(s_T, 1)

            def w1_T(e):
                pe.wait_ge(p_c, KC * e + KC)
                for b in range(2):
                    if e >= 2:
                        pe.wait_ge(p_wtc, 2 * (e - 2) + b + 1)
                    for j in range(2):
                        for c in range(KC):
                            last = pe.transpose(bank[2 * (e % 2) + b][:, j * D + c * P:j * D + (c + 1) * P],
                                                w1r[:, e, c, (2 * b + j) * P:(2 * b + j + 1) * P], identf[:, :])
                    last.then_inc(p_wt, 1)

            def w1_gram(e):
                pe.wait_ge(p_wtc, 2 * e + 2)
                if e == 1:
                    pe.wait_ge(p_rc, 1)
                if e >= 2:
                    pe.wait_ge(p_gl, e - 1)
                for c in range(KC):
                    for k in range(HC):
                        last = pe.matmul(bank[4 + e % 2][:, c * D:(c + 1) * D], w1T[:, e % 2, k, c * P:(c + 1) * P],
                                         w1T[:, e % 2, k, :], start=(k == 0), stop=(k == HC - 1))
                last.then_inc(p_g, 1)

            def first_block_and_weights():
                pe.wait_ge(p_id, 1)
                pe.wait_ge(l_rw, 48)
                for c in range(KC):
                    last = pe.transpose(bank[5][:, c * E:(c + 1) * E], rw[:, c * P:(c + 1) * P], identf[0:E, 0:E])
                last.then_inc(p_rt, 1)
                w1_T(0)
                w1_T(1)
                w1_gram(0)
                h_T(0)
                w1_T(2)
                w1_gram(1)
                w1_T(3)
                w1_gram(2)
                pe.wait_ge(p_rw, 1)
                wait(pe, s_hTl, KC)
                for c in range(KC):
                    last = pe.matmul(bank[7][:, 0:E], rnbB[:, c, :], rwT[:, c, :], start=(c == 0), stop=(c == KC - 1))
                last.then_inc(p_rt, 1)
                router(0, 0, 0)
                w1_gram(3)
                pe.wait_ge(p_gl, E)
                pe.wait_ge(p_rc, 2)
                for j in range(NU):
                    gram(0, 0, j)

            def weight_T(k):
                if k >= 2:
                    pe.wait_ge(a_wl, k - 1)
                for c in range(KC):
                    for o in range(KC):
                        last = pe.transpose(bank[6 + k % 2][:, c * D + o * P:c * D + (o + 1) * P],
                                            wqkv[:, k, o, c * P:(c + 1) * P], identf[:, :])
                last.then_inc(a_w, 1)

            def router(n, g, par):
                wait(pe, s_hTl, KC * g + KC)
                for t in range(TB):
                    rows = slice(t * P, (t + 1) * P)
                    o = bank[6][:, t * 2 * E:(t + 1) * 2 * E]
                    pe.matmul(o, hTh[:, par, 0, rows], routw[:, 0, :], start=True, stop=False)
                    pe.matmul(o, hTh[:, par, 1, rows], routw[:, 1, :], start=False, stop=False)
                    pe.matmul(o[:, 0:E], hTl[:, par, 0, rows], routw[:, 0, 0:E], start=False, stop=False)
                    last = pe.matmul(o[:, 0:E], hTl[:, par, 1, rows], routw[:, 1, 0:E], start=False, stop=True)
                last.then_inc(s_L, 1)

            def gram(n, par, j):
                t, e0 = j // 2, 2 * (j % 2)
                if j == 1:
                    wait(pe, s_lg, n + 1)
                if j >= 2:
                    wait(pe, s_var, NU * n + (j - 1))
                for c in range(KC):
                    for part, g in enumerate((gramh, graml)):
                        last = pe.matmul(bank[7 - j % 2][:, :], hTh[:, par, c, t * P:(t + 1) * P],
                                         g[:, c, e0:e0 + 2, :].rearrange("p e n -> p (e n)"),
                                         start=(c == 0 and part == 0), stop=(c == KC - 1 and part == 1))
                last.then_inc(s_U, 1)

            def std_rows(n):
                wait(pe, s_s12, n + 1)
                o = bank[7][0:NSTD, 0:BT // 2].bitcast(F16)
                for t in range(TB):
                    last = pe.transpose(o[:, t * P:(t + 1) * P], s12[:, t, :], ident16[:, :])
                last.then_inc(s_ST, 1)

            def std_spread(n, e):
                if e == 0:
                    wait(pe, s_sdT, n + 1)
                if e >= 2:
                    wait(pe, s_sdB, E * n + (e - 1))
                pe.matmul(bank[6 + e % 2][:, :], sel[:, e, :], sdT, start=True, stop=True).then_inc(s_SB, 1)

            def layer1(n, par, e, m):
                a = e * HC + m
                wait(pe, s_V, NA * n + (a - HC + 1))
                cols = slice(m * P, (m + 1) * P)
                o = bank[m][:, :]
                for c in range(KC):
                    pe.matmul(o, w1h[:, e, c, cols], hTh[:, par, c, :], start=(c == 0), stop=False)
                    pe.matmul(o, w1h[:, e, c, cols], hTl[:, par, c, :], start=False, stop=False)
                    last = pe.matmul(o, w1l[:, e, c, cols], hTh[:, par, c, :], start=False, stop=(c == KC - 1))
                last.then_inc(s_A, 1)

            def layer2(n, e, t):
                o = e * TB + t
                if t == 0:
                    if isinstance(n, int) and n == 0:
                        wait(pe, p_w2l, e + 1)
                    wait(pe, s_Rl, NA * n + (e + 1) * HC)
                wait(pe, s_acc, NO * n + (o - 1))
                rows = slice(t * P, (t + 1) * P)
                dst = bank[4 + t % 2][:, 0:D]
                for k in range(HC):
                    pe.matmul(dst, Rh[:, e % 2, k, rows], w2h[:, e, k, :], start=(k == 0), stop=False)
                    pe.matmul(dst, Rh[:, e % 2, k, rows], w2l[:, e, k, :], start=False, stop=False)
                    last = pe.matmul(dst, Rl[:, e % 2, k, rows], w2h[:, e, k, :], start=False, stop=(k == HC - 1))
                last.then_inc(s_O, 1)

            def split_product(o, lhs, rhs, start, stop, **kw):
                (lh, ll), (rh, rl) = lhs, rhs
                pe.matmul(o, lh, rh, start=start, stop=False, **kw)
                pe.matmul(o, lh, rl, start=False, stop=False, **kw)
                return pe.matmul(o, ll, rh, start=False, stop=stop, **kw)

            def rows_T(n):
                wait(pe, a_vf, 2 * n)
                h_T(n + NBLK)

            def queries_keys(n, par):
                for k in range(2):
                    for m in range(KC):
                        if k == 0:
                            wait(pe, s_hTl, KC * n + (KC * NBLK + m + 1))
                            if m == 0:
                                wait(pe, s_hTl, KC * n + (KC * NBLK + KC))
                        else:
                            wait(pe, a_qf, 4 * n + (m + 1))
                        cols = slice(m * P, (m + 1) * P)
                        for c in range(KC):
                            last = split_product(bank[6 + m][:, :],
                                                 (wTh[:, k, c, cols], wTl[:, k, c, cols]),
                                                 (hTh[:, par, c, :], hTl[:, par, c, :]),
                                                 c == 0, c == KC - 1)
                        last.then_inc(a_qk, 1)

            def keys_T(n):
                wait(pe, a_qf, 4 * n + 4)
                for j in range(2):
                    for t in range(2 * j, 2 * j + 2):
                        for m in range(KC):
                            last = pe.transpose(bank[6 + j][:, (t % 2) * D + m * P:(t % 2) * D + (m + 1) * P],
                                                kf[:, m, t * P:(t + 1) * P], identf[:, :])
                    last.then_inc(a_kt, 1)

            def values(n, par):
                for j in range(2):
                    wait(pe, a_ktl, 2 * n + (j + 1))
                    for t in range(2 * j, 2 * j + 2):
                        rows = slice(t * P, (t + 1) * P)
                        for c in range(KC):
                            last = split_product(bank[6 + j][:, (t % 2) * D:(t % 2 + 1) * D],
                                                 (hTh[:, par, c, rows], hTl[:, par, c, rows]),
                                                 (wTh[:, 2, c, :], wTl[:, 2, c, :]),
                                                 c == 0, c == KC - 1)
                    last.then_inc(a_v, 1)

            def scores(c, n, par, t, g):
                if g == 0:
                    if t == 0:
                        wait(pe, a_kl, n + 1)
                    if t % 2 == 0:
                        wait(pe, a_qx[t // 2], NX * n + NX)
                wait(pe, a_sm, NG * (c - 1) + (g + 1))
                m, j0 = g // 2, 4 * (g % 2)
                cols = slice(t * P, (t + 1) * P)
                split_product(bank[g][:, :].rearrange("p (j t) -> p j t", j=4),
                              (kp[:, par, m, 0, cols], kp[:, par, m, 1, cols]),
                              (qx[:, j0:j0 + 4, m, 0, cols], qx[:, j0:j0 + 4, m, 1, cols]),
                              True, True).then_inc(a_s, 1)

            def outputs(c, n, par, t):
                wait(pe, a_z, c)
                wait(pe, a_ytc, c)
                cols = slice(t * P, (t + 1) * P)
                for m in range(KC):
                    pe.matmul(bank[4][:, m * P:(m + 1) * P], qf[:, par, m, cols], zst[:, par, m, :],
                              start=(m == 0), stop=False, skip_group_check=True)
                wait(pe, a_sl, (NG - 1) * c + (NG - 1))
                wait(pe, a_sll, c + 1)
                if t == 0:
                    wait(pe, a_vl, n + 1)
                for hd in range(4 * NG):
                    vs = slice(hd * HD, (hd + 1) * HD)
                    g, j = hd // 4, hd % 4
                    last = split_product(bank[4][:, vs], (shl[:, t % 2, 0, g, j], shl[:, t % 2, 1, g, j]),
                                         (vtok[:, par, 0, t, vs], vtok[:, par, 1, t, vs]),
                                         False, hd == 4 * NG - 1, skip_group_check=True)
                last.then_inc(a_y, 1)

            def keys_values(c, par, t):
                wait(pe, a_x, c)
                for m in range(KC):
                    cols = slice(m * P, (m + 1) * P)
                    last = split_product(bank[5][:, cols], (ktok[:, par, 0, t, cols], ktok[:, par, 1, t, cols]),
                                         (vtok[:, par, 0, t, cols], vtok[:, par, 1, t, cols]),
                                         True, True)
                last.then_inc(a_dz, 1)

            def y_T(c):
                wait(pe, a_ysb, c + 1)
                for m in range(KC):
                    last = pe.transpose(bank[4][:, m * P:(m + 1) * P], ysb[:, m * P:(m + 1) * P], identf[:, :])
                last.then_inc(a_yt, 1)

            def project(c):
                wait(pe, a_ytc, c + 1)
                wait(pe, a_dzm, c + 1)
                for m in range(KC):
                    last = pe.matmul(bank[5][:, 0:D], yT[:, m, :], woT[:, m, :], start=(m == 0), stop=(m == KC - 1))
                last.then_inc(a_wo, 1)

            def ffn(f):
                n0 = f * NBLK
                dg = n0 + 1
                if f == 0:
                    first_block_and_weights()

                def body(n, par, last):
                    for m in range(HC):
                        if f == 0 and m == 0 and isinstance(n, int) and n == n0:
                            pe.wait_ge(p_w1l, 1)
                        layer1(n, par, 0, m)
                        if isinstance(n, int) and n == n0 and m >= 1:
                            if m == 1:
                                if f == 0:
                                    pe.wait_ge(p_sel, 1)
                                std_rows(n)
                            else:
                                std_spread(n, 2 * m - 4)
                                std_spread(n, 2 * m - 3)
                    if f == 0 and isinstance(n, int) and n == n0:
                        pe.wait_ge(p_w1l, E)
                    for m in range(HC):
                        layer1(n, par, 1, m)
                    if not last or f == 0:
                        wait(pe, s_sdB, E * (n + 1))
                        h_T(n + dg)
                    if f == 1 and isinstance(n, int) and n == n0:
                        pe.wait_ge(a_x, TB * NBLK)
                    for t in range(TB):
                        layer2(n, 0, t)
                    if last and f == 0:
                        pe.wait_ge(l_att, 16 * 8)
                        wait(pe, s_hTl, KC * NBLK + KC)
                        weight_T(0)
                        weight_T(1)
                    if not last:
                        router(n + 1, n + dg, 1 - par)
                    for m in range(HC):
                        layer1(n, par, 2, m)
                        if not last:
                            gram(n + 1, 1 - par, m)
                    if last and f == 0:
                        weight_T(2)
                        weight_T(3)
                    for t in range(TB):
                        layer2(n, 1, t)
                    for m in range(HC):
                        layer1(n, par, 3, m)
                        if not last:
                            gram(n + 1, 1 - par, 4 + m)
                    if last and f == 0:
                        pe.wait_ge(a_wl, 3)
                        pe.wait_ge(a_wh, 4)
                        queries_keys(0, 0)
                    for t in range(TB):
                        layer2(n, 2, t)
                    if last and f == 0:
                        keys_T(0)
                    for t in range(TB):
                        if t == TB // 2 and last and f == 0:
                            values(0, 0)
                        layer2(n, 3, t)
                        if t == 1 and not last:
                            std_rows(n + 1)
                        if t >= 2 and not last:
                            std_spread(n + 1, 2 * t - 4)
                            std_spread(n + 1, 2 * t - 3)

                blocks(pe, n0, body)

            def attention():
                pe.wait_ge(s_V, NA * NBLK)
                for g in range(NG):
                    scores(0, 0, 0, 0, g)

                def body(n, par, last):
                    for t in range(TB):
                        c = n * TB + t
                        first = t == 0 and isinstance(n, int) and n == 0
                        more = not (last and t == TB - 1)
                        nn, np_ = (n, par) if t < TB - 1 else (n + 1, 1 - par)
                        for g in range(NG):
                            if more:
                                scores(c + 1, nn, np_, (t + 1) % TB, g)
                            if g == 0 and not first:
                                y_T(c - 1)
                            if g == 1 and not first:
                                project(c - 1)
                        if t == 1 and not last:
                            rows_T(n + 1)
                        if t == 2 and not last:
                            keys_T(n + 1)
                        if t == 1 and last:
                            wait(pe, a_vf, 2 * NBLK)
                            h_T(2 * NBLK)
                        if t >= 2 and last:
                            gram(NBLK, 0, 6 * (t - 2))
                            gram(NBLK, 0, 6 * (t - 2) + 1)
                        if t == 0 and isinstance(n, int) and n == 0:
                            pe.wait_ge(s_acc, NO * NBLK)
                            pe.wait_ge(a_mask, 1)
                        outputs(c, n, par, t)
                        if t == 2 and last:
                            gram(NBLK, 0, 2)
                            gram(NBLK, 0, 3)
                        keys_values(c, par, t)
                        if t == 1 and last:
                            router(NBLK, 2 * NBLK, 0)
                        if t == 2 and last:
                            gram(NBLK, 0, 4)
                            gram(NBLK, 0, 5)
                        if t == 1 and not last:
                            queries_keys(n + 1, 1 - par)
                        if t == 2 and not last:
                            values(n + 1, 1 - par)

                blocks(pe, 0, body)
                y_T(TB * NBLK - 1)
                project(TB * NBLK - 1)
                pe.wait_ge(a_sm, NG * TB * NBLK)

            ffn(0)
            attention()
            ffn(1)


_INS = ['L0_attn_x', 'L0_attn_Wq', 'L0_attn_bq', 'L0_attn_Wk', 'L0_attn_bk', 'L0_attn_Wv', 'L0_attn_bv', 'L0_attn_Wo',
        'L0_attn_bo', 'L0_ffn_router_w', 'L0_ffn_rn_g', 'L0_ffn_rn_b', 'L0_ffn_w1', 'L0_ffn_ln_g', 'L0_ffn_ln_b',
        'L0_ffn_w2', 'L0_ffn_on_g', 'L0_ffn_on_b']
_OUTS = [((2, 2048, 256), 'float32')]


def kernel(**inputs):
    import numpy as _np
    import concourse.bacc as _bacc
    from concourse import mybir as _mybir
    from concourse.bass_utils import run_bass_kernel_spmd as _run

    nc = _bacc.Bacc("TRN2", target_bir_lowering=False, num_devices=1)
    arrays, args = {}, []
    for name in _INS:
        a = _np.ascontiguousarray(inputs[name])
        arrays[f"in_{name}_dram"] = a
        args.append(nc.dram_tensor(f"in_{name}_dram", a.shape, _mybir.dt.from_np(a.dtype), kind="ExternalInput").ap())
    for i, (shape, dtype) in enumerate(_OUTS):
        dt = _mybir.dt.from_np(_np.dtype(dtype))
        args.append(nc.dram_tensor(f"out_{i}_dram", shape, dt, kind="ExternalOutput").ap())
    macaron_kernel(nc, *args)
    r = _run(nc, [arrays], core_ids=[0])
    return r.results[0]["out_0_dram"]
```
